# Optimizing a Trainium2 kernel written in Bass

```python
import numpy as np
import jax
import jax.numpy as jnp

def _softmax(x, axis=-1):
    return jax.nn.softmax(x, axis=axis)

def _gelu(x):
    return jax.nn.gelu(x, approximate=True)

def _silu(x):
    return jax.nn.silu(x)

def _sigmoid(x):
    return jax.nn.sigmoid(x)

def _layernorm(x, axis=-1, eps=1e-05):
    m = jnp.mean(x, axis=axis, keepdims=True)
    v = jnp.var(x, axis=axis, keepdims=True)
    return (x - m) / jnp.sqrt(v + eps)

def _scatter_add(tgt, idx, src, axis=0):
    return tgt.at[idx].add(src)

def _segment_sum(src, seg, n):
    return jax.ops.segment_sum(src, seg, n)
kernel_name = 'mk_vit_tower_cls_d2_tok_img768_r4_b59916'

def setup_inputs(seed: int=0):
    np.random.seed(seed)
    _w = jnp.asarray

    def _rec_inputs():
        import jax
        import jax.numpy as jnp
        _rk = jax.random.key(seed)
        x = -0.000147625 + 0.999875 * jax.random.normal(jax.random.fold_in(_rk, 1), (32, 3, 128, 128), jnp.float32)
        cls_tok = 0.02 * jax.random.normal(jax.random.fold_in(_rk, 5), (1, 1, 192), jnp.float32)
        return (x, cls_tok)
    x, cls_tok = _rec_inputs()

    def _L0_tok_setup():
        import jax, jax.numpy as jnp
        import numpy as np
        IN_CH = 3
        PATCH = 16
        EMB = 192
        IMG = 224
        BATCH = 64
        key = jax.random.key(seed)
        kx, kw, kb = jax.random.split(key, 3)
        x = jax.random.normal(kx, (BATCH, IN_CH, IMG, IMG), dtype=jnp.float32)
        in_feat = IN_CH * PATCH * PATCH
        bound = 1.0 / np.sqrt(in_feat)
        W = jax.random.uniform(kw, (EMB, in_feat), minval=-bound, maxval=bound, dtype=jnp.float32)
        b = jax.random.uniform(kb, (EMB,), minval=-bound, maxval=bound, dtype=jnp.float32)
        return {'x': x, 'W': W, 'b': b}
    _L0_tok_all = _L0_tok_setup()
    _L0_tok_in = {k: v for k, v in _L0_tok_all.items() if k in ('W', 'b')}
    del _L0_tok_all

    def _L0_attn_setup():
        import jax, jax.numpy as jnp
        import numpy as np
        B, S, D = (2, 512, 192)
        H, STRIDE = (12, 8)
        HD = D // H

        def _stride_mask(S, stride, causal):
            i = jnp.arange(S)[:, None]
            j = jnp.arange(S)[None, :]
            strided = j % stride == 0
            if causal:
                strided = strided & (j <= i)
            return strided | (j == i) | (j == i - 1)
        key = jax.random.key(seed)
        k0, k1, k2 = jax.random.split(key, 3)
        x = jax.random.normal(k0, (B, S, D), dtype=jnp.float32)
        qkv_w = jax.random.normal(k1, (3 * D, D), dtype=jnp.float32) * 0.02
        qkv_b = jnp.zeros((3 * D,), dtype=jnp.float32)
        out_w = jax.random.normal(k2, (D, D), dtype=jnp.float32) * 0.02
        out_b = jnp.zeros((D,), dtype=jnp.float32)
        return {'x': x, 'qkv_w': qkv_w, 'qkv_b': qkv_b, 'out_w': out_w, 'out_b': out_b}
    _L0_attn_all = _L0_attn_setup()
    _L0_attn_in = {k: v for k, v in _L0_attn_all.items() if k in ('qkv_w', 'qkv_b', 'out_w', 'out_b')}
    del _L0_attn_all

    def _L0_ffn_setup():
        import jax, jax.numpy as jnp
        import numpy as np
        B, S, D, F, E = (4, 512, 192, 768, 8)
        key = jax.random.key(seed)
        ks = jax.random.split(key, 5)
        return {'x': jax.random.normal(ks[0], (B, S, D), dtype=jnp.float32), 'Ws': jax.random.normal(ks[1], (D, E), dtype=jnp.float32) * 0.02, 'bs': jnp.zeros((E,), dtype=jnp.float32), 'W1': jax.random.normal(ks[2], (E, D, F), dtype=jnp.float32) * 0.02, 'b1': jnp.zeros((E, F), dtype=jnp.float32), 'W2': jax.random.normal(ks[3], (E, F, D), dtype=jnp.float32) * 0.02, 'b2': jnp.zeros((E, D), dtype=jnp.float32)}
    _L0_ffn_all = _L0_ffn_setup()
    _L0_ffn_in = {k: v for k, v in _L0_ffn_all.items() if k in ('Ws', 'bs', 'W1', 'b1', 'W2', 'b2')}
    del _L0_ffn_all

    def _L1_attn_setup():
        import jax, jax.numpy as jnp
        import numpy as np
        LEVEL = 8
        NUM_HEADS = 12
        QN_SYM = float(-(LEVEL // 2))
        QP_SYM = float(LEVEL // 2 - 1)
        QN_ASYM = 0.0
        QP_ASYM = float(LEVEL - 1)

        def fake_quant(x, s, qn, qp):
            xc = jnp.clip(x / s, qn, qp)
            xr = xc + jax.lax.stop_gradient(jnp.round(xc) - xc)
            return s * xr
        key = jax.random.key(seed)
        k0, k1, k2 = jax.random.split(key, 3)
        B, N, C = (4, 512, 192)
        x = jax.random.normal(k0, (B, N, C), dtype=jnp.float32)
        Wqkv = jax.random.normal(k1, (3 * C, C), dtype=jnp.float32) * C ** (-0.5)
        Wproj = jax.random.normal(k2, (C, C), dtype=jnp.float32) * C ** (-0.5)
        bproj = jnp.zeros((C,), dtype=jnp.float32)
        s_q = jnp.asarray(1.0, dtype=jnp.float32)
        s_k = jnp.asarray(1.0, dtype=jnp.float32)
        s_v = jnp.asarray(1.0, dtype=jnp.float32)
        s_attn = jnp.asarray(1.0 / QP_ASYM, dtype=jnp.float32)
        s_after = jnp.asarray(1.0, dtype=jnp.float32)
        return {'x': x, 'Wqkv': Wqkv, 'Wproj': Wproj, 'bproj': bproj, 's_q': s_q, 's_k': s_k, 's_v': s_v, 's_attn': s_attn, 's_after': s_after}
    _L1_attn_all = _L1_attn_setup()
    _L1_attn_in = {k: v for k, v in _L1_attn_all.items() if k in ('Wqkv', 'Wproj', 'bproj', 's_q', 's_k', 's_v', 's_attn', 's_after')}
    del _L1_attn_all

    def _L1_ffn_setup():
        import jax, jax.numpy as jnp
        import numpy as np
        NHEAD = 12
        EPS_Z = 1e-05
        EPS_LN = 1e-05

        def _zscore_last(t, n):
            m = t.mean(axis=-1, keepdims=True)
            var = ((t - m) ** 2).sum(axis=-1, keepdims=True) / (n - 1)
            return (t - m) / (jnp.sqrt(var) + EPS_Z)

        def _layernorm(x, g, b):
            m = x.mean(axis=-1, keepdims=True)
            v = ((x - m) ** 2).mean(axis=-1, keepdims=True)
            return (x - m) * jax.lax.rsqrt(v + EPS_LN) * g + b
        key = jax.random.key(seed)
        ks = jax.random.split(key, 20)
        B, T, D, FF, E = (2, 256, 192, 768, 4)
        p = lambda k, shape: jax.random.normal(k, shape, jnp.float32) * 0.02
        return {'src': jax.random.normal(ks[0], (B, T, D), jnp.float32), 'frac': jax.random.uniform(ks[1], (B, T), jnp.float32), 'Wq': p(ks[2], (D, D)), 'bq': jnp.zeros((D,), jnp.float32), 'Wk': p(ks[3], (D, D)), 'bk': jnp.zeros((D,), jnp.float32), 'Wv': p(ks[4], (D, D)), 'bv': jnp.zeros((D,), jnp.float32), 'Wo': p(ks[5], (D, D)), 'bo': jnp.zeros((D,), jnp.float32), 'gamma': jnp.float32(1.0), 'ln1_g': jnp.ones((D,), jnp.float32), 'ln1_b': jnp.zeros((D,), jnp.float32), 'ln2_g': jnp.ones((D,), jnp.float32), 'ln2_b': jnp.zeros((D,), jnp.float32), 'Wg': p(ks[6], (E, D)), 'bg': jnp.zeros((E,), jnp.float32), 'W1': p(ks[7], (E, D, FF)), 'b1': jnp.zeros((E, FF), jnp.float32), 'W2': p(ks[8], (E, FF, D)), 'b2': jnp.zeros((E, D), jnp.float32)}
    _L1_ffn_all = _L1_ffn_setup()
    _L1_ffn_in = {k: v for k, v in _L1_ffn_all.items() if k in ('frac', 'Wq', 'bq', 'Wk', 'bk', 'Wv', 'bv', 'Wo', 'bo', 'gamma', 'ln1_g', 'ln1_b', 'ln2_g', 'ln2_b', 'Wg', 'bg', 'W1', 'b1', 'W2', 'b2')}
    del _L1_ffn_all
    return {'x': x, 'cls_tok': cls_tok, 'L0_tok_W': _L0_tok_in['W'], 'L0_tok_b': _L0_tok_in['b'], 'L0_attn_qkv_w': _L0_attn_in['qkv_w'], 'L0_attn_qkv_b': _L0_attn_in['qkv_b'], 'L0_attn_out_w': _L0_attn_in['out_w'], 'L0_attn_out_b': _L0_attn_in['out_b'], 'L0_ffn_Ws': _L0_ffn_in['Ws'], 'L0_ffn_bs': _L0_ffn_in['bs'], 'L0_ffn_W1': _L0_ffn_in['W1'], 'L0_ffn_b1': _L0_ffn_in['b1'], 'L0_ffn_W2': _L0_ffn_in['W2'], 'L0_ffn_b2': _L0_ffn_in['b2'], 'L1_attn_Wqkv': _L1_attn_in['Wqkv'], 'L1_attn_Wproj': _L1_attn_in['Wproj'], 'L1_attn_bproj': _L1_attn_in['bproj'], 'L1_attn_s_q': _L1_attn_in['s_q'], 'L1_attn_s_k': _L1_attn_in['s_k'], 'L1_attn_s_v': _L1_attn_in['s_v'], 'L1_attn_s_attn': _L1_attn_in['s_attn'], 'L1_attn_s_after': _L1_attn_in['s_after'], 'L1_ffn_frac': _L1_ffn_in['frac'], 'L1_ffn_Wq': _L1_ffn_in['Wq'], 'L1_ffn_bq': _L1_ffn_in['bq'], 'L1_ffn_Wk': _L1_ffn_in['Wk'], 'L1_ffn_bk': _L1_ffn_in['bk'], 'L1_ffn_Wv': _L1_ffn_in['Wv'], 'L1_ffn_bv': _L1_ffn_in['bv'], 'L1_ffn_Wo': _L1_ffn_in['Wo'], 'L1_ffn_bo': _L1_ffn_in['bo'], 'L1_ffn_gamma': _L1_ffn_in['gamma'], 'L1_ffn_ln1_g': _L1_ffn_in['ln1_g'], 'L1_ffn_ln1_b': _L1_ffn_in['ln1_b'], 'L1_ffn_ln2_g': _L1_ffn_in['ln2_g'], 'L1_ffn_ln2_b': _L1_ffn_in['ln2_b'], 'L1_ffn_Wg': _L1_ffn_in['Wg'], 'L1_ffn_bg': _L1_ffn_in['bg'], 'L1_ffn_W1': _L1_ffn_in['W1'], 'L1_ffn_b1': _L1_ffn_in['b1'], 'L1_ffn_W2': _L1_ffn_in['W2'], 'L1_ffn_b2': _L1_ffn_in['b2']}

def reference(x, cls_tok, L0_tok_W, L0_tok_b, L0_attn_qkv_w, L0_attn_qkv_b, L0_attn_out_w, L0_attn_out_b, L0_ffn_Ws, L0_ffn_bs, L0_ffn_W1, L0_ffn_b1, L0_ffn_W2, L0_ffn_b2, L1_attn_Wqkv, L1_attn_Wproj, L1_attn_bproj, L1_attn_s_q, L1_attn_s_k, L1_attn_s_v, L1_attn_s_attn, L1_attn_s_after, L1_ffn_frac, L1_ffn_Wq, L1_ffn_bq, L1_ffn_Wk, L1_ffn_bk, L1_ffn_Wv, L1_ffn_bv, L1_ffn_Wo, L1_ffn_bo, L1_ffn_gamma, L1_ffn_ln1_g, L1_ffn_ln1_b, L1_ffn_ln2_g, L1_ffn_ln2_b, L1_ffn_Wg, L1_ffn_bg, L1_ffn_W1, L1_ffn_b1, L1_ffn_W2, L1_ffn_b2):
    import jax
    import jax.numpy as jnp

    def _L0_tok_ref(x, W, b):
        import jax, jax.numpy as jnp
        import numpy as np
        IN_CH = 3
        PATCH = 16
        EMB = 192
        IMG = 224
        BATCH = 64
        B, C, H, Wd = x.shape
        p = PATCH
        nh, nw = (H // p, Wd // p)
        patches = x.reshape(B, C, nh, p, nw, p).transpose(0, 1, 2, 4, 3, 5)
        patches = patches.reshape(B, C, nh * nw, p, p).transpose(0, 2, 3, 4, 1)
        feats = patches.reshape(B, nh * nw, p * p * C)
        return jnp.einsum('bnf,ef->bne', feats, W) + b

    def _L0_attn_ref(x, qkv_w, qkv_b, out_w, out_b):
        import jax, jax.numpy as jnp
        import numpy as np
        B, S, D = (2, 512, 192)
        H, STRIDE = (12, 8)
        HD = D // H

        def _stride_mask(S, stride, causal):
            i = jnp.arange(S)[:, None]
            j = jnp.arange(S)[None, :]
            strided = j % stride == 0
            if causal:
                strided = strided & (j <= i)
            return strided | (j == i) | (j == i - 1)
        Bx, Sx, Dx = x.shape
        qkv = x @ qkv_w.T + qkv_b
        qkv = qkv.reshape(Bx, Sx, 3, H, HD)
        q, k, v = jnp.transpose(qkv, (2, 0, 3, 1, 4))
        scale = HD ** (-0.5)
        attn = jnp.einsum('bhid,bhjd->bhij', q, k) * scale
        mask = _stride_mask(Sx, STRIDE, True)
        attn = jnp.where(mask[None, None], attn, -jnp.inf)
        a = jax.nn.softmax(attn, axis=-1)
        a = jnp.nan_to_num(a, nan=0.0)
        out = jnp.einsum('bhij,bhjd->bhid', a, v)
        out = jnp.transpose(out, (0, 2, 1, 3)).reshape(Bx, Sx, Dx)
        return out @ out_w.T + out_b

    def _L0_ffn_ref(x, Ws, bs, W1, b1, W2, b2):
        import jax, jax.numpy as jnp
        import numpy as np
        B, S, D, F, E = (4, 512, 192, 768, 8)
        b, s, d = x.shape
        xt = x.reshape(-1, d)
        logits = xt @ Ws + bs
        probs = jax.nn.softmax(logits, axis=-1)
        routes = jnp.argmax(probs, axis=-1)
        prob_max = jnp.max(probs, axis=-1)
        h = jax.nn.gelu(jnp.einsum('td,edf->etf', xt, W1) + b1[:, None, :], approximate=False)
        y = jnp.einsum('etf,efd->etd', h, W2) + b2[:, None, :]
        out = jnp.take_along_axis(y, routes[None, :, None], axis=0)[0]
        out = out * prob_max[:, None]
        return out.reshape(b, s, d)

    def _L1_attn_ref(x, Wqkv, Wproj, bproj, s_q, s_k, s_v, s_attn, s_after):
        import jax, jax.numpy as jnp
        import numpy as np
        LEVEL = 8
        NUM_HEADS = 12
        QN_SYM = float(-(LEVEL // 2))
        QP_SYM = float(LEVEL // 2 - 1)
        QN_ASYM = 0.0
        QP_ASYM = float(LEVEL - 1)

        def fake_quant(x, s, qn, qp):
            xc = jnp.clip(x / s, qn, qp)
            xr = xc + jax.lax.stop_gradient(jnp.round(xc) - xc)
            return s * xr
        B, N, C = x.shape
        H = NUM_HEADS
        D = C // H
        scale = D ** (-0.5)
        qkv = jnp.einsum('bnc,dc->bnd', x, Wqkv).reshape(B, N, 3, H, D).transpose(2, 0, 3, 1, 4)
        q, k, v = (qkv[0], qkv[1], qkv[2])
        q = fake_quant(q, s_q, QN_SYM, QP_SYM) * scale
        k = fake_quant(k, s_k, QN_SYM, QP_SYM)
        v = fake_quant(v, s_v, QN_SYM, QP_SYM)
        attn = jnp.einsum('bhnd,bhmd->bhnm', q, k)
        attn = fake_quant(attn / N, s_attn, QN_ASYM, QP_ASYM)
        out = jnp.einsum('bhnm,bhmd->bhnd', attn, v)
        out = fake_quant(out, s_after, QN_SYM, QP_SYM)
        out = out.transpose(0, 2, 1, 3).reshape(B, N, C)
        return out @ Wproj.T + bproj

    def _L1_ffn_ref(src, frac, Wq, bq, Wk, bk, Wv, bv, Wo, bo, gamma, ln1_g, ln1_b, ln2_g, ln2_b, Wg, bg, W1, b1, W2, b2):
        import jax, jax.numpy as jnp
        import numpy as np
        NHEAD = 12
        EPS_Z = 1e-05
        EPS_LN = 1e-05

        def _zscore_last(t, n):
            m = t.mean(axis=-1, keepdims=True)
            var = ((t - m) ** 2).sum(axis=-1, keepdims=True) / (n - 1)
            return (t - m) / (jnp.sqrt(var) + EPS_Z)

        def _layernorm(x, g, b):
            m = x.mean(axis=-1, keepdims=True)
            v = ((x - m) ** 2).mean(axis=-1, keepdims=True)
            return (x - m) * jax.lax.rsqrt(v + EPS_LN) * g + b
        B, T, D = src.shape
        H = NHEAD
        hd = D // H
        scale = hd ** (-0.5)
        Q = (src @ Wq.T + bq).reshape(B, T, H, hd)
        K = (src @ Wk.T + bk).reshape(B, T, H, hd)
        V = (src @ Wv.T + bv).reshape(B, T, H, hd)
        logits = jnp.einsum('bqhd,bkhd->bhqk', Q, K) * scale
        logits = gamma * _zscore_last(logits, T)
        probs = jax.nn.softmax(logits, axis=-1)
        attn = jnp.einsum('bhqk,bkhd->bqhd', probs, V).reshape(B, T, D)
        attn = attn @ Wo.T + bo
        x = _layernorm(src + attn, ln1_g, ln1_b)
        E = Wg.shape[0]
        gate_scores = jax.nn.softmax(x @ Wg.T + bg, axis=-1)
        top2_val, top2_idx = jax.lax.top_k(gate_scores, 2)
        combine = (jax.nn.one_hot(top2_idx, E, dtype=x.dtype) * top2_val[..., None]).sum(axis=-2)
        h = jax.nn.relu(jnp.einsum('btd,edf->ebtf', x, W1) + b1[:, None, None, :])
        y = jnp.einsum('ebtf,efd->ebtd', h, W2) + b2[:, None, None, :]
        ff = jnp.einsum('ebtd,bte->btd', y, combine)
        return _layernorm(x + ff, ln2_g, ln2_b)
    h = _L0_tok_ref(x, L0_tok_W, L0_tok_b)
    h = jnp.concatenate([jnp.broadcast_to(cls_tok, (h.shape[0], 1, h.shape[2])), h], axis=1)
    h = h + _L0_attn_ref(_layernorm(h, axis=-1), L0_attn_qkv_w, L0_attn_qkv_b, L0_attn_out_w, L0_attn_out_b)
    h = h + _L0_ffn_ref(_layernorm(h, axis=-1), L0_ffn_Ws, L0_ffn_bs, L0_ffn_W1, L0_ffn_b1, L0_ffn_W2, L0_ffn_b2)
    h = h + _L1_attn_ref(_layernorm(h, axis=-1), L1_attn_Wqkv, L1_attn_Wproj, L1_attn_bproj, L1_attn_s_q, L1_attn_s_k, L1_attn_s_v, L1_attn_s_attn, L1_attn_s_after)
    h = h + _L1_ffn_ref(_layernorm(h, axis=-1), L1_ffn_frac, L1_ffn_Wq, L1_ffn_bq, L1_ffn_Wk, L1_ffn_bk, L1_ffn_Wv, L1_ffn_bv, L1_ffn_Wo, L1_ffn_bo, L1_ffn_gamma, L1_ffn_ln1_g, L1_ffn_ln1_b, L1_ffn_ln2_g, L1_ffn_ln2_b, L1_ffn_Wg, L1_ffn_bg, L1_ffn_W1, L1_ffn_b1, L1_ffn_W2, L1_ffn_b2)
    return h

_drawn_inputs = setup_inputs


def setup_inputs(seed=0):
    import zlib

    import numpy as np

    out = dict(_drawn_inputs(seed))
    spreads = {'L0_attn_qkv_b': (0.0, 0.1),
     'L0_attn_out_b': (0.0, 0.1),
     'L0_ffn_bs': (0.0, 0.312),
     'L0_ffn_b1': (0.0, 0.777),
     'L0_ffn_b2': (0.0, 0.1),
     'L1_attn_bproj': (0.0, 0.8),
     'L1_ffn_bq': (0.0, 2.0),
     'L1_ffn_bk': (0.0, 2.0),
     'L1_ffn_bv': (0.0, 2.0),
     'L1_ffn_bo': (0.0, 2.0),
     'L1_ffn_ln1_g': (1.0, 0.6),
     'L1_ffn_ln1_b': (0.0, 0.8),
     'L1_ffn_ln2_g': (1.0, 0.6),
     'L1_ffn_ln2_b': (0.0, 0.8),
     'L1_ffn_bg': (0.0, 2.0),
     'L1_ffn_b1': (0.0, 2.0),
     'L1_ffn_b2': (0.0, 2.0)}
    factors = {'L1_attn_Wqkv': 8.0,
     'L1_attn_Wproj': 8.0,
     'L1_ffn_Wq': 56.968,
     'L1_ffn_Wk': 54.36,
     'L1_ffn_Wv': 24.102,
     'L1_ffn_Wo': 5.911,
     'L1_ffn_Wg': 8.0,
     'L1_ffn_W1': 8.0,
     'L1_ffn_W2': 7.971}
    for name, (base, spread) in spreads.items():
        noise = np.random.default_rng([zlib.crc32(name.encode()), seed]).standard_normal(out[name].shape)
        drawn = base * np.exp(spread * noise) if base else spread * noise
        out[name] = jnp.asarray(drawn.astype(out[name].dtype))
    for name, factor in factors.items():
        out[name] = (out[name] * factor).astype(out[name].dtype)
    return out
```

```python
from contextlib import ExitStack

import numpy as np

import concourse.bass as bass
from concourse import mybir

ALU = mybir.AluOpType
ACT = mybir.ActivationFunctionType
AX = mybir.AxisListType
F32 = mybir.dt.float32
BF16 = mybir.dt.bfloat16
I32 = mybir.dt.int32

P = 128
IMAGES, CHANNELS, SIDE, PATCH = 32, 3, 128, 16
GRID = SIDE // PATCH
S = GRID * GRID
TOK = S + 1
D, H, HD = 192, 12, 16
PAIRS = IMAGES // 2
CLS = PAIRS
TILES = PAIRS + 1
FEAT = CHANNELS * PATCH * PATCH
FK = FEAT // P
C = D // 96
HC = H // C
STRIDE = 8
MS = S // STRIDE
KEYS0 = MS + 3
FF = 768
FFK = FF // P
HALF = FF // 2
E0, TOP0 = 8, 1
E1, TOP1 = 4, 2
NT0 = (IMAGES * TOK * TOP0 + E0 * (P - 1)) // P
NT1 = (IMAGES * TOK * TOP1 + E1 * (P - 1)) // P
ZERO_PARTS = 4
EPS_LN = 1e-5
EPS_Z = 1e-5
MAGIC = 12582912.0
NEG = -1e30
HEAD_SCALE = HD ** -0.5
LEVEL_LO, LEVEL_HI, LEVEL_ATTN = -4.0, 3.0, 7.0

W_AT = {}
WCOLS = 0
for _n, _w in (("qkv0", 3 * D), ("out0", D), ("gate0", E0), ("qkv1", 3 * D), ("out1", D),
               ("qkv2", 3 * D), ("out2", D), ("gate2", E1)):
    W_AT[_n] = WCOLS
    WCOLS += _w

R_AT = {}
RCOLS = 0
for _n, _w in (("b_tok", D), ("cls", D), ("ln1_g", D), ("ln1_b", D), ("ln2_g", D), ("ln2_b", D),
               ("s_q", 1), ("s_k", 1), ("s_v", 1), ("s_attn", 1), ("s_after", 1), ("gamma", 1),
               ("b2_0", E0 * D), ("b2_1", E1 * D)):
    R_AT[_n] = RCOLS
    RCOLS += _w

K_AT, K_W = {}, {}
KCOLS = 0
for _n, _w in (("ident", P), ("before", P), ("ones", P), ("mask0", KEYS0 * H), ("pick_v", 2 * MS * H),
               ("head_rows", D), ("head6", HC), ("half", 2), ("half_cols", D), ("head12", C * H),
               ("twice", 2 * P), ("prio", 8), ("valid", TILES), ("tile_no", max(NT0, NT1)), ("first", H)):
    K_AT[_n], K_W[_n] = KCOLS, _w
    KCOLS += _w


def shape_constants():
    k = np.zeros((P, KCOLS), np.float32)

    def put(name, a):
        k[:a.shape[0], K_AT[name]:K_AT[name] + a.shape[1]] = a

    r = np.arange(P)
    put("ident", np.eye(P))
    put("before", (r[:, None] < r[None, :]) * 1.0)
    put("ones", np.ones((P, P)))
    patch = r % S
    mask = np.zeros((P, KEYS0, H))
    for m in range(MS):
        mask[STRIDE * (m + 1) > patch + 1, m] = NEG
    mask[(patch + 1) % STRIDE == 0, MS + 1] = NEG
    mask[patch % STRIDE == 0, MS + 2] = NEG
    put("mask0", mask.reshape(P, -1))
    pick = np.zeros((P, 2, MS, H))
    for s in range(2):
        for m in range(MS):
            pick[S * s + STRIDE * m + STRIDE - 1, s, m] = 1
    put("pick_v", pick.reshape(P, -1))
    put("head_rows", (r[:(MS + 1) * H, None] % H == np.arange(D)[None, :] // HD) * 1.0)
    put("head6", (r[:96, None] // HD == np.arange(HC)) * 1.0)
    put("half", ((r[:96, None] // HD) % 2 == np.arange(2)) * 1.0)
    put("half_cols", (r[:, None] // S == (np.arange(D)[None, :] // HD) % 2) * 1.0)
    h12 = np.zeros((96, C, H))
    for c in range(C):
        h12[:, c] = (r[:96, None] // HD + HC * c == np.arange(H)) * 1.0
    put("head12", h12.reshape(96, -1))
    twice = np.zeros((P, 2, 2, S))
    for s in range(2):
        twice[S * s + np.arange(S), s, :, np.arange(S)] = 1
    put("twice", twice.reshape(P, -1))
    put("prio", np.broadcast_to(8.0 - np.arange(8), (P, 8)))
    valid = np.ones((P, TILES))
    valid[IMAGES:, CLS] = 0
    put("valid", valid)
    put("tile_no", np.broadcast_to(np.arange(max(NT0, NT1)), (P, max(NT0, NT1))))
    first = np.zeros((P, H))
    first[0] = 1
    put("first", first)
    return k


def bodies(order, n):
    for i in range(max(n.values()) + max(lag for _, lag in order)):
        for stage, lag in order:
            if 0 <= i - lag < n[stage]:
                yield stage, i - lag


def issued_before(order, n, other, stage, t):
    names = [s for s, _ in order]
    lag = dict(order)
    done = t + lag[stage] - lag[other] + (names.index(other) < names.index(stage))
    return max(0, min(done, n[other]))


def wait(eng, sem, n):
    if n > 0:
        eng.wait_ge(sem, n)


class Chain:

    def __init__(self, eng, sem, n=0):
        self.eng, self.sem, self.n = eng, sem, n

    def link(self, ins):
        self.n += 1
        ins.then_inc(self.sem, 1)
        self.eng.wait_ge(self.sem, self.n)


def tile_of(u):
    return CLS if u == 0 else u - 1


AREA = 15200


def build(nc, x_feat, w_tok, w_small, rows_in, consts_in, w1_0, w2_0, w1_1, w2_1, out):
    with ExitStack() as ctx:
        def sb(name, shape, dt=F32):
            return ctx.enter_context(nc.sbuf_tensor(name, shape, dt))

        def sem(name):
            return ctx.enter_context(nc.semaphore(name))

        def sems(prefix, names):
            return [sem(prefix + n) for n in names.split()]

        PS = ctx.enter_context(nc.psum_tensor("banks", [P, 8, 512], F32))
        KON = sb("consts_sb", [P, KCOLS])
        ROWS = sb("rows_sb", [P, RCOLS])
        WS = sb("w_small_sb", [97, C, WCOLS])
        HT = sb("h_tok", [P, TILES, D])
        X1 = sb("x_tok", [P, TILES, D])
        LG = sb("gate_logits", [P, TILES, E0])
        W1 = sb("w1_sb", [97, C, E0, FF])
        W2 = sb("w2_sb", [P, E0, FFK, D])
        AR = sb("scratch", [P, AREA])

        def K(name):
            return KON[:, K_AT[name]:K_AT[name] + K_W[name]]

        def ROW(name, w=D, at=0):
            return ROWS[:, R_AT[name] + at:R_AT[name] + at + w]

        def w_small_at(name, c, a, b):
            return WS[0:KC[c], c, W_AT[name] + a:W_AT[name] + b]

        KC = (96, 97)
        ident = K("ident")
        head6 = K("head6")[0:96]
        taken = [0]

        def area(width, parts=P):
            at = taken[0]
            taken[0] += width
            assert taken[0] <= AREA, taken[0]
            return AR[0:parts, at:at + width]

        def chunks(parts, width=P):
            return area(C * width, parts).rearrange("p (c t) -> p c t", c=C)

        loaded = {n: sem("loaded_" + n) for n in ("first", "small", "w_tok", "later", "experts0")}
        vec, pool = sem("vector_chain"), sem("pool_chain")
        out_stored = [sem(f"out_stored{i}") for i in range(3)]
        xg_zeroed = sem("xg_zeroed")
        block = ctx.enter_context(nc.Block())

        XGT = [chunks(97) for _ in range(2)]
        PROB = area(2 * TILES).rearrange("p (k t) -> p k t", k=2)
        between_start = taken[0]
        XG_IN = [area(D) for _ in range(3)]
        shared = area(FK * (3 * P + D))
        HID = [shared[:, i * FF:(i + 1) * FF] for i in range(2)]
        HIDT = [shared[:, (2 + i) * FF:(3 + i) * FF].rearrange("p (k t) -> p k t", k=FFK) for i in range(2)]
        YG = [area(D) for _ in range(2)]
        g_exp, g_prob, g_eq, g_pick, g_off = [area(TILES * E0) for _ in range(5)]
        g_onehot = [area(TILES * E0) for _ in range(3)]
        g_scan = area(TILES * E0)
        g_max, g_sum = area(TILES), area(TILES)
        g_tiles, g_cum, g_base = area(E0), area(E0), area(E0)
        g_le = area(max(NT0 * E0, NT1 * E1))
        g_eid = area(max(NT0, NT1))
        SLOT = sb("slot_of", [P, 2, TILES], I32)
        EID = sb("expert_of", [P, max(NT0, NT1)], I32)
        ZERO = sb("zero", [P, D])
        xg_dram = nc.dram_tensor("tokens_by_expert", [max(NT0, NT1) * P, D], F32, kind="Internal").ap()
        yg_dram = nc.dram_tensor("results_by_expert", [max(NT0, NT1) * P, D], F32, kind="Internal").ap()
        scratch_start = taken[0]

        x_in = [shared[:, i * FK * P:(i + 1) * FK * P].rearrange("p (k t) -> p k t", k=FK) for i in range(3)]
        w_tok_sb = shared[:, 3 * FK * P:].rearrange("p (k e) -> p k e", k=FK)
        xn = [area(D) for _ in range(2)]
        stats1, stats2 = area(6), area(6)
        mv1, mv2 = [area(2) for _ in range(2)], [area(2) for _ in range(2)]
        rstd1, rstd2 = [area(1) for _ in range(2)], [area(1) for _ in range(2)]
        var_eps1, var_eps2, minus_half = area(1), area(1), area(1)
        xT = [chunks(97) for _ in range(2)]
        QKV = [area(5 * D) for _ in range(2)]
        qT = [chunks(96) for _ in range(2)]
        kblk = [area(C * 2 * (MS + 1) * HC, 96).rearrange("p (c s m h) -> p c s m h", c=C, s=2, m=MS + 1)
                for _ in range(2)]
        NV = (MS + 1) * H
        vblk = [area(2 * D, NV).rearrange("p (s e) -> p s e", s=2) for _ in range(2)]
        prod = [area(2 * D).rearrange("p (a e) -> p a e", a=2) for _ in range(2)]
        sraw = area(KEYS0 * H)
        smax = area(H)
        ssub = [area(KEYS0 * H) for _ in range(2)]
        ex = [area(KEYS0 * H) for _ in range(2)]
        rsum = area(H)
        rinv = [area(H) for _ in range(2)]
        exT = [area(P, NV) for _ in range(2)]
        own2 = area(2 * D).rearrange("p (a e) -> p a e", a=2)
        own = [area(D) for _ in range(2)]
        o1 = area(D)
        oatt = [area(D) for _ in range(2)]
        oT = [chunks(97) for _ in range(2)]
        x1T = [chunks(97) for _ in range(2)]

        ORDER_A = [("xT", 1), ("scores", 2), ("x1T", 4), ("pv", 3), ("embed", 0), ("oT", 3), ("logits", 4),
                   ("oproj", 3), ("softmax", 2), ("qkv", 1), ("exp", 2), ("heads", 1), ("expT", 2), ("xn", 0), ("x1", 3),
                   ("dots", 1)]
        NA = {s: TILES for s, _ in ORDER_A}

        def before_a(other, stage, u):
            return issued_before(ORDER_A, NA, other, stage, u)

        x_loaded = [sem(f"x_loaded{i}") for i in range(3)]
        prev_loaded = [sem(f"previous_loaded{i}") for i in range(2)]
        set_up = sem("set_up")
        (embed_done, h_embedded, ln1_var, ln1_rstd, xn_ready, xT_done, xT_ready, qk_done, v_done, qk_taken,
         v_taken, qT_done, kT_done, vrep_done, qT_ready, kblk_ready, vblk_ready, dots_ready, s_done, s_taken,
         s_ready, ex_ready, eT_done, eT_ready, own_ready, pv_done, o_ready, oT_done, oT_ready, oproj_done,
         h_attn, ln2_var, ln2_rstd, x1_ready, x1T_done, x1T_ready, lg_done, lg_taken) = sems(
            "a_", "embed_done h_embedded ln1_var ln1_rstd xn_ready xT_done xT_ready qk_done v_done qk_taken "
                  "v_taken qT_done kT_done vrep_done qT_ready kblk_ready vblk_ready dots_ready s_done s_taken "
                  "s_ready ex_ready eT_done eT_ready own_ready pv_done o_ready oT_done oT_ready oproj_done "
                  "h_attn ln2_var ln2_rstd x1_ready x1T_done x1T_ready lg_done lg_taken")

        def zero_rows(sp, first, tiles):
            sp.dma_start(xg_dram[first * P:(first + tiles) * P].rearrange("(t p) d -> p t d", p=P),
                         ZERO[:, :].unsqueeze(1).broadcast_to([P, tiles, D])).then_inc(xg_zeroed, 16)

        def a_sync(sp):
            first_rows, first_cols = R_AT["ln1_g"], W_AT["qkv1"]
            sp.dma_start(ROWS[:, 0:first_rows], rows_in[:, 0:first_rows].broadcast_to([P, first_rows]))\
                .then_inc(loaded["first"], 16)
            sp.dma_start(KON[:, :], consts_in).then_inc(loaded["first"], 16)
            sp.dma_start(WS[:, :, 0:first_cols], w_small[:, :, 0:first_cols]).then_inc(loaded["small"], 16)
            sp.dma_start(w_tok_sb, w_tok).then_inc(loaded["w_tok"], 16)
            for stage, u in bodies(ORDER_A, NA):
                if stage == "embed" and u == TILES - 1:
                    sp.wait_ge(set_up, 2)
                    zero_rows(sp, 0, NT0)
                if stage == "embed" and u > 0:
                    wait(sp, embed_done, u - 3)
                    sp.dma_start(x_in[(u - 1) % 3], x_feat[u - 1]).then_inc(x_loaded[(u - 1) % 3], 16)
                    if u == 12:
                        sp.dma_start(ROWS[:, first_rows:], rows_in[:, first_rows:].broadcast_to([P, RCOLS - first_rows]))\
                            .then_inc(loaded["later"], 16)
                        sp.dma_start(WS[:, :, first_cols:], w_small[:, :, first_cols:]).then_inc(loaded["later"], 16)
                    if u % 2 == 0:
                        e = u // 2 - 1
                        sp.dma_start(W1[:, :, e, :], w1_0[:, :, e, :]).then_inc(loaded["experts0"], 16)
                        sp.dma_start(W2[:, e], w2_0[:, e]).then_inc(loaded["experts0"], 16)

        def a_tensor(pe):
            def embed(u):
                if u == 0:
                    return
                pe.wait_ge(x_loaded[(u - 1) % 3], 16 * ((u - 1) // 3 + 1))
                wait(pe, h_embedded, u)
                wait(pe, lg_taken, before_a("logits", "embed", u))
                for k in range(FK):
                    mm = pe.matmul(PS[:, 0, 0:D], x_in[(u - 1) % 3][:, k, :], w_tok_sb[:, k, :],
                                   start=k == 0, stop=k == FK - 1)
                mm.then_inc(embed_done, 1)

            def transposed(u, src, bank, done):
                for c in range(C):
                    mm = pe.transpose(PS[0:96, bank, c * P:(c + 1) * P], src[:, 96 * c:96 * c + 96], ident)
                mm.then_inc(done, 1)

            def projected(xt, name, a, b, bank, done):
                for c in range(C):
                    mm = pe.matmul(PS[:, bank, 0:b - a], xt[0:KC[c], c, :], w_small_at(name, c, a, b),
                                   start=c == 0, stop=c == C - 1)
                mm.then_inc(done, 1)

            def to_features(u):
                pe.wait_ge(xn_ready, u + 1)
                wait(pe, xT_ready, u)
                wait(pe, x1T_ready, before_a("x1T", "xT", u))
                transposed(u, xn[u % 2], 1, xT_done)

            def qkv(u):
                pe.wait_ge(xT_ready, u + 1)
                wait(pe, qk_taken, u)
                projected(xT[u % 2], "qkv0", 0, 2 * D, 2, qk_done)
                wait(pe, v_taken, u)
                wait(pe, h_attn, before_a("oproj", "qkv", u))
                projected(xT[u % 2], "qkv0", 2 * D, 3 * D, 3, v_done)

            def heads(u):
                pe.wait_ge(qk_taken, u + 1)
                qkv_u = QKV[u % 2]
                if u > 0:
                    wait(pe, qT_ready, u - 1)
                    wait(pe, oT_ready, before_a("oT", "heads", u))
                    transposed(u, qkv_u[:, 0:D], 4, qT_done)
                wait(pe, kblk_ready, u)
                transposed(u, qkv_u[:, D:2 * D], 5, kT_done)
                pe.wait_ge(v_taken, u + 1)
                wait(pe, vblk_ready, u)
                wait(pe, o_ready, before_a("pv", "heads", u))
                v = qkv_u[:, 2 * D:3 * D]
                if u == 0:
                    mm = pe.matmul(PS[MS * H:NV, 7, 0:D], K("first"), v, start=True, stop=True)
                else:
                    for s in range(2):
                        mm = pe.matmul(PS[0:MS * H, 7, s * D:(s + 1) * D],
                                       K("pick_v")[:, s * MS * H:(s + 1) * MS * H], v, start=True, stop=True)
                mm.then_inc(vrep_done, 1)

            def scores(u):
                if u == 0:
                    return
                pe.wait_ge(qT_ready, u)
                pe.wait_ge(kblk_ready, u + 1)
                wait(pe, s_taken, u - 1)
                wait(pe, eT_ready, before_a("expT", "scores", u) - 1)
                for s in range(2):
                    for c in range(C):
                        out_s = PS[S * s:S * s + S, 6, 0:NV].rearrange("p (m c h) -> p c m h", c=C, h=HC)[:, c]
                        mm = pe.matmul(out_s, qT[u % 2][:, c, S * s:S * s + S], kblk[u % 2][:, c, s],
                                       start=True, stop=True)
                mm.then_inc(s_done, 1)

            def exp_t(u):
                if u == 0:
                    return
                pe.wait_ge(ex_ready, u)
                wait(pe, s_taken, u)
                pe.transpose(PS[0:NV, 6, 0:P], ex[u % 2][:, 0:NV], ident).then_inc(eT_done, 1)

            def pv(u):
                if u == 0:
                    return
                pe.wait_ge(eT_ready, u)
                pe.wait_ge(vblk_ready, before_a("heads", "pv", u))
                wait(pe, o_ready, u)
                for s in range(2):
                    mm = pe.matmul(PS[S * s:S * s + S, 7, 0:D], exT[u % 2][:, S * s:S * s + S],
                                   vblk[u % 2][:, s], start=True, stop=True)
                mm.then_inc(pv_done, 1)

            def out_t(u):
                pe.wait_ge(o_ready, u + 1)
                wait(pe, oT_ready, u)
                wait(pe, qT_ready, before_a("heads", "oT", u) - 1)
                transposed(u, oatt[u % 2], 4, oT_done)

            def out_projection(u):
                pe.wait_ge(oT_ready, u + 1)
                wait(pe, h_attn, u)
                wait(pe, v_taken, before_a("qkv", "oproj", u))
                projected(oT[u % 2], "out0", 0, D, 3, oproj_done)

            def x1_t(u):
                pe.wait_ge(x1_ready, u + 1)
                wait(pe, x1T_ready, u)
                wait(pe, xT_ready, before_a("xT", "x1T", u))
                transposed(u, X1[:, tile_of(u), :], 1, x1T_done)

            def logits(u):
                pe.wait_ge(x1T_ready, u + 1)
                wait(pe, lg_taken, u)
                wait(pe, h_embedded, before_a("embed", "logits", u))
                projected(x1T[u % 2], "gate0", 0, E0, 0, lg_done)

            pe.wait_ge(loaded["first"], 16 * 2)
            pe.wait_ge(loaded["small"], 16)
            pe.wait_ge(loaded["w_tok"], 16)
            pe.wait_ge(set_up, 2)
            step = {"embed": embed, "xT": to_features, "qkv": qkv, "heads": heads, "scores": scores,
                    "expT": exp_t, "pv": pv, "oT": out_t, "oproj": out_projection, "x1T": x1_t, "logits": logits}
            for stage, u in bodies(ORDER_A, NA):
                if stage in step:
                    step[stage](u)

        def a_scalar(act):
            def copy(out_ap, in_ap):
                return act.activation(out_ap, in_ap, ACT.Copy)

            for stage, u in bodies(ORDER_A, NA):
                i = u % 2
                if stage == "xT":
                    act.wait_ge(xT_done, u + 1)
                    wait(act, v_done, u - 1)
                    copy(xT[i][0:96], PS[0:96, 1, 0:C * P].rearrange("p (c t) -> p c t", c=C)).then_inc(xT_ready, 1)
                elif stage == "qkv":
                    act.wait_ge(qk_done, u + 1)
                    wait(act, vrep_done, u - 1)
                    wait(act, own_ready, u - 2)
                    if u == 12:
                        act.wait_ge(o_ready, 1)
                    copy(QKV[i][:, 0:2 * D], PS[:, 2, 0:2 * D]).then_inc(qk_taken, 1)
                    act.wait_ge(v_done, u + 1)
                    copy(QKV[i][:, 2 * D:3 * D], PS[:, 3, 0:D]).then_inc(v_taken, 1)
                elif stage == "heads" and u > 0:
                    act.wait_ge(qT_done, u)
                    wait(act, s_done, u - 2)
                    copy(qT[i], PS[0:96, 4, 0:C * P].rearrange("p (c t) -> p c t", c=C)).then_inc(qT_ready, 1)
                    act.wait_ge(qk_taken, u + 1)
                    act.wait_ge(v_taken, u + 1)
                    for a, b in ((0, 112), (112, 127)):
                        act.dma_start(QKV[i][a + 1:b + 1, 3 * D:5 * D], QKV[i][a:b, D:3 * D]).then_inc(prev_loaded[i], 16)
                elif stage == "exp" and u > 0:
                    act.wait_ge(s_ready, u)
                    wait(act, eT_done, u - 2)
                    wait(act, own_ready, u - 2)
                    act.activation(ex[i], ssub[i], ACT.Exp, scale=HEAD_SCALE).then_inc(ex_ready, 1)
                elif stage == "expT" and u > 0:
                    act.wait_ge(eT_done, u)
                    wait(act, pv_done, u - 2)
                    copy(exT[i], PS[0:NV, 6, 0:P]).then_inc(eT_ready, 1)
                elif stage == "oT":
                    act.wait_ge(oT_done, u + 1)
                    wait(act, oproj_done, u - 1)
                    copy(oT[i][0:96], PS[0:96, 4, 0:C * P].rearrange("p (c t) -> p c t", c=C)).then_inc(oT_ready, 1)
                elif stage == "x1T":
                    act.wait_ge(x1T_done, u + 1)
                    wait(act, lg_done, u - 1)
                    copy(x1T[i][0:96], PS[0:96, 1, 0:C * P].rearrange("p (c t) -> p c t", c=C)).then_inc(x1T_ready, 1)

        def layer_norm_stats(v, chain, src, stats, mv, done):
            chain.link(v.bn_stats(stats, src))
            v.bn_aggr(mv, stats).then_inc(done, 1)

        def a_vector(v, chain):
            v.memset(minus_half, -0.5).then_inc(set_up, 1)
            for i in range(2):
                v.memset(QKV[i][:, 3 * D:5 * D], 0.0)
                v.memset(xT[i][96:97], 1.0)
                v.memset(oT[i][96:97], 1.0)
                v.memset(XGT[i][96:97], 1.0)
                v.memset(x1T[i][96:97], 1.0)
            v.memset(ZERO[:, :], 0.0).then_inc(set_up, 1)
            v.wait_ge(loaded["first"], 16 * 2)
            v.wait_ge(set_up, 2)
            for stage, u in bodies(ORDER_A, NA):
                i, t = u % 2, tile_of(u)
                if stage == "embed":
                    if u == 0:
                        v.tensor_copy(HT[:, t], ROW("cls")).then_inc(h_embedded, 1)
                    else:
                        v.wait_ge(embed_done, u)
                        v.tensor_tensor(HT[:, t], PS[:, 0, 0:D], ROW("b_tok"), ALU.add).then_inc(h_embedded, 1)
                    v.wait_ge(h_embedded, u + 1)
                    layer_norm_stats(v, chain, HT[:, t], stats1, mv1[i], ln1_var)
                elif stage == "xn":
                    v.wait_ge(ln1_rstd, u + 1)
                    wait(v, xT_done, u - 1)
                    v.tensor_scalar(xn[i], HT[:, t], mv1[i][:, 0:1], rstd1[i], ALU.subtract, ALU.mult)\
                        .then_inc(xn_ready, 1)
                elif stage == "heads":
                    v.wait_ge(kT_done, u + 1)
                    wait(v, s_done, u - 2)
                    kT = PS[0:96, 5, 0:C * P].rearrange("p (c t) -> p c t", c=C)
                    mask = head6.unsqueeze(1).unsqueeze(1)
                    if u == 0:
                        for j in range(2):
                            last = v.tensor_tensor(
                                kblk[j][:, :, :, MS, :], kT[:, :, 0:1].unsqueeze(2).broadcast_to([96, C, 2, HC]),
                                mask.broadcast_to([96, C, 2, HC]), ALU.mult)
                    else:
                        for s in range(2):
                            keys = kT[:, :, S * s + STRIDE - 1:S * (s + 1):STRIDE]
                            last = v.tensor_tensor(kblk[i][:, :, s, 0:MS, :],
                                                   keys.unsqueeze(3).broadcast_to([96, C, MS, HC]),
                                                   mask.broadcast_to([96, C, MS, HC]), ALU.mult)
                    last.then_inc(kblk_ready, 1)
                    v.wait_ge(vrep_done, u + 1)
                    wait(v, pv_done, u - 2)
                    if u == 0:
                        rows = slice(MS * H, NV)
                        for j in range(2):
                            last = v.tensor_tensor(vblk[j][rows], PS[rows, 7, 0:D].unsqueeze(1).broadcast_to([H, 2, D]),
                                                   K("head_rows")[rows].unsqueeze(1).broadcast_to([H, 2, D]), ALU.mult)
                    else:
                        n = MS * H
                        last = v.tensor_tensor(vblk[i][0:n], PS[0:n, 7, 0:2 * D].rearrange("p (s e) -> p s e", s=2),
                                               K("head_rows")[0:n].unsqueeze(1).broadcast_to([n, 2, D]), ALU.mult)
                    last.then_inc(vblk_ready, 1)
                elif stage == "scores" and u > 0:
                    v.wait_ge(s_done, u)
                    v.tensor_tensor(sraw[:, 0:NV], PS[:, 6, 0:NV], K("mask0")[:, 0:NV], ALU.add).then_inc(s_taken, 1)
                elif stage == "softmax" and u > 0:
                    v.wait_ge(dots_ready, u)
                    chain.link(v.tensor_reduce(sraw[:, NV:], prod[i].rearrange("p a (h d) -> p (a h) d", d=HD),
                                               AX.X, ALU.add))
                    chain.link(v.tensor_tensor(sraw[:, NV:], sraw[:, NV:], K("mask0")[:, NV:], ALU.add))
                    v.wait_ge(s_taken, u)
                    chain.link(v.tensor_reduce(smax, sraw.rearrange("p (m h) -> p h m", h=H), AX.X, ALU.max))
                    wait(v, ex_ready, u - 2)
                    v.tensor_tensor(ssub[i].rearrange("p (m h) -> p m h", h=H),
                                    sraw.rearrange("p (m h) -> p m h", h=H),
                                    smax.unsqueeze(1).broadcast_to([P, KEYS0, H]), ALU.subtract).then_inc(s_ready, 1)
                elif stage == "expT" and u > 0:
                    v.wait_ge(ex_ready, u)
                    chain.link(v.tensor_reduce(rsum, ex[i].rearrange("p (m h) -> p h m", h=H), AX.X, ALU.add))
                    chain.link(v.reciprocal(rinv[i], rsum))
                elif stage == "pv":
                    wait(v, oT_done, u - 1)
                    if u == 0:
                        v.wait_ge(v_taken, 1)
                        v.tensor_copy(oatt[i], QKV[i][:, 2 * D:3 * D]).then_inc(o_ready, 1)
                    else:
                        v.wait_ge(pv_done, u)
                        v.wait_ge(own_ready, u)
                        chain.link(v.tensor_tensor(o1, PS[:, 7, 0:D], own[i], ALU.add))
                        v.tensor_tensor(oatt[i].rearrange("p (h d) -> p h d", h=H),
                                        o1.rearrange("p (h d) -> p h d", h=H),
                                        rinv[i].unsqueeze(2).broadcast_to([P, H, HD]), ALU.mult).then_inc(o_ready, 1)
                elif stage == "oproj":
                    v.wait_ge(oproj_done, u + 1)
                    v.tensor_tensor(HT[:, t], PS[:, 3, 0:D], HT[:, t], ALU.add).then_inc(h_attn, 1)
                    v.wait_ge(h_attn, u + 1)
                    layer_norm_stats(v, chain, HT[:, t], stats2, mv2[i], ln2_var)
                elif stage == "x1":
                    v.wait_ge(ln2_rstd, u + 1)
                    v.tensor_scalar(X1[:, t], HT[:, t], mv2[i][:, 0:1], rstd2[i], ALU.subtract, ALU.mult)\
                        .then_inc(x1_ready, 1)
                elif stage == "logits":
                    v.wait_ge(lg_done, u + 1)
                    v.tensor_copy(LG[:, t], PS[:, 0, 0:E0]).then_inc(lg_taken, 1)

        def root(g, chain, mv, var_eps, rstd, done):
            chain.link(g.tensor_scalar(var_eps, mv[:, 1:2], EPS_LN, None, ALU.add))
            g.tensor_tensor(rstd, var_eps, minus_half, ALU.pow).then_inc(done, 1)

        def a_gpsimd(g, chain):
            g.wait_ge(set_up, 1)
            for stage, u in bodies(ORDER_A, NA):
                i = u % 2
                if stage == "embed":
                    g.wait_ge(ln1_var, u + 1)
                    root(g, chain, mv1[i], var_eps1, rstd1[i], ln1_rstd)
                elif stage == "oproj":
                    g.wait_ge(ln2_var, u + 1)
                    root(g, chain, mv2[i], var_eps2, rstd2[i], ln2_rstd)
                elif stage == "dots" and u > 0:
                    g.wait_ge(qk_taken, u + 1)
                    n = (u + 1) // 2 if i else u // 2
                    g.wait_ge(prev_loaded[i], 32 * n)
                    wait(g, s_ready, u - 2)
                    keys = QKV[i][:, D:5 * D].rearrange("p (a e) -> p a e", a=2)[:, :, 0:D]
                    g.tensor_tensor(prod[i], keys, QKV[i][:, 0:D].unsqueeze(1).broadcast_to([P, 2, D]), ALU.mult)\
                        .then_inc(dots_ready, 1)
                elif stage == "expT" and u > 0:
                    g.wait_ge(ex_ready, u)
                    vals = QKV[i][:, D:5 * D].rearrange("p (a e) -> p a e", a=2)[:, :, D:2 * D]
                    w = ex[i][:, NV:].unsqueeze(2).broadcast_to([P, 2 * H, HD])
                    chain.link(g.tensor_tensor(own2.rearrange("p a (h d) -> p a h d", h=H),
                                               vals.rearrange("p a (h d) -> p a h d", h=H),
                                               w.rearrange("p (a h) d -> p a h d", a=2), ALU.mult))
                    wait(g, o_ready, u - 1)
                    g.tensor_tensor(own[i], own2[:, 0], own2[:, 1], ALU.add).then_inc(own_ready, 1)


        (r_shifted, r_exp, r_onehot, r_counted, r_slots, r_done) = sems(
            "r_", "shifted exp onehot counted slots done")

        def r_vector(v, chain, layer):
            E, top, tiles = ((E0, TOP0, NT0), (E1, TOP1, NT1))[layer]

            def grid(a):
                return a[:, 0:TILES * E].rearrange("p (t e) -> p t e", e=E)

            def per_tile(a):
                return a.unsqueeze(2).broadcast_to([P, TILES, E])

            def per_expert(a):
                return a.unsqueeze(1).broadcast_to([P, TILES, E])

            lg, ex_, pr, eq, pk, off = LG[:, :, 0:E], grid(g_exp), grid(g_prob), grid(g_eq), grid(g_pick), grid(g_off)
            hot = [grid(a) for a in g_onehot]
            v.wait_ge(lg_taken, TILES * (layer + 1))
            v.wait_ge(loaded["later"], 16 * 2)
            chain.link(v.tensor_reduce(g_max, lg, AX.X, ALU.max))
            v.tensor_tensor(ex_, lg, per_tile(g_max), ALU.subtract).then_inc(r_shifted, 1)
            v.wait_ge(r_exp, layer + 1)
            chain.link(v.tensor_reduce(g_sum, pr, AX.X, ALU.add))
            chain.link(v.reciprocal(g_sum, g_sum))
            chain.link(v.tensor_tensor(pr, pr, per_tile(g_sum), ALU.mult))
            src = pr
            for k in range(top):
                chain.link(v.tensor_reduce(PROB[:, k], src, AX.X, ALU.max))
                chain.link(v.tensor_tensor(eq, src, per_tile(PROB[:, k]), ALU.is_equal))
                chain.link(v.tensor_tensor(pk, eq, per_expert(K("prio")[:, 0:E]), ALU.mult))
                chain.link(v.tensor_reduce(g_max, pk, AX.X, ALU.max))
                chain.link(v.tensor_tensor(hot[k], pk, per_tile(g_max), ALU.is_equal))
                if k + 1 < top:
                    chain.link(v.scalar_tensor_tensor(ex_, hot[k], -2.0, pr, ALU.mult, ALU.add))
                    src = ex_
            for k in range(top):
                chain.link(v.tensor_tensor(hot[k], hot[k], per_tile(K("valid")), ALU.mult))
            if top == 2:
                v.tensor_tensor(hot[2], hot[0], hot[1], ALU.add).then_inc(r_onehot, 1)
            else:
                v.tensor_copy(hot[2], hot[0]).then_inc(r_onehot, 1)
            v.wait_ge(r_counted, layer + 1)
            rows_before = PS[:, 0, 0:TILES * E].rearrange("p (t e) -> p t e", e=E)
            counts = PS[:, 1, 0:TILES * E].rearrange("p (t e) -> p t e", e=E)
            scan = g_scan[:, 0:TILES * E].rearrange("p (e t) -> p e t", e=E)
            for e in range(E):
                last = v.tensor_tensor_scan(scan[:, e], K("ones")[:, 0:TILES], counts[:, :, e], 0.0, ALU.mult, ALU.add)
            chain.link(last)
            chain.link(v.tensor_tensor(off, rows_before, scan.rearrange("p e t -> p t e"), ALU.add))
            chain.link(v.tensor_tensor(off, off, counts, ALU.subtract))
            tl, cum, base = g_tiles[:, 0:E], g_cum[:, 0:E], g_base[:, 0:E]
            chain.link(v.tensor_scalar(tl, scan[:, :, TILES - 1], 1.0 / P, (P - 1) / P - (P - 1) / (2 * P), ALU.mult, ALU.add))
            chain.link(v.tensor_scalar(tl, tl, MAGIC, MAGIC, ALU.add, ALU.subtract))
            chain.link(v.tensor_tensor_scan(cum, K("ones")[:, 0:E], tl, 0.0, ALU.mult, ALU.add))
            chain.link(v.tensor_tensor(base, cum, tl, ALU.subtract))
            chain.link(v.scalar_tensor_tensor(off, per_expert(base), float(P), off, ALU.mult, ALU.add))
            for k in range(top):
                chain.link(v.tensor_tensor(pk, hot[k], off, ALU.mult))
                chain.link(v.tensor_reduce(g_max, pk, AX.X, ALU.add))
                last = v.tensor_copy(SLOT[:, k], g_max)
                last.then_inc(r_slots, 1)
                v.wait_ge(r_slots, (0, TOP0)[layer] + k + 1)
            le = g_le[:, 0:tiles * E].rearrange("p (t e) -> p t e", e=E)
            chain.link(v.tensor_tensor(le, cum.unsqueeze(1).broadcast_to([P, tiles, E]),
                                       K("tile_no")[:, 0:tiles].unsqueeze(2).broadcast_to([P, tiles, E]), ALU.is_le))
            chain.link(v.tensor_reduce(g_eid[:, 0:tiles], le, AX.X, ALU.add))
            v.tensor_scalar(EID[:, 0:tiles], g_eid[:, 0:tiles], float(E - 1), None, ALU.min).then_inc(r_done, 1)
            v.wait_ge(r_done, layer + 1)

        def r_scalar(act, layer):
            E = (E0, E1)[layer]
            act.wait_ge(r_shifted, layer + 1)
            act.activation(g_prob[:, 0:TILES * E], g_exp[:, 0:TILES * E], ACT.Exp).then_inc(r_exp, 1)

        def r_tensor(pe, layer, bank_free):
            E = (E0, E1)[layer]
            pe.wait_ge(loaded["later"], 16 * 2)
            pe.wait_ge(r_onehot, layer + 1)
            bank_free(pe)
            pe.matmul(PS[:, 0, 0:TILES * E], K("before"), g_onehot[2][:, 0:TILES * E], start=True, stop=True)
            pe.matmul(PS[:, 1, 0:TILES * E], K("ones"), g_onehot[2][:, 0:TILES * E], start=True, stop=True)\
                .then_inc(r_counted, 1)

        def r_gpsimd(g, layer):
            top = (TOP0, TOP1)[layer]
            g.wait_ge(xg_zeroed, 16 * (1, 1 + ZERO_PARTS)[layer])
            for k in range(top):
                g.wait_ge(r_slots, (0, TOP0)[layer] + k + 1)
                for t in range(TILES):
                    n = P if t < CLS else IMAGES
                    g.indirect_dma_start(out=xg_dram[0:(NT0, NT1)[layer] * P], out_offset=bass.IndirectOffsetOnAxis(ap=SLOT[0:n, k, t:t + 1], axis=0),
                                         in_=X1[0:n, t], in_offset=None).then_inc(xg_written, 16)

        xg_written = sem("xg_written")
        xg_loaded = [sem(f"xg_loaded{i}") for i in range(3)]
        yg_stored = [sem(f"yg_stored{i}") for i in range(2)]
        (m_xT_done, m_xT_ready, m_h_done, m_act_ready, m_hT_done, m_hT_ready_a, m_hT_ready_v, m_y_done,
         m_y_ready) = sems("m_", "xT_done xT_ready h_done act_ready hT_done hT_ready_a hT_ready_v y_done y_ready")
        ORDER_M = [("hT", 2), ("xT", 0), ("h", 1), ("y", 2)]
        LAYER = ((E0, NT0, 0), (E1, NT1, NT0))

        def m_items(layer):
            _, tiles, _ = LAYER[layer]
            return bodies(ORDER_M, {s: tiles for s, _ in ORDER_M})

        def m_sync(sp, layer):
            _, tiles, t0 = LAYER[layer]
            sp.wait_ge(xg_written, 16 * TILES * (TOP0, TOP0 + TOP1)[layer])
            for stage, j in bodies([("load", 0), ("store", 3)], {"load": tiles, "store": tiles}):
                n = t0 + j
                if stage == "load":
                    wait(sp, m_xT_done, n - 2)
                    sp.dma_start(XG_IN[n % 3], xg_dram[j * P:(j + 1) * P]).then_inc(xg_loaded[n % 3], 16)
                else:
                    sp.wait_ge(m_y_ready, n + 1)
                    sp.dma_start(yg_dram[j * P:(j + 1) * P], YG[n % 2]).then_inc(yg_stored[n % 2], 16)

        def m_tensor(pe, layer):
            E, tiles, t0 = LAYER[layer]
            pe.wait_ge(r_done, layer + 1)
            experts = {}
            for stage, j in m_items(layer):
                n = t0 + j
                i = n % 2
                if stage == "xT":
                    pe.wait_ge(xg_loaded[n % 3], 16 * (n // 3 + 1))
                    wait(pe, m_xT_ready, n)
                    for c in range(C):
                        mm = pe.transpose(PS[0:96, 0, c * P:(c + 1) * P], XG_IN[n % 3][:, 96 * c:96 * c + 96], ident)
                    mm.then_inc(m_xT_done, 1)
                elif stage == "h":
                    e = pe.value_load(EID[0:1, j:j + 1], min_val=0, max_val=E - 1)
                    experts[j] = e
                    pe.wait_ge(m_xT_ready, n + 1)
                    wait(pe, m_act_ready, n)
                    for b in range(2):
                        for c in range(C):
                            mm = pe.matmul(PS[:, 2 + b, 0:HALF], XGT[i][0:KC[c], c],
                                           W1[0:KC[c], c, bass.ds(e, 1), b * HALF:(b + 1) * HALF]
                                           .rearrange("p a f -> p (a f)"), start=c == 0, stop=c == C - 1)
                    mm.then_inc(m_h_done, 1)
                elif stage == "hT":
                    pe.wait_ge(m_act_ready, n + 1)
                    wait(pe, m_hT_ready_a, n)
                    wait(pe, m_hT_ready_v, n)
                    for k in range(FFK):
                        mm = pe.transpose(PS[:, 4 + k // 3, (k % 3) * P:(k % 3 + 1) * P],
                                          HID[i][:, k * P:(k + 1) * P], ident)
                    mm.then_inc(m_hT_done, 1)
                elif stage == "y":
                    e = experts.pop(j)
                    pe.wait_ge(m_hT_ready_a, n + 1)
                    pe.wait_ge(m_hT_ready_v, n + 1)
                    wait(pe, m_y_ready, n)
                    for k in range(FFK):
                        mm = pe.matmul(PS[:, 6, 0:D], HIDT[i][:, k],
                                       W2[:, bass.ds(e, 1), k].rearrange("p a d -> p (a d)"),
                                       start=k == 0, stop=k == FFK - 1)
                    mm.then_inc(m_y_done, 1)

        def m_scalar(act, layer):
            _, _, t0 = LAYER[layer]
            func = (ACT.Gelu, ACT.Relu)[layer]
            for stage, j in m_items(layer):
                n = t0 + j
                i = n % 2
                if stage == "xT":
                    act.wait_ge(m_xT_done, n + 1)
                    wait(act, m_h_done, n - 1)
                    act.activation(XGT[i][0:96], PS[0:96, 0, 0:C * P].rearrange("p (c t) -> p c t", c=C),
                                   ACT.Copy).then_inc(m_xT_ready, 1)
                elif stage == "h":
                    act.wait_ge(m_h_done, n + 1)
                    wait(act, m_hT_done, n - 1)
                    act.activation(HID[i].rearrange("p (b f) -> p b f", b=2), PS[:, 2:4, 0:HALF], func)\
                        .then_inc(m_act_ready, 1)
                elif stage == "hT":
                    act.wait_ge(m_hT_done, n + 1)
                    wait(act, m_y_done, n - 1)
                    act.activation(HIDT[i][:, 0:3], PS[:, 4, 0:3 * P].rearrange("p (k t) -> p k t", k=3),
                                   ACT.Copy).then_inc(m_hT_ready_a, 1)

        def m_vector(v, layer):
            E, _, t0 = LAYER[layer]
            for stage, j in m_items(layer):
                n = t0 + j
                i = n % 2
                if stage == "hT":
                    v.wait_ge(m_hT_done, n + 1)
                    wait(v, m_y_done, n - 1)
                    v.tensor_copy(HIDT[i][:, 3:6], PS[:, 5, 0:3 * P].rearrange("p (k t) -> p k t", k=3))\
                        .then_inc(m_hT_ready_v, 1)
                elif stage == "y":
                    e = v.value_load(EID[0:1, j:j + 1], min_val=0, max_val=E - 1)
                    v.wait_ge(m_y_done, n + 1)
                    wait(v, yg_stored[i], 16 * ((n - 2) // 2 + 1))
                    b2 = ROWS[:, bass.ds(e * D + R_AT[("b2_0", "b2_1")[layer]], D)]
                    v.tensor_tensor(YG[i], PS[:, 6, 0:D], b2, ALU.add).then_inc(m_y_ready, 1)

        taken[0] = between_start
        Y = [area(D) for _ in range(3)]
        c_stats = area(6)
        c_mv = [area(2) for _ in range(2)]
        c_eps, c_minus_half, c_magic = area(1), area(1), area(1)
        c_rstd = [area(1) for _ in range(2)]
        inv_q, inv_k, inv_v, alpha, beta = [area(1) for _ in range(5)]
        c_xn = [area(D) for _ in range(2)]
        common_start = taken[0]

        def half_area(width, parts=P):
            return area((width + 1) // 2, parts).bitcast(BF16)[:, 0:width]

        def tokens(parts=97):
            return area(C * 2 * TOK, parts).rearrange("p (c t) -> p c t", c=C)

        def patches(a):
            return a[:, :, 0:P].rearrange("p c (s t) -> p c s t", s=2)

        c_xT = [tokens() for _ in range(2)]
        clsT = area(C * IMAGES, 97).rearrange("p (c b) -> p c b", c=C)
        clsOT = area(C * IMAGES, 97).rearrange("p (c b) -> p c b", c=C)
        cls_v = half_area(D, IMAGES)
        ident_h = half_area(P)
        twice = half_area(2 * P).rearrange("p (s d t) -> p s d t", s=2, d=2)
        t_qk = [area(2 * C * 2 * TOK, 96).rearrange("p (a c t) -> p a c t", a=2, c=C) for _ in range(2)]
        t_v = [area(D) for _ in range(2)]
        t_v_h = [half_area(D) for _ in range(2)]
        t_s = [area(3 * C * 2 * TOK).rearrange("p (j t) -> p j t", j=3) for _ in range(2)]
        t_sc = [area(2 * TOK, H).rearrange("p (s t) -> p s t", s=2) for _ in range(2)]
        t_o = [area(C * 2 * TOK, 96).rearrange("p (c s t) -> p c s t", c=C, s=2) for _ in range(2)]
        q_h = [half_area(C * 2 * TOK, 96).rearrange("p (c s t) -> p c s t", c=C, s=2) for _ in range(2)]
        k_h = [half_area(C * 2 * P, 96).rearrange("p (c s a t) -> p c s a t", c=C, s=2, a=2) for _ in range(2)]
        kc_h = [half_area(C * 2 * H, 96).rearrange("p (c s h) -> p c s h", c=C, s=2) for _ in range(2)]
        v_h = [half_area(2 * D).rearrange("p (s e) -> p s e", s=2) for _ in range(2)]
        c_kc = area(2 * C, 96).rearrange("p (c s) -> p c s", c=C)
        vc_h = [half_area(2 * D, H).rearrange("p (s e) -> p s e", s=2) for _ in range(2)]
        a_h = [half_area(3 * C * 2 * TOK).rearrange("p (j t) -> p j t", j=3) for _ in range(2)]
        ac_h = [half_area(2 * TOK, H).rearrange("p (s t) -> p s t", s=2) for _ in range(2)]
        c_oT = [chunks(97) for _ in range(2)]

        c_gathered = [sem(f"c_gathered{i}") for i in range(3)]
        (h_moe, q_var, q_rstd, q_xn, q_xT_done, q_xT_ready, q_cls_ready, q_qk_done, q_v_done, q_vc_done,
         q_qk_taken, q_v_taken, q_qk_clipped, q_q_ready, q_k_ready, q_kc_ready, q_v_whole, q_vrep_done, q_v_ready, q_vc_ready, q_s_done, q_s_taken,
         q_s_clipped, q_a_ready, q_pv_done, q_o_taken, q_o_clipped, q_oT_ready, q_oproj_done, h_quant) = sems(
            "q_", "moe var rstd xn xT_done xT_ready cls_ready qk_done v_done vc_done qk_taken v_taken "
                  "qk_clipped q_ready k_ready kc_ready v_whole vrep_done v_ready vc_ready s_done s_taken s_clipped a_ready pv_done o_taken "
                  "o_clipped oT_ready oproj_done h_quant")
        loaded_experts1 = sem("loaded_experts1")
        ORDER_Q = [("gather", 0), ("oproj", 6), ("quant", 4), ("xT", 3), ("pv", 5), ("vrep", 4), ("moe", 2),
                   ("scores", 4), ("norm", 2), ("qkv", 3)]
        NQ = {s: TILES for s, _ in ORDER_Q}

        def before_q(other, stage, u):
            return issued_before(ORDER_Q, NQ, other, stage, u)

        def stored_total(layer):
            n = LAYER[layer][1] + LAYER[layer][2]
            return [16 * ((n + 1 - i) // 2) for i in range(2)]

        def experts_done(eng, layer):
            for i, n in enumerate(stored_total(layer)):
                eng.wait_ge(yg_stored[i], n)

        def q_sync(sp):
            experts_done(sp, 0)
            for part in range(ZERO_PARTS):
                sp.wait_ge(h_moe, part + 1)
                zero_rows(sp, part * NT1 // ZERO_PARTS, NT1 // ZERO_PARTS)
            for e in range(E1):
                sp.wait_ge(h_moe, ZERO_PARTS + 2 * e + 2)
                sp.dma_start(W1[:, :, e, :], w1_1[:, :, e, :]).then_inc(loaded_experts1, 16)
                sp.dma_start(W2[:, e], w2_1[:, e]).then_inc(loaded_experts1, 16)

        def q_tensor(pe):
            def to_features(u):
                pe.wait_ge(q_xn, u + 1)
                wait(pe, q_xT_ready, u)
                wait(pe, q_v_taken, u)
                for c in range(C):
                    mm = pe.transpose(PS[0:96, 0, c * P:(c + 1) * P], c_xn[u % 2][:, 96 * c:96 * c + 96], ident)
                mm.then_inc(q_xT_done, 1)

            def qkv(u):
                pe.wait_ge(q_xT_ready, u + 1)
                if u == 0:
                    for c in range(C):
                        mm = pe.matmul(PS[0:IMAGES, 0, C * P:C * P + D], clsT[0:KC[c], c],
                                       w_small_at("qkv1", c, 2 * D, 3 * D), start=c == 0, stop=c == C - 1)
                    mm.then_inc(q_v_done, 1)
                    return
                x = c_xT[u % 2]
                for c in range(C):
                    mm = pe.matmul(PS[:, 0, C * P:C * P + D], x[0:KC[c], c, 0:P], w_small_at("qkv1", c, 2 * D, 3 * D),
                                   start=c == 0, stop=c == C - 1)
                mm.then_inc(q_v_done, 1)
                pe.wait_ge(q_cls_ready, u)
                wait(pe, q_qk_taken, u - 1)
                wait(pe, q_vc_ready, before_q("vrep", "qkv", u) - 1)
                for a in range(2):
                    for oc in range(C):
                        for c in range(C):
                            at = a * D + 96 * oc
                            mm = pe.matmul(PS[0:96, 1 + a, oc * 2 * TOK:(oc + 1) * 2 * TOK],
                                           w_small_at("qkv1", c, at, at + 96), x[0:KC[c], c],
                                           start=c == 0, stop=c == C - 1)
                mm.then_inc(q_qk_done, 1)

            def replicate(u):
                if u == 0:
                    return
                pe.wait_ge(q_v_whole, u + 1)
                wait(pe, q_v_ready, u - 1)
                for s in range(2):
                    mm = pe.matmul(PS[:, 3, s * D:(s + 1) * D], twice[:, s].rearrange("p d t -> p (d t)"),
                                   t_v_h[u % 2], start=True, stop=True)
                mm.then_inc(q_vrep_done, 1)
                wait(pe, q_vc_ready, u - 1)
                wait(pe, q_qk_taken, before_q("qkv", "vrep", u) - 1)
                for s in range(2):
                    b = 2 * (u - 1) + s
                    mm = pe.matmul(PS[0:H, 1 + s, 4 * TOK:4 * TOK + D], ident_h[0:IMAGES, b:b + 1].broadcast_to([IMAGES, H]),
                                   cls_v, start=True, stop=True)
                mm.then_inc(q_vc_done, 1)

            def scores(u):
                if u == 0:
                    return
                q, k, kc = q_h[u % 2], k_h[u % 2], kc_h[u % 2]
                pe.wait_ge(q_q_ready, u)
                pe.wait_ge(q_k_ready, u)
                pe.wait_ge(q_kc_ready, u)
                wait(pe, q_s_taken, u - 1)
                wait(pe, h_quant, before_q("oproj", "scores", u) - 1)
                for c in range(C):
                    for s in range(2):
                        for j in range(3):
                            r, at = slice(32 * j, 32 * j + 32), (2 * c + s) * TOK
                            pe.matmul(PS[:, 4 + j, at:at + TOK], k[r, c, s].rearrange("p a t -> p (a t)"),
                                      q[r, c, s], start=True, stop=True)
                for s in range(2):
                    for c in range(C):
                        mm = pe.matmul(PS[0:H, 4, (4 + s) * TOK:(5 + s) * TOK], kc[:, c, s], q[:, c, s],
                                       start=c == 0, stop=c == C - 1)
                mm.then_inc(q_s_done, 1)

            def pv(u):
                if u == 0:
                    return
                pe.wait_ge(q_a_ready, u)
                pe.wait_ge(q_v_ready, u)
                pe.wait_ge(q_vc_ready, u)
                wait(pe, q_o_taken, u - 1)
                for s in range(2):
                    for c in range(C):
                        out_at = PS[0:96, 7, (c * 2 + s) * TOK:(c * 2 + s + 1) * TOK]
                        pe.matmul(out_at, vc_h[u % 2][:, s, 96 * c:96 * c + 96], ac_h[u % 2][:, s],
                                  start=True, stop=False, skip_group_check=True)
                        for jj in range(3):
                            cols = slice(96 * c + 32 * jj, 96 * c + 32 * jj + 32)
                            mm = pe.matmul(PS[32 * jj:32 * jj + 32, 7, (c * 2 + s) * TOK:(c * 2 + s + 1) * TOK],
                                           v_h[u % 2][:, s, cols], a_h[u % 2][:, jj, (c * 2 + s) * TOK:(c * 2 + s + 1) * TOK],
                                           start=False, stop=True, skip_group_check=True)
                mm.then_inc(q_pv_done, 1)

            def out_projection(n, u):
                pe.wait_ge(q_oT_ready, u or PAIRS)
                wait(pe, h_quant, n - 1)
                wait(pe, q_s_taken, before_q("scores", "oproj", u) - 1 if u else PAIRS)
                m = IMAGES if u == 0 else P
                for c in range(C):
                    o = clsOT[0:KC[c], c] if u == 0 else c_oT[u % 2][0:KC[c], c]
                    mm = pe.matmul(PS[0:m, 5, 4 * TOK:4 * TOK + D], o, w_small_at("out1", c, 0, D), start=c == 0, stop=c == C - 1)
                mm.then_inc(q_oproj_done, 1)

            pe.wait_ge(set_up, 3)
            for stage, u in bodies(ORDER_Q, NQ):
                if stage == "xT":
                    to_features(u)
                elif stage == "qkv":
                    qkv(u)
                elif stage == "vrep":
                    replicate(u)
                elif stage == "scores":
                    scores(u)
                elif stage == "pv":
                    pv(u)
                elif stage == "oproj" and u > 0:
                    out_projection(u, u)
            out_projection(TILES, 0)

        def q_scalar(act):
            def rounded(out_ap, in_ap, scale):
                n = in_ap.shape[0]
                return act.activation(out_ap, in_ap, ACT.Identity, bias=c_magic[0:n], scale=scale[0:n])

            act.wait_ge(set_up, 3)
            for stage, u in bodies(ORDER_Q, NQ):
                i = u % 2
                if stage == "xT":
                    act.wait_ge(q_xT_done, u + 1)
                    ps = PS[0:96, 0, 0:C * P].rearrange("p (c t) -> p c t", c=C)
                    if u == 0:
                        act.activation(clsT[0:96], ps[:, :, 0:IMAGES], ACT.Copy).then_inc(q_xT_ready, 1)
                    else:
                        wait(act, q_qk_done, u - 2)
                        act.activation(c_xT[i][0:96, :, 0:P], ps, ACT.Copy).then_inc(q_xT_ready, 1)
                elif stage == "qkv":
                    act.wait_ge(q_v_done, u + 1)
                    wait(act, q_v_whole, u - 1)
                    n = IMAGES if u == 0 else P
                    rounded(t_v[i][0:n], PS[0:n, 0, C * P:C * P + D], inv_v).then_inc(q_v_taken, 1)
                    if u > 0:
                        act.wait_ge(q_qk_done, u)
                        wait(act, q_q_ready, u - 2)
                        wait(act, q_k_ready, u - 2)
                        wait(act, q_kc_ready, u - 2)
                        for a, inv in ((0, inv_q), (1, inv_k)):
                            last = rounded(t_qk[i][:, a], PS[0:96, 1 + a, 0:C * 2 * TOK]
                                           .rearrange("p (c t) -> p c t", c=C), inv)
                        last.then_inc(q_qk_taken, 1)
                elif stage == "scores" and u > 0:
                    act.wait_ge(q_s_done, u)
                    wait(act, q_a_ready, u - 2)
                    rounded(t_s[i], PS[:, 4:7, 0:4 * TOK], alpha)
                    rounded(t_sc[i], PS[0:H, 4, 4 * TOK:6 * TOK].rearrange("p (s t) -> p s t", s=2), alpha).then_inc(q_s_taken, 1)
                elif stage == "pv" and u > 0:
                    act.wait_ge(q_pv_done, u)
                    wait(act, q_oT_ready, u - 2)
                    rounded(t_o[i], PS[0:96, 7, 0:C * 2 * TOK].rearrange("p (c s t) -> p c s t", c=C, s=2), beta)\
                        .then_inc(q_o_taken, 1)

        def q_vector(v, chain):
            def clip(x, lo, hi):
                return v.tensor_scalar(x, x, MAGIC + lo, MAGIC + hi, ALU.max, ALU.min)

            experts_done(v, 0)
            v.memset(c_minus_half, -0.5)
            v.memset(c_magic, MAGIC)
            for i in range(2):
                v.memset(c_xT[i][96:97], 1.0)
                v.memset(c_oT[i][96:97], 1.0)
            v.memset(clsT[96:97], 1.0)
            v.memset(clsOT[96:97], 1.0)
            v.tensor_copy(ident_h, ident)
            for s in range(2):
                last = v.tensor_copy(twice[:, s], ident[:, s * S:(s + 1) * S].unsqueeze(1).broadcast_to([P, 2, S]))
            chain.link(last)
            chain.link(v.reciprocal(inv_q, ROW("s_q", 1)))
            chain.link(v.reciprocal(inv_k, ROW("s_k", 1)))
            chain.link(v.reciprocal(inv_v, ROW("s_v", 1)))
            chain.link(v.reciprocal(alpha, ROW("s_attn", 1)))
            chain.link(v.tensor_scalar(alpha, alpha, float(np.float32(HEAD_SCALE) * np.float32(1.0 / TOK)), None, ALU.mult))
            chain.link(v.tensor_tensor(alpha, alpha, ROW("s_q", 1), ALU.mult))
            chain.link(v.tensor_tensor(alpha, alpha, ROW("s_k", 1), ALU.mult))
            chain.link(v.reciprocal(beta, ROW("s_after", 1)))
            chain.link(v.tensor_tensor(beta, beta, ROW("s_attn", 1), ALU.mult))
            v.tensor_tensor(beta, beta, ROW("s_v", 1), ALU.mult).then_inc(set_up, 1)
            for stage, u in bodies(ORDER_Q, NQ):
                i, t = u % 2, tile_of(u)
                if stage == "moe":
                    v.wait_ge(c_gathered[u % 3], 16 * (u // 3 + 1))
                    n = IMAGES if u == 0 else P
                    v.scalar_tensor_tensor(HT[0:n, t], Y[u % 3][0:n], PROB[0:n, 0, t:t + 1], HT[0:n, t], ALU.mult,
                                           ALU.add)\
                        .then_inc(h_moe, 1)
                    v.wait_ge(h_moe, u + 1)
                    layer_norm_stats(v, chain, HT[:, t], c_stats, c_mv[i], q_var)
                elif stage == "norm":
                    v.wait_ge(q_rstd, u + 1)
                    wait(v, q_xT_done, u - 1)
                    v.tensor_scalar(c_xn[i], HT[:, t], c_mv[i][:, 0:1], c_rstd[i], ALU.subtract, ALU.mult)\
                        .then_inc(q_xn, 1)
                elif stage == "qkv":
                    v.wait_ge(q_v_taken, u + 1)
                    n = IMAGES if u == 0 else P
                    chain.link(clip(t_v[i][0:n], LEVEL_LO, LEVEL_HI))
                    wait(v, q_vrep_done, u - 2)
                    v.tensor_scalar(cls_v if u == 0 else t_v_h[i], t_v[i][0:n], MAGIC, None, ALU.subtract)\
                        .then_inc(q_v_whole, 1)
                elif stage == "quant" and u > 0:
                    v.wait_ge(q_qk_taken, u)
                    clip(t_qk[i], LEVEL_LO, LEVEL_HI).then_inc(q_qk_clipped, 1)
                    v.wait_ge(q_qk_clipped, u)
                    wait(v, q_s_done, u - 2)
                    k = t_qk[i][:, 1]
                    for a in range(2):
                        last = v.tensor_scalar(k_h[i][:, :, :, a], patches(k), MAGIC, K("half")[0:96, a:a + 1],
                                               ALU.subtract, ALU.mult)
                    last.then_inc(q_k_ready, 1)
                    v.tensor_scalar(q_h[i][:, :, :, 0:S], patches(t_qk[i][:, 0]), MAGIC, None, ALU.subtract)\
                        .then_inc(q_q_ready, 1)
                elif stage == "vrep" and u > 0:
                    v.wait_ge(q_vrep_done, u)
                    wait(v, q_pv_done, u - 2)
                    v.tensor_tensor(v_h[i], PS[:, 3, 0:2 * D].rearrange("p (s e) -> p s e", s=2),
                                    K("half_cols").unsqueeze(1).broadcast_to([P, 2, D]), ALU.mult)\
                        .then_inc(q_v_ready, 1)
                    v.wait_ge(q_vc_done, u)
                    v.tensor_tensor(vc_h[i], PS[0:H, 1:3, 4 * TOK:4 * TOK + D],
                                    K("head_rows")[0:H].unsqueeze(1).broadcast_to([H, 2, D]), ALU.mult)\
                        .then_inc(q_vc_ready, 1)
                elif stage == "scores" and u > 0:
                    v.wait_ge(q_s_taken, u)
                    clip(t_s[i], 0.0, LEVEL_ATTN)
                    chain.link(clip(t_sc[i], 0.0, LEVEL_ATTN))
                    wait(v, q_pv_done, u - 2)
                    v.tensor_scalar(ac_h[i], t_sc[i], MAGIC, None, ALU.subtract)
                    v.tensor_scalar(a_h[i], t_s[i], MAGIC, None, ALU.subtract).then_inc(q_a_ready, 1)
                elif stage == "pv" and u > 0:
                    v.wait_ge(q_o_taken, u)
                    clip(t_o[i], LEVEL_LO, LEVEL_HI).then_inc(q_o_clipped, 1)
                    v.wait_ge(q_o_clipped, u)
                    wait(v, q_oproj_done, u - 2)
                    v.tensor_scalar(patches(c_oT[i][0:96]), t_o[i][:, :, :, 0:S], MAGIC, ROW("s_after", 1)[0:96], ALU.subtract, ALU.mult)
                    b = 2 * (u - 1)
                    v.tensor_scalar(clsOT[0:96, :, b:b + 2], t_o[i][:, :, :, S], MAGIC, ROW("s_after", 1)[0:96],
                                    ALU.subtract, ALU.mult).then_inc(q_oT_ready, 1)
                elif stage == "oproj" and u > 0:
                    v.wait_ge(q_oproj_done, u)
                    v.tensor_tensor(HT[:, t], PS[:, 5, 4 * TOK:4 * TOK + D], HT[:, t], ALU.add).then_inc(h_quant, 1)
            v.wait_ge(q_oproj_done, TILES)
            v.tensor_tensor(HT[0:IMAGES, CLS], PS[0:IMAGES, 5, 4 * TOK:4 * TOK + D], HT[0:IMAGES, CLS], ALU.add).then_inc(h_quant, 1)

        def q_gpsimd(g, chain):
            experts_done(g, 0)
            for stage, u in bodies(ORDER_Q, NQ):
                i, t = u % 2, tile_of(u)
                if stage == "gather":
                    n = IMAGES if u == 0 else P
                    wait(g, h_moe, u - 2)
                    g.indirect_dma_start(out=Y[u % 3][0:n], out_offset=None, in_=yg_dram[0:NT0 * P],
                                         in_offset=bass.IndirectOffsetOnAxis(ap=SLOT[0:n, 0, t:t + 1], axis=0))\
                        .then_inc(c_gathered[u % 3], 16)
                elif stage == "moe":
                    g.wait_ge(set_up, 3)
                    g.wait_ge(q_var, u + 1)
                    wait(g, q_rstd, u)
                    chain.link(g.tensor_scalar(c_eps, c_mv[i][:, 1:2], EPS_LN, None, ALU.add))
                    g.tensor_tensor(c_rstd[i], c_eps, c_minus_half, ALU.pow).then_inc(q_rstd, 1)
                elif stage == "xT" and u > 0:
                    g.wait_ge(q_xT_ready, 1)
                    wait(g, q_qk_done, u - 2)
                    b = 2 * (u - 1)
                    g.tensor_copy(c_xT[i][0:96, :, P:], clsT[0:96, :, b:b + 2]).then_inc(q_cls_ready, 1)
                elif stage == "quant" and u > 0:
                    g.wait_ge(q_qk_clipped, u)
                    wait(g, q_s_done, u - 2)
                    g.tensor_scalar(q_h[i][:, :, :, S], t_qk[i][:, 0, :, P:], MAGIC, None, ALU.subtract)
                    wait(g, q_kc_ready, u - 1)
                    chain.link(g.tensor_scalar(c_kc, t_qk[i][:, 1, :, P:], MAGIC, None, ALU.subtract))
                    g.tensor_tensor(kc_h[i], c_kc.unsqueeze(3).broadcast_to([96, C, 2, H]),
                                    K("head12")[0:96].rearrange("p (c h) -> p c h", c=C).unsqueeze(2)
                                    .broadcast_to([96, C, 2, H]), ALU.mult).then_inc(q_kc_ready, 1)

        taken[0] = common_start
        G = 2 * 2 * 3
        z_xT = [chunks(97) for _ in range(2)]
        z_clsT = area(C * IMAGES, 97).rearrange("p (c b) -> p c b", c=C)
        q_clsT = area(C * IMAGES, 96).rearrange("p (c b) -> p c b", c=C)
        k_clsT = area(C * IMAGES, 96).rearrange("p (c b) -> p c b", c=C)
        z_cls_v = area(D, IMAGES)
        z_qT = [chunks(96) for _ in range(2)]
        z_kT = [chunks(96) for _ in range(2)]
        k_sum = area(C * 2, 96).rearrange("p (c s) -> p c s", c=C)
        free_w1 = W1[0:96, 0, E1:].rearrange("p e f -> p (e f)")
        kc = [free_w1[:, i * C * 2 * TOK:(i + 1) * C * 2 * TOK].rearrange("p (c s t) -> p c s t", c=C, s=2)
              for i in range(2)]
        z_kblk = [free_w1[:, i * 2 * C * 2 * TOK:(i + 1) * 2 * C * 2 * TOK]
                  .rearrange("p (c s a t) -> p c s a t", c=C, s=2, a=2) for i in range(1, 3)]
        q_cls6 = [area(C * 2 * HC, 96).rearrange("p (c s h) -> p c s h", c=C, s=2) for _ in range(2)]
        BLOCKS, BW = H // 2, 2 * HD + 2
        z_vblk = [area(2 * BLOCKS * BW).rearrange("p (s b w) -> p s b w", s=2, b=BLOCKS) for _ in range(3)]
        vb = [area(D) for _ in range(2)]
        w_s = [area(3 * 4 * TOK).rearrange("p (j g t) -> p j g t", j=3, g=4) for _ in range(2)]
        sq = area(3 * 4 * TOK).rearrange("p (j g t) -> p j g t", j=3, g=4)
        p_j = [area(6 * P).rearrange("p (g t) -> p g t", g=G) for _ in range(2)]
        p_c = [area(H) for _ in range(2)]
        pT = [area(6 * P).rearrange("p (b t) -> p b t", b=6) for _ in range(2)]
        s_max, s_sq = area(G), [area(G) for _ in range(2)]
        deviation = [area(G) for _ in range(2)]
        z_r = [area(G) for _ in range(2)]
        p_sum = area(G)
        z_rinv = area(H)
        z_own = [area(D) for _ in range(2)]
        z_o1 = area(D)
        z_o = [area(D) for _ in range(2)]
        z_oT = [chunks(97) for _ in range(2)]
        xs = [area(D) for _ in range(2)]
        x2n = [area(D) for _ in range(2)]
        x2g = area(D)
        z_x2T = [chunks(97) for _ in range(2)]
        z_stats, z_mv2 = area(6), [area(2) for _ in range(2)]
        z_eps2, z_rstd2 = area(1), [area(1) for _ in range(2)]
        sign, gamma_abs = area(1), area(1)
        z_half, z_var_scaled = area(G), area(G)
        cls_scores = area(IMAGES * H, TOK)
        pT_cls = pT[0].rearrange("p b t -> p (b t)")[:, 0:G * PAIRS]
        cls_mine = pT[1].rearrange("p b t -> p (b t)")[0:96, 0:2 * C * PAIRS * HC]\
            .rearrange("p (s t h) -> p s t h", s=2, h=HC)
        o_cls = area(C * IMAGES, 96).rearrange("p (c b) -> p c b", c=C)
        V_ALL = W2[:, E1:].rearrange("p e k d -> p (e k d)")[:, 0:PAIRS * D].rearrange("p (t d) -> p t d", t=PAIRS)

        (z_var, z_rstd, z_src, z_xT_done, z_xT_ready, z_v_done, z_k_done, z_q_done, z_v_taken, z_q_taken, z_k_taken,
         z_centred, z_masked, z_qcls_ready, z_vrep_done, z_vblk_ready, z_vb_ready, z_s_done, z_sq_ready,
         z_w_ready, z_squares, z_deviation, z_r_ready, z_zs_ready, z_ex_ready, z_pT_done, z_pT_ready_a, z_pT_ready_v,
         z_own_ready, z_pv_done, z_o_ready, z_oT_done, z_oT_ready, z_op_done, z_var2, z_rstd2_ready, z_x2n,
         z_x2_ready, z_x2T_done, z_x2T_ready) = sems(
            "z_", "var rstd src xT_done xT_ready v_done k_done q_done v_taken q_taken k_taken centred masked qcls_ready vrep_done "
                  "vblk_ready vb_ready s_done sq_ready w_ready squares deviation r_ready zs_ready ex_ready pT_done pT_ready_a "
                  "pT_ready_v own_ready pv_done o_ready oT_done oT_ready op_done var2 rstd2 x2n "
                  "x2_ready x2T_done x2T_ready")
        z_cls_scores, z_cls_p = sems("z_", "cls_scores cls_p")
        ORDER_Z = [("norm", 1), ("norm2", 6), ("stats", 0), ("square", 3), ("exp", 4), ("scored", 3), ("qkv", 2),
                   ("oT", 5), ("centre", 2), ("pT", 4), ("own", 4), ("root", 3), ("xT", 1), ("mask", 2), ("vrep", 2),
                   ("x2T", 6), ("cls", 2), ("pv", 4), ("logits", 6), ("oproj", 5), ("scale", 3), ("scores", 2)]
        NZ = {s: TILES for s, _ in ORDER_Z}
        ALL = TILES

        def before_z(other, stage, u):
            return PAIRS if u == ALL else issued_before(ORDER_Z, NZ, other, stage, u) - 1

        def rows_of(m):
            return IMAGES if m == ALL else P

        def tile_z(m):
            return CLS if m == ALL else m - 1

        def z_tensor(pe):
            def to_features(u):
                pe.wait_ge(z_src, u + 1)
                wait(pe, z_xT_ready, u)
                wait(pe, z_v_taken, issued_before(ORDER_Z, NZ, "qkv", "xT", u))
                wait(pe, z_oT_ready, before_z("oT", "xT", u))
                wait(pe, z_x2T_ready, before_z("x2T", "xT", u))
                for c in range(C):
                    mm = pe.transpose(PS[0:96, 0, c * P:(c + 1) * P], X1[:, tile_of(u), 96 * c:96 * c + 96], ident)
                mm.then_inc(z_xT_done, 1)

            def qkv(u):
                pe.wait_ge(z_xT_ready, u + 1)
                x, n = (z_clsT, IMAGES) if u == 0 else (z_xT[u % 2], P)
                wait(pe, z_q_taken, u)
                wait(pe, z_k_taken, u)
                wait(pe, z_vb_ready, before_z("vrep", "qkv", u))

                def features(a, done):
                    for oc in range(C):
                        for c in range(C):
                            at = a * D + 96 * oc
                            mm = pe.matmul(PS[0:96, 1, (a * C + oc) * P:(a * C + oc) * P + n],
                                           w_small_at("qkv2", c, at, at + 96), x[0:KC[c], c],
                                           start=c == 0, stop=c == C - 1)
                    mm.then_inc(done, 1)

                features(1, z_k_done)
                wait(pe, z_oT_ready, before_z("oT", "qkv", u))
                wait(pe, z_x2T_ready, before_z("x2T", "qkv", u))
                wait(pe, z_v_taken, u)
                for c in range(C):
                    mm = pe.matmul(PS[0:n, 0, C * P:C * P + D], x[0:KC[c], c], w_small_at("qkv2", c, 2 * D, 3 * D),
                                   start=c == 0, stop=c == C - 1)
                mm.then_inc(z_v_done, 1)
                pe.wait_ge(z_k_taken, u + 1)
                features(0, z_q_done)

            def replicate(u):
                pe.wait_ge(z_v_taken, u + 1)
                wait(pe, z_vblk_ready, u - 1)
                wait(pe, z_pT_ready_v, before_z("pT", "vrep", u))
                wait(pe, z_var2, before_z("oproj", "vrep", u))
                wait(pe, z_vb_ready, u - 1)
                pe.wait_ge(z_k_taken, u + 1)
                pe.wait_ge(z_q_taken, u + 1)
                tw = K("twice").rearrange("p (s m) -> p s m", s=2)
                for s in range(2):
                    pe.matmul(PS[:, 2, s * D:(s + 1) * D], tw[:, s], V_ALL[:, u - 1], start=True, stop=True)
                    b = 2 * (u - 1) + s
                    mm = pe.matmul(PS[S * s:S * s + S, 1, 0:D],
                                   ident[0:IMAGES, b:b + 1].broadcast_to([IMAGES, S]), z_cls_v, start=True, stop=True)
                mm.then_inc(z_vrep_done, 1)

            def scores(u):
                i = u % 2
                pe.wait_ge(z_q_taken, u + 1)
                pe.wait_ge(z_masked, u)
                wait(pe, z_w_ready, u - 1)
                wait(pe, z_sq_ready, u - 1)
                for c in range(C):
                    for s in range(2):
                        for j in range(3):
                            r = slice(32 * j, 32 * j + 32)
                            mm = pe.matmul(PS[S * s:S * s + S, 4 + j, c * 2 * TOK:(c + 1) * 2 * TOK],
                                      z_qT[i][r, c, S * s:S * s + S],
                                      z_kblk[i][r, c, s].rearrange("p a t -> p (a t)"), start=True, stop=True)
                mm.then_inc(z_s_done, 1)

            def class_scores(u):
                i = u % 2
                pe.wait_ge(z_q_taken, 1)
                pe.wait_ge(z_centred, u)
                pe.wait_ge(z_qcls_ready, u)
                wait(pe, lg_taken, TILES + before_z("logits", "cls", u))
                for s in range(2):
                    for c in range(C):
                        b = 2 * (u - 1) + s
                        mm = pe.matmul(PS[0:TOK, 3, b * H + c * HC:b * H + (c + 1) * HC], kc[i][:, c, s],
                                       q_cls6[i][:, c, s], start=True, stop=True)

            def p_t(u):
                pe.wait_ge(z_ex_ready, u)
                wait(pe, z_pT_ready_a, u - 1)
                wait(pe, z_o_ready, before_z("pv", "pT", u))
                wait(pe, z_pT_ready_v, u - 1)
                wait(pe, z_vblk_ready, before_z("vrep", "pT", u))
                wait(pe, z_var2, before_z("oproj", "pT", u))
                for b in range(6):
                    bank, at = (7, b * P) if b < 4 else (2, (b - 4) * P)
                    mm = pe.transpose(PS[:, bank, at:at + P],
                                      p_j[u % 2].rearrange("p g t -> p (g t)")[:, b * P:(b + 1) * P], ident)
                mm.then_inc(z_pT_done, 1)

            def pv(u):
                pe.wait_ge(z_pT_ready_a, u)
                pe.wait_ge(z_pT_ready_v, u)
                pe.wait_ge(z_vblk_ready, u)
                wait(pe, z_o_ready, u - 1)
                for s in range(2):
                    for j in range(3):
                        for c in range(C):
                            b = 3 * c + j
                            mm = pe.matmul(PS[S * s:S * s + S, 7, b * BW:(b + 1) * BW],
                                           pT[u % 2][:, 2 * j + c, S * s:S * s + S], z_vblk[u % 3][:, s, b],
                                           start=True, stop=True)
                mm.then_inc(z_pv_done, 1)

            def transposed(m, src, done):
                n = rows_of(m)
                for c in range(C):
                    mm = pe.transpose(PS[0:96, 0, c * P:c * P + n], src[0:n, 96 * c:96 * c + 96], ident[0:n, 0:n])
                mm.then_inc(done, 1)

            def out_t(m):
                pe.wait_ge(z_o_ready, m)
                wait(pe, z_oT_ready, m - 1)
                wait(pe, z_xT_ready, before_z("xT", "oT", m) + 1)
                wait(pe, z_v_taken, before_z("qkv", "oT", m) + 1)
                wait(pe, z_x2T_ready, before_z("x2T", "oT", m))
                transposed(m, z_o[m % 2], z_oT_done)

            def out_projection(m):
                pe.wait_ge(z_oT_ready, m)
                wait(pe, z_var2, m - 1)
                wait(pe, z_vblk_ready, before_z("vrep", "oproj", m))
                wait(pe, z_pT_ready_v, before_z("pT", "oproj", m))
                n = rows_of(m)
                for c in range(C):
                    mm = pe.matmul(PS[0:n, 2, 0:D], z_oT[m % 2][0:KC[c], c, 0:n],
                                   w_small_at("out2", c, 0, D), start=c == 0, stop=c == C - 1)
                mm.then_inc(z_op_done, 1)

            def x2_t(m):
                pe.wait_ge(z_x2_ready, m)
                wait(pe, z_x2T_ready, m - 1)
                wait(pe, z_xT_ready, before_z("xT", "x2T", m) + 1)
                wait(pe, z_v_taken, before_z("qkv", "x2T", m) + 1)
                wait(pe, z_oT_ready, ALL if m == ALL else before_z("oT", "x2T", m))
                transposed(m, X1[:, tile_z(m)], z_x2T_done)

            def logits(m):
                n = rows_of(m)
                pe.wait_ge(z_x2T_ready, m)
                wait(pe, lg_taken, TILES + m - 1)
                for c in range(C):
                    mm = pe.matmul(PS[0:n, 3, IMAGES * H:IMAGES * H + E1], z_x2T[m % 2][0:KC[c], c, 0:n],
                                   w_small_at("gate2", c, 0, E1), start=c == 0, stop=c == C - 1)
                mm.then_inc(lg_done, 1)

            pe.wait_ge(set_up, 4)
            pe.wait_ge(h_quant, TILES)
            step = {"xT": to_features, "qkv": qkv, "vrep": replicate, "cls": class_scores, "scores": scores, "pT": p_t, "pv": pv,
                    "oT": out_t, "oproj": out_projection, "x2T": x2_t, "logits": logits}
            for stage, u in bodies(ORDER_Z, NZ):
                if stage in step and (u > 0 or stage in ("xT", "qkv")):
                    step[stage](u)
            pe.wait_ge(z_cls_scores, 1)
            pe.wait_ge(z_w_ready, PAIRS)
            pe.wait_ge(z_sq_ready, PAIRS)
            for h in range(H):
                c, j, a = h // HC, h % HC // 2, h % 2
                mm = pe.transpose(PS[0:IMAGES, 4 + j, (2 * c + a) * TOK:(2 * c + a + 1) * TOK],
                                  cls_scores[:, h:IMAGES * H:H], ident[0:TOK, 0:TOK])
            mm.then_inc(z_s_done, 1)
            pe.wait_ge(z_cls_p, 1)
            pe.wait_ge(z_o_ready, PAIRS)
            for g in range(G):
                for s in range(2):
                    mm = pe.matmul(PS[S * s:S * s + S, 7, g * PAIRS:(g + 1) * PAIRS], p_j[ALL % 2][0:IMAGES, g],
                                   ident[0:IMAGES, s:IMAGES:2], start=True, stop=True)
            mm.then_inc(z_pT_done, 1)
            pe.wait_ge(z_pT_ready_a, ALL)
            pe.wait_ge(z_w_ready, ALL)
            pe.wait_ge(z_sq_ready, ALL)
            pcT = pT_cls.rearrange("p (j c a t) -> p c j a t", j=3, c=C, a=2)
            for t in range(PAIRS):
                for c in range(C):
                    for s in range(2):
                        mm = pe.matmul(PS[0:96, 4 + s, (c * PAIRS + t) * HC:(c * PAIRS + t + 1) * HC],
                                       V_ALL[S * s:S * s + S, t, 96 * c:96 * c + 96],
                                       pcT[S * s:S * s + S, c, :, :, t], start=True, stop=True)
            mm.then_inc(z_pv_done, 1)
            out_t(ALL)
            out_projection(ALL)
            x2_t(ALL)
            logits(ALL)

        def z_scalar(act):
            def copy(out_ap, in_ap):
                return act.activation(out_ap, in_ap, ACT.Copy)

            def square(m):
                n = rows_of(m)
                act.wait_ge(z_s_done, m)
                wait(act, z_w_ready, m - 1)
                act.activation(sq[0:n].rearrange("p j g t -> p j (g t)"), PS[0:n, 4:7, 0:4 * TOK], ACT.Square)\
                    .then_inc(z_sq_ready, 1)

            def exponent(m):
                n, i = rows_of(m), m % 2
                act.wait_ge(z_zs_ready, m)
                if m != ALL:
                    wait(act, z_pT_done, m - 2)
                    wait(act, z_own_ready, m - 2)
                    wait(act, z_o_ready, m - 2)
                else:
                    act.wait_ge(z_pT_done, PAIRS)
                    act.wait_ge(z_own_ready, PAIRS)
                    act.wait_ge(z_o_ready, PAIRS)
                w = w_s[i][0:n]
                act.activation(p_j[i][0:n].rearrange("p (j g) t -> p j g t", j=3), w[:, :, :, 0:S], ACT.Exp)
                act.activation(p_c[i][0:n].rearrange("p (c j a) -> p j c a", c=C, a=2),
                               w[:, :, :, S].rearrange("p j (c a) -> p j c a", c=C), ACT.Exp).then_inc(z_ex_ready, 1)

            def o_t(m):
                act.wait_ge(z_oT_done, m)
                wait(act, z_op_done, m - 2)
                copy(z_oT[m % 2][0:96], PS[0:96, 0, 0:C * P].rearrange("p (c t) -> p c t", c=C)).then_inc(z_oT_ready, 1)

            def x2_t(m):
                n = rows_of(m)
                act.wait_ge(z_x2T_done, m)
                wait(act, lg_done, TILES + m - 2)
                copy(z_x2T[m % 2][0:96, :, 0:n], PS[0:96, 0, 0:C * P].rearrange("p (c t) -> p c t", c=C)[:, :, 0:n])\
                    .then_inc(z_x2T_ready, 1)

            act.wait_ge(set_up, 4)
            for stage, u in bodies(ORDER_Z, NZ):
                i = u % 2
                if stage == "xT":
                    act.wait_ge(z_xT_done, u + 1)
                    ps = PS[0:96, 0, 0:C * P].rearrange("p (c t) -> p c t", c=C)
                    if u == 0:
                        copy(z_clsT[0:96], ps[:, :, 0:IMAGES]).then_inc(z_xT_ready, 1)
                    else:
                        wait(act, z_q_done, u - 1)
                        copy(z_xT[i][0:96], ps).then_inc(z_xT_ready, 1)
                elif stage == "qkv":
                    n = IMAGES if u == 0 else P
                    ps = PS[0:96, 1].rearrange("p (a c t) -> p a c t", a=2, c=C)
                    act.wait_ge(z_k_done, u + 1)
                    wait(act, z_centred, u - 2)
                    copy(k_clsT if u == 0 else z_kT[i], ps[:, 1, :, 0:n]).then_inc(z_k_taken, 1)
                    act.wait_ge(z_v_done, u + 1)
                    copy(z_cls_v if u == 0 else V_ALL[:, u - 1], PS[0:n, 0, C * P:C * P + D]).then_inc(z_v_taken, 1)
                    act.wait_ge(z_q_done, u + 1)
                    wait(act, z_s_done, u - 2)
                    act.activation(q_clsT if u == 0 else z_qT[i], ps[:, 0, :, 0:n], ACT.Copy, scale=sign[0:96])\
                        .then_inc(z_q_taken, 1)
                elif stage == "vrep" and u > 0:
                    act.wait_ge(z_vrep_done, u)
                    wait(act, z_own_ready, u - 2)
                    copy(vb[i], PS[:, 1, 0:D]).then_inc(z_vb_ready, 1)
                elif stage == "square" and u > 0:
                    square(u)
                elif stage == "mask" and u > 0:
                    act.wait_ge(z_centred, u)
                    wait(act, z_s_done, u - 2)
                    for a in range(2):
                        last = act.activation(z_kblk[i][:, :, :, a], kc[i], ACT.Copy, scale=K("half")[0:96, a:a + 1])
                    last.then_inc(z_masked, 1)
                elif stage == "exp" and u > 0:
                    exponent(u)
                elif stage == "pT" and u > 0:
                    act.wait_ge(z_pT_done, u)
                    wait(act, z_pv_done, u - 2)
                    copy(pT[i][:, 0:4], PS[:, 7].rearrange("p (b t) -> p b t", b=4)).then_inc(z_pT_ready_a, 1)
                elif stage == "oT" and u > 0:
                    o_t(u)
                elif stage == "x2T" and u > 0:
                    x2_t(u)
            act.wait_ge(z_s_done, PAIRS)
            act.wait_ge(lg_taken, TILES + PAIRS)
            copy(cls_scores, PS[0:TOK, 3, 0:IMAGES * H]).then_inc(z_cls_scores, 1)
            square(ALL)
            exponent(ALL)
            act.wait_ge(z_pT_done, ALL)
            copy(pT_cls, PS[:, 7, 0:G * PAIRS]).then_inc(z_pT_ready_a, 1)
            x2_t(ALL)

        def z_vector(v, chain):
            def scored(m):
                n, i = rows_of(m), m % 2
                v.wait_ge(z_sq_ready, m)
                ps = PS[0:n, 4:7, 0:4 * TOK].rearrange("p j (g t) -> p j g t", g=4)
                mx = s_max[0:n].rearrange("p (j g) -> p j g", j=3)
                chain.link(v.tensor_reduce(mx, ps, AX.X, ALU.max))
                wait(v, z_ex_ready, m - 2)
                last = [v.tensor_tensor(w_s[i][0:n, j], ps[:, j], mx[:, j].unsqueeze(2).broadcast_to([n, 4, TOK]),
                                        ALU.subtract) for j in range(3)][-1]
                last.then_inc(z_w_ready, 1)
                wait(v, z_deviation, m - 2)
                v.tensor_reduce(s_sq[i][0:n].rearrange("p (j g) -> p j g", j=3), sq[0:n], AX.X, ALU.add)\
                    .then_inc(z_squares, 1)

            def scale(m):
                n, i = rows_of(m), m % 2
                v.wait_ge(z_deviation, m)
                wait(v, z_zs_ready, m - 2)
                chain.link(v.tensor_scalar(z_r[i][0:n], deviation[i][0:n], EPS_Z, None, ALU.add))
                chain.link(v.reciprocal(z_r[i][0:n], z_r[i][0:n]))
                v.tensor_scalar(z_r[i][0:n], z_r[i][0:n], gamma_abs[0:n], None, ALU.mult).then_inc(z_r_ready, 1)

            def attended(m):
                n, i, t = rows_of(m), m % 2, tile_z(m)
                v.wait_ge(z_op_done, m)
                chain.link(v.tensor_tensor(xs[i][0:n], PS[0:n, 2, 0:D], X1[0:n, t], ALU.add))
                chain.link(v.bn_stats(z_stats[0:n], xs[i][0:n]))
                v.bn_aggr(z_mv2[i][0:n], z_stats[0:n]).then_inc(z_var2, 1)

            def normed(m):
                n, i = rows_of(m), m % 2
                v.wait_ge(z_rstd2_ready, m)
                wait(v, z_x2_ready, m - 2)
                v.tensor_scalar(x2n[i][0:n], xs[i][0:n], z_mv2[i][0:n, 0:1], z_rstd2[i][0:n], ALU.subtract, ALU.mult)\
                    .then_inc(z_x2n, 1)

            def logits(m):
                n = rows_of(m)
                v.wait_ge(lg_done, TILES + m)
                v.tensor_copy(LG[0:n, tile_z(m), 0:E1], PS[0:n, 3, IMAGES * H:IMAGES * H + E1]).then_inc(lg_taken, 1)

            v.wait_ge(q_oproj_done, TILES)
            v.wait_ge(h_quant, TILES)
            for i in range(2):
                v.memset(z_xT[i][96:97], 1.0)
                v.memset(z_oT[i][96:97], 1.0)
                v.memset(z_x2T[i][96:97], 1.0)
            v.memset(z_clsT[96:97], 1.0)
            v.memset(z_half, 0.5)
            for i in range(3):
                for a in range(2):
                    v.memset(z_vblk[i][S * a:S * a + S, :, :, 2 * HD + 1 - a], 0.0)
                    v.memset(z_vblk[i][S * a:S * a + S, :, :, 2 * HD + a], 1.0)
            gamma = ROW("gamma", 1)
            v.tensor_scalar(gamma_abs, gamma, 0.0, None, ALU.is_lt)
            chain.link(v.tensor_scalar(sign, gamma, 0.0, None, ALU.is_gt))
            chain.link(v.tensor_tensor(sign, sign, gamma_abs, ALU.subtract))
            v.tensor_scalar(gamma_abs, gamma, sign, HEAD_SCALE, ALU.mult, ALU.mult).then_inc(set_up, 1)
            v.wait_ge(set_up, 4)
            for stage, u in bodies(ORDER_Z, NZ):
                i, t = u % 2, tile_of(u)
                if stage == "stats":
                    wait(v, z_var, u)
                    layer_norm_stats(v, chain, HT[:, t], c_stats, c_mv[i], z_var)
                elif stage == "norm":
                    v.wait_ge(z_rstd, u + 1)
                    v.tensor_scalar(X1[:, t], HT[:, t], c_mv[i][:, 0:1], c_rstd[i], ALU.subtract, ALU.mult)\
                        .then_inc(z_src, 1)
                if u == 0:
                    continue
                if stage == "centre":
                    v.wait_ge(z_k_taken, u + 1)
                    kT = z_kT[i].rearrange("p c (s t) -> p c s t", s=2)
                    k_cls = k_clsT[:, :, 2 * (u - 1):2 * u]
                    chain.link(v.tensor_reduce(k_sum, kT, AX.X, ALU.add))
                    chain.link(v.tensor_tensor(k_sum, k_sum, k_cls, ALU.add))
                    chain.link(v.tensor_scalar(k_sum, k_sum, 1.0 / TOK, None, ALU.mult))
                    wait(v, z_s_done, u - 2)
                    wait(v, z_masked, u - 2)
                    v.tensor_tensor(kc[i][:, :, :, 0:S], kT, k_sum.unsqueeze(3).broadcast_to([96, C, 2, S]), ALU.subtract)
                    v.tensor_tensor(kc[i][:, :, :, S], k_cls, k_sum, ALU.subtract).then_inc(z_centred, 1)
                elif stage == "vrep":
                    v.wait_ge(z_vrep_done, u)
                    wait(v, z_pv_done, u - 3)
                    v.tensor_tensor(z_vblk[u % 3][:, :, :, 0:2 * HD],
                                    PS[:, 2, 0:2 * D].rearrange("p (s b e) -> p s b e", s=2, b=BLOCKS),
                                    K("half_cols").rearrange("p (b e) -> p b e", b=BLOCKS).unsqueeze(1)
                                    .broadcast_to([P, 2, BLOCKS, 2 * HD]), ALU.mult)\
                        .then_inc(z_vblk_ready, 1)
                elif stage == "scored":
                    scored(u)
                elif stage == "scale":
                    scale(u)
                elif stage == "pT":
                    v.wait_ge(z_pT_done, u)
                    wait(v, z_pv_done, u - 2)
                    v.tensor_copy(pT[i][:, 4:6], PS[:, 2, 0:2 * P].rearrange("p (b t) -> p b t", b=2))\
                        .then_inc(z_pT_ready_v, 1)
                elif stage == "pv":
                    v.wait_ge(z_pv_done, u)
                    v.wait_ge(z_own_ready, u)
                    ps = PS[:, 7, 0:BLOCKS * BW].rearrange("p (b w) -> p b w", b=BLOCKS)
                    chain.link(v.tensor_tensor(z_rinv.rearrange("p (b a) -> p b a", a=2), ps[:, :, 2 * HD:],
                                               p_c[i].rearrange("p (b a) -> p b a", a=2), ALU.add))
                    v.tensor_tensor(z_o1.rearrange("p (b e) -> p b e", b=BLOCKS), ps[:, :, 0:2 * HD],
                                    z_own[i].rearrange("p (b e) -> p b e", b=BLOCKS), ALU.add)
                    chain.link(v.reciprocal(z_rinv, z_rinv))
                    wait(v, z_oT_done, u - 2)
                    v.tensor_tensor(z_o[i].rearrange("p (h d) -> p h d", h=H), z_o1.rearrange("p (h d) -> p h d", h=H),
                                    z_rinv.unsqueeze(2).broadcast_to([P, H, HD]), ALU.mult).then_inc(z_o_ready, 1)
                elif stage == "oproj":
                    attended(u)
                elif stage == "norm2":
                    normed(u)
                elif stage == "logits":
                    logits(u)
            i, n = ALL % 2, IMAGES
            scored(ALL)
            scale(ALL)
            v.wait_ge(z_ex_ready, ALL)
            by_groups = "p (c j a) -> p j c a"
            sums = p_sum[0:n].rearrange("p (j c a) -> p j c a", j=3, c=C)
            chain.link(v.tensor_reduce(p_sum[0:n], p_j[i][0:n], AX.X, ALU.add))
            chain.link(v.tensor_tensor(sums, sums, p_c[i][0:n].rearrange(by_groups, c=C, a=2), ALU.add))
            chain.link(v.reciprocal(p_sum[0:n], p_sum[0:n]))
            chain.link(v.tensor_copy(z_rinv[0:n].rearrange(by_groups, c=C, a=2), sums))
            v.tensor_tensor(p_j[i][0:n], p_j[i][0:n], p_sum[0:n].unsqueeze(2).broadcast_to([n, G, S]), ALU.mult)\
                .then_inc(z_cls_p, 1)
            chain.link(v.tensor_tensor(p_c[i][0:n], p_c[i][0:n], z_rinv[0:n], ALU.mult))
            v.wait_ge(z_oT_done, PAIRS - 1)
            v.tensor_tensor(z_o[i][0:n].rearrange("p (h d) -> p h d", h=H), z_cls_v.rearrange("p (h d) -> p h d", h=H),
                            p_c[i][0:n].unsqueeze(2).broadcast_to([n, H, HD]), ALU.mult).then_inc(z_o_ready, 1)
            v.wait_ge(z_pv_done, ALL)
            chain.link(v.tensor_tensor(cls_mine, PS[0:96, 4:6, 0:C * PAIRS * HC].rearrange("p s (t h) -> p s t h", h=HC),
                                       head6.unsqueeze(1).unsqueeze(1).broadcast_to([96, 2, C * PAIRS, HC]), ALU.mult))
            chain.link(v.tensor_reduce(o_cls.rearrange("p c (t s) -> p s (c t)", s=2), cls_mine, AX.X, ALU.add))
            v.wait_ge(z_oT_done, ALL)
            v.tensor_tensor(z_oT[i][0:96, :, 0:n], PS[0:96, 0, 0:C * P].rearrange("p (c t) -> p c t", c=C)[:, :, 0:n],
                            o_cls, ALU.add).then_inc(z_oT_ready, 1)
            attended(ALL)
            normed(ALL)
            logits(ALL)

        def z_gpsimd(g, chain):
            def root(m):
                n, i = rows_of(m), m % 2
                g.wait_ge(z_squares, m)
                wait(g, z_deviation, m - 1)
                chain.link(g.tensor_scalar(z_var_scaled[0:n], s_sq[i][0:n], HEAD_SCALE * HEAD_SCALE / (TOK - 1), None,
                                           ALU.mult))
                wait(g, z_r_ready, m - 2)
                g.tensor_tensor(deviation[i][0:n], z_var_scaled[0:n], z_half[0:n], ALU.pow).then_inc(z_deviation, 1)

            def z_scores(m):
                n, i = rows_of(m), m % 2
                g.wait_ge(z_w_ready, m)
                g.wait_ge(z_r_ready, m)
                w = w_s[i][0:n].rearrange("p j g t -> p (j g) t")
                g.tensor_tensor(w, w, z_r[i][0:n].unsqueeze(2).broadcast_to([n, G, TOK]), ALU.mult).then_inc(z_zs_ready, 1)

            def root2(m):
                n, i = rows_of(m), m % 2
                g.wait_ge(z_var2, m)
                wait(g, z_rstd2_ready, m - 1)
                chain.link(g.tensor_scalar(z_eps2[0:n], z_mv2[i][0:n, 1:2], EPS_LN, None, ALU.add))
                g.tensor_tensor(z_rstd2[i][0:n], z_eps2[0:n], c_minus_half[0:n], ALU.pow).then_inc(z_rstd2_ready, 1)

            def scaled(m):
                n, i = rows_of(m), m % 2
                g.wait_ge(z_x2n, m)
                wait(g, z_x2_ready, m - 1)
                chain.link(g.tensor_tensor(x2g[0:n], x2n[i][0:n], ROW("ln1_g")[0:n], ALU.mult))
                g.tensor_tensor(X1[0:n, tile_z(m)], x2g[0:n], ROW("ln1_b")[0:n], ALU.add).then_inc(z_x2_ready, 1)

            g.wait_ge(set_up, 4)
            g.wait_ge(loaded["later"], 16 * 2)
            for stage, u in bodies(ORDER_Z, NZ):
                i, t = u % 2, tile_of(u)
                if stage == "stats":
                    g.wait_ge(z_var, u + 1)
                    wait(g, z_rstd, u)
                    chain.link(g.tensor_scalar(c_eps, c_mv[i][:, 1:2], EPS_LN, None, ALU.add))
                    g.tensor_tensor(c_rstd[i], c_eps, c_minus_half, ALU.pow).then_inc(z_rstd, 1)
                if u == 0:
                    continue
                if stage == "qkv":
                    b = 2 * (u - 1)
                    wait(g, z_s_done, u - 2)
                    g.wait_ge(z_q_taken, 1)
                    g.tensor_tensor(q_cls6[i], q_clsT[:, :, b:b + 2].unsqueeze(3).broadcast_to([96, C, 2, HC]),
                                    head6.unsqueeze(1).unsqueeze(1).broadcast_to([96, C, 2, HC]), ALU.mult)\
                        .then_inc(z_qcls_ready, 1)
                elif stage == "root":
                    root(u)
                elif stage == "scale":
                    z_scores(u)
                elif stage == "own":
                    g.wait_ge(z_ex_ready, u)
                    g.wait_ge(z_vb_ready, u)
                    wait(g, z_o_ready, u - 2)
                    g.tensor_tensor(z_own[i].rearrange("p (h d) -> p h d", h=H), vb[i].rearrange("p (h d) -> p h d", h=H),
                                    p_c[i].unsqueeze(2).broadcast_to([P, H, HD]), ALU.mult).then_inc(z_own_ready, 1)
                elif stage == "oproj":
                    root2(u)
                elif stage == "norm2":
                    scaled(u)
            root(ALL)
            z_scores(ALL)
            root2(ALL)
            scaled(ALL)

        taken[0] = between_start
        F_Y = [[area(D) for _ in range(TOP1)] for _ in range(3)]
        f_one, f_two = area(D), [area(D) for _ in range(2)]
        f_stats, f_mv = area(6), [area(2) for _ in range(2)]
        f_eps, f_rs, f_half = area(1), [area(1) for _ in range(2)], area(1)
        f_n, f_g, f_b = [area(D) for _ in range(2)], [area(D) for _ in range(2)], area(D)
        f_out = [area(D) for _ in range(3)]
        f_var, f_rstd, f_normed, f_scaled, f_ready = sems("f_", "var rstd normed scaled ready")
        ORDER_F = [("gather", 0), ("sum", 2), ("norm", 3), ("out", 4)]
        NF = {s: TILES for s, _ in ORDER_F}

        def rows_u(u):
            return IMAGES if u == 0 else P

        def f_gpsimd(g, chain):
            experts_done(g, 1)
            for stage, u in bodies(ORDER_F, NF):
                i, n, t = u % 2, rows_u(u), tile_of(u)
                if stage == "gather":
                    wait(g, f_var, u - 2)
                    for k in range(TOP1):
                        g.indirect_dma_start(out=F_Y[u % 3][k][0:n], out_offset=None, in_=yg_dram,
                                             in_offset=bass.IndirectOffsetOnAxis(ap=SLOT[0:n, k, t:t + 1], axis=0))\
                            .then_inc(c_gathered[u % 3], 16)
                elif stage == "sum":
                    g.wait_ge(f_var, u + 1)
                    wait(g, f_rstd, u)
                    chain.link(g.tensor_scalar(f_eps[0:n], f_mv[i][0:n, 1:2], EPS_LN, None, ALU.add))
                    g.tensor_tensor(f_rs[i][0:n], f_eps[0:n], f_half[0:n], ALU.pow).then_inc(f_rstd, 1)
                elif stage == "norm":
                    g.wait_ge(f_normed, u + 1)
                    wait(g, f_ready, u - 1)
                    g.tensor_tensor(f_g[i][0:n], f_n[i][0:n], ROW("ln2_g")[0:n], ALU.mult).then_inc(f_scaled, 1)

        def f_vector(v, chain):
            experts_done(v, 1)
            chain.link(v.memset(f_half, -0.5))
            for stage, u in bodies(ORDER_F, NF):
                i, n, t = u % 2, rows_u(u), tile_of(u)
                if stage == "sum":
                    first_layer = (TILES + 2 - u % 3) // 3
                    v.wait_ge(c_gathered[u % 3], 16 * (first_layer + TOP1 * (u // 3 + 1)))
                    wait(v, f_var, u)
                    chain.link(v.scalar_tensor_tensor(f_one[0:n], F_Y[u % 3][0][0:n], PROB[0:n, 0, t:t + 1], X1[0:n, t],
                                                      ALU.mult, ALU.add))
                    chain.link(v.scalar_tensor_tensor(f_two[i][0:n], F_Y[u % 3][1][0:n], PROB[0:n, 1, t:t + 1],
                                                      f_one[0:n], ALU.mult, ALU.add))
                    layer_norm_stats(v, chain, f_two[i][0:n], f_stats[0:n], f_mv[i][0:n], f_var)
                elif stage == "norm":
                    v.wait_ge(f_rstd, u + 1)
                    wait(v, f_scaled, u - 1)
                    v.tensor_scalar(f_n[i][0:n], f_two[i][0:n], f_mv[i][0:n, 0:1], f_rs[i][0:n], ALU.subtract, ALU.mult)\
                        .then_inc(f_normed, 1)
                elif stage == "out":
                    v.wait_ge(f_scaled, u + 1)
                    wait(v, f_ready, u)
                    chain.link(v.tensor_tensor(f_b[0:n], f_g[i][0:n], ROW("ln2_b")[0:n], ALU.add))
                    wait(v, out_stored[u % 3], 16 * (u // 3))
                    v.tensor_tensor(f_out[u % 3][0:n], f_b[0:n], HT[0:n, t], ALU.add).then_inc(f_ready, 1)

        def f_sync(sp):
            for u in range(TILES):
                sp.wait_ge(f_ready, u + 1)
                if u == 0:
                    sp.dma_start(out[:, 0], f_out[0][0:IMAGES]).then_inc(out_stored[u % 3], 16)
                else:
                    sp.dma_start(out[2 * (u - 1):2 * u, 1:TOK], f_out[u % 3]).then_inc(out_stored[u % 3], 16)
            for i in range(3):
                sp.wait_ge(out_stored[i], 16 * ((TILES + 2 - i) // 3))

        @block.sync
        def _(sp):
            a_sync(sp)
            sp.wait_ge(loaded["experts0"], 16 * 2 * E0)
            m_sync(sp, 0)
            q_sync(sp)
            sp.wait_ge(loaded_experts1, 16 * 2 * E1)
            m_sync(sp, 1)
            f_sync(sp)

        @block.tensor
        def _(pe):
            a_tensor(pe)
            r_tensor(pe, 0, lambda pe: pe.wait_ge(lg_taken, TILES))
            pe.wait_ge(loaded["experts0"], 16 * 2 * E0)
            m_tensor(pe, 0)
            q_tensor(pe)
            z_tensor(pe)
            r_tensor(pe, 1, lambda pe: pe.wait_ge(lg_taken, 2 * TILES))
            pe.wait_ge(loaded_experts1, 16 * 2 * E1)
            m_tensor(pe, 1)

        @block.scalar
        def _(act):
            a_scalar(act)
            r_scalar(act, 0)
            m_scalar(act, 0)
            q_scalar(act)
            z_scalar(act)
            r_scalar(act, 1)
            m_scalar(act, 1)

        @block.vector
        def _(v):
            chain = Chain(v, vec)
            a_vector(v, chain)
            r_vector(v, chain, 0)
            m_vector(v, 0)
            q_vector(v, chain)
            z_vector(v, chain)
            r_vector(v, chain, 1)
            m_vector(v, 1)
            f_vector(v, chain)

        @block.gpsimd
        def _(g):
            chain = Chain(g, pool)
            a_gpsimd(g, chain)
            r_gpsimd(g, 0)
            q_gpsimd(g, chain)
            z_gpsimd(g, chain)
            r_gpsimd(g, 1)
            f_gpsimd(g, chain)




def arrays_of(i):
    a = {k: np.asarray(v) for k, v in i.items()}
    f = np.float32
    x = a["x"].reshape(PAIRS, 2, CHANNELS, GRID, PATCH, GRID, PATCH)
    x = x.transpose(0, 4, 6, 2, 1, 3, 5).reshape(PAIRS, FK, P, P).transpose(0, 2, 1, 3)

    def small(w, b):
        o = np.zeros((97, C, w.shape[1]), f)
        o[0:96, 0], o[0:96, 1] = w[0:96], w[96:D]
        if b is not None:
            o[96, 1] = b
        return o

    qkv2 = np.concatenate([a["L1_ffn_Wq"].T, a["L1_ffn_Wk"].T, a["L1_ffn_Wv"].T], 1)
    qkv2_b = np.concatenate([a["L1_ffn_bq"], a["L1_ffn_bk"], a["L1_ffn_bv"]])
    w_small = np.concatenate([
        small(a["L0_attn_qkv_w"].T, a["L0_attn_qkv_b"]), small(a["L0_attn_out_w"].T, a["L0_attn_out_b"]),
        small(a["L0_ffn_Ws"], a["L0_ffn_bs"]), small(a["L1_attn_Wqkv"].T, None),
        small(a["L1_attn_Wproj"].T, a["L1_attn_bproj"]), small(qkv2, qkv2_b),
        small(a["L1_ffn_Wo"].T, a["L1_ffn_bo"]), small(a["L1_ffn_Wg"].T, a["L1_ffn_bg"])], 2)
    rows = np.concatenate([a[n].reshape(-1) for n in (
        "L0_tok_b", "cls_tok", "L1_ffn_ln1_g", "L1_ffn_ln1_b", "L1_ffn_ln2_g", "L1_ffn_ln2_b", "L1_attn_s_q",
        "L1_attn_s_k", "L1_attn_s_v", "L1_attn_s_attn", "L1_attn_s_after", "L1_ffn_gamma", "L0_ffn_b2",
        "L1_ffn_b2")])[None]

    def first(w, b):
        o = np.zeros((97, C, w.shape[0], FF), f)
        o[0:96] = w.reshape(-1, C, 96, FF).transpose(2, 1, 0, 3)
        o[96, 1] = b
        return o

    def second(w):
        return np.ascontiguousarray(w.reshape(-1, FFK, P, D).transpose(2, 0, 1, 3))

    return {
        "x_feat": np.ascontiguousarray(x),
        "w_tok": np.ascontiguousarray(a["L0_tok_W"].T.reshape(FK, P, D).transpose(1, 0, 2)),
        "w_small": w_small, "rows": rows, "consts": shape_constants(),
        "w1_0": first(a["L0_ffn_W1"], a["L0_ffn_b1"]), "w2_0": second(a["L0_ffn_W2"]),
        "w1_1": first(a["L1_ffn_W1"], a["L1_ffn_b1"]), "w2_1": second(a["L1_ffn_W2"]),
    }


def kernel(**inputs):
    import concourse.bacc as bacc
    from concourse.bass_utils import run_bass_kernel_spmd

    nc = bacc.Bacc("TRN2", target_bir_lowering=False, num_devices=1)
    arrays, args = {}, []
    for name, a in arrays_of(inputs).items():
        arrays["in_" + name] = a
        args.append(nc.dram_tensor("in_" + name, a.shape, mybir.dt.from_np(a.dtype), kind="ExternalInput").ap())
    args.append(nc.dram_tensor("out_0", (IMAGES, TOK, D), F32, kind="ExternalOutput").ap())
    build(nc, *args)
    return run_bass_kernel_spmd(nc, [arrays], core_ids=[0]).results[0]["out_0"]
```

```python
from contextlib import ExitStack

import numpy as np

import concourse.bass as bass
from concourse import mybir

ALU = mybir.AluOpType
ACT = mybir.ActivationFunctionType
AX = mybir.AxisListType
F32 = mybir.dt.float32
BF16 = mybir.dt.bfloat16
I32 = mybir.dt.int32

P = 128
IMAGES, CHANNELS, SIDE, PATCH = 32, 3, 128, 16
GRID = SIDE // PATCH
S = GRID * GRID
TOK = S + 1
D, H, HD = 192, 12, 16
PAIRS = IMAGES // 2
CLS = PAIRS
TILES = PAIRS + 1
FEAT = CHANNELS * PATCH * PATCH
FK = FEAT // P
C = D // 96
HC = H // C
STRIDE = 8
MS = S // STRIDE
KEYS0 = MS + 3
FF = 768
FFK = FF // P
HALF = FF // 2
E0, TOP0 = 8, 1
E1, TOP1 = 4, 2
NT0 = (IMAGES * TOK * TOP0 + E0 * (P - 1)) // P
NT1 = (IMAGES * TOK * TOP1 + E1 * (P - 1)) // P
UNROLL = 6
ZERO_PARTS = 4
EPS_LN = 1e-5
EPS_Z = 1e-5
MAGIC = 12582912.0
NEG = -1e30
HEAD_SCALE = HD ** -0.5
LEVEL_LO, LEVEL_HI, LEVEL_ATTN = -4.0, 3.0, 7.0

W_AT = {}
WCOLS = 0
for _n, _w in (("qkv0", 3 * D), ("out0", D), ("gate0", E0), ("qkv1", 3 * D), ("out1", D),
               ("qkv2", 3 * D), ("out2", D), ("gate2", E1)):
    W_AT[_n] = WCOLS
    WCOLS += _w

R_AT = {}
RCOLS = 0
for _n, _w in (("b_tok", D), ("cls", D), ("ln1_g", D), ("ln1_b", D), ("ln2_g", D), ("ln2_b", D),
               ("s_q", 1), ("s_k", 1), ("s_v", 1), ("s_attn", 1), ("s_after", 1), ("gamma", 1),
               ("b2_0", E0 * D), ("b2_1", E1 * D)):
    R_AT[_n] = RCOLS
    RCOLS += _w

K_AT, K_W = {}, {}
KCOLS = 0
for _n, _w in (("ident", P), ("before", P), ("ones", P), ("mask0", KEYS0 * H), ("pick_v", 2 * MS * H),
               ("head_rows", D), ("head6", HC), ("half", 2), ("half_cols", D), ("head12", C * H),
               ("twice", 2 * P), ("prio", 8), ("valid", TILES), ("tile_no", max(NT0, NT1)), ("first", H)):
    K_AT[_n], K_W[_n] = KCOLS, _w
    KCOLS += _w


def shape_constants():
    k = np.zeros((P, KCOLS), np.float32)

    def put(name, a):
        k[:a.shape[0], K_AT[name]:K_AT[name] + a.shape[1]] = a

    r = np.arange(P)
    put("ident", np.eye(P))
    put("before", (r[:, None] < r[None, :]) * 1.0)
    put("ones", np.ones((P, P)))
    patch = r % S
    mask = np.zeros((P, KEYS0, H))
    for m in range(MS):
        mask[STRIDE * (m + 1) > patch + 1, m] = NEG
    mask[(patch + 1) % STRIDE == 0, MS + 1] = NEG
    mask[patch % STRIDE == 0, MS + 2] = NEG
    put("mask0", mask.reshape(P, -1))
    pick = np.zeros((P, 2, MS, H))
    for s in range(2):
        for m in range(MS):
            pick[S * s + STRIDE * m + STRIDE - 1, s, m] = 1
    put("pick_v", pick.reshape(P, -1))
    put("head_rows", (r[:(MS + 1) * H, None] % H == np.arange(D)[None, :] // HD) * 1.0)
    put("head6", (r[:96, None] // HD == np.arange(HC)) * 1.0)
    put("half", ((r[:96, None] // HD) % 2 == np.arange(2)) * 1.0)
    put("half_cols", (r[:, None] // S == (np.arange(D)[None, :] // HD) % 2) * 1.0)
    h12 = np.zeros((96, C, H))
    for c in range(C):
        h12[:, c] = (r[:96, None] // HD + HC * c == np.arange(H)) * 1.0
    put("head12", h12.reshape(96, -1))
    twice = np.zeros((P, 2, 2, S))
    for s in range(2):
        twice[S * s + np.arange(S), s, :, np.arange(S)] = 1
    put("twice", twice.reshape(P, -1))
    put("prio", np.broadcast_to(8.0 - np.arange(8), (P, 8)))
    valid = np.ones((P, TILES))
    valid[IMAGES:, CLS] = 0
    put("valid", valid)
    put("tile_no", np.broadcast_to(np.arange(max(NT0, NT1)), (P, max(NT0, NT1))))
    first = np.zeros((P, H))
    first[0] = 1
    put("first", first)
    return k


def bodies(order, n):
    for i in range(max(n.values()) + max(lag for _, lag in order)):
        for stage, lag in order:
            if 0 <= i - lag < n[stage]:
                yield stage, i - lag


def issued_before(order, n, other, stage, t):
    names = [s for s, _ in order]
    lag = dict(order)
    done = t + lag[stage] - lag[other] + (names.index(other) < names.index(stage))
    return max(0, min(done, n[other]))


def wait(eng, sem, n):
    if n > 0:
        eng.wait_ge(sem, n)


class Chain:

    def __init__(self, eng, sem, n=0):
        self.eng, self.sem, self.n = eng, sem, n

    def link(self, ins):
        self.n += 1
        ins.then_inc(self.sem, 1)
        self.eng.wait_ge(self.sem, self.n)

    def mark(self, ins):
        self.n += 1
        ins.then_inc(self.sem, 1)
        return self.n


def tile_of(u):
    return CLS if u == 0 else u - 1


AREA = 15200


def build(nc, x_feat, w_tok, w_small, rows_in, consts_in, w1_0, w2_0, w1_1, w2_1, out):
    with ExitStack() as ctx:
        def sb(name, shape, dt=F32):
            return ctx.enter_context(nc.sbuf_tensor(name, shape, dt))

        def sem(name):
            return ctx.enter_context(nc.semaphore(name))

        def sems(prefix, names):
            return [sem(prefix + n) for n in names.split()]

        PS = ctx.enter_context(nc.psum_tensor("banks", [P, 8, 512], F32))
        KON = sb("consts_sb", [P, KCOLS])
        ROWS = sb("rows_sb", [P, RCOLS])
        WS = sb("w_small_sb", [97, C, WCOLS])
        HT = sb("h_tok", [P, TILES, D])
        X1 = sb("x_tok", [P, TILES, D])
        LG = sb("gate_logits", [P, TILES, E0])
        W1 = sb("w1_sb", [97, C, E0, FF])
        W2 = sb("w2_sb", [P, E0, FFK, D])
        AR = sb("scratch", [P, AREA])

        def K(name):
            return KON[:, K_AT[name]:K_AT[name] + K_W[name]]

        def ROW(name, w=D, at=0):
            return ROWS[:, R_AT[name] + at:R_AT[name] + at + w]

        def w_small_at(name, c, a, b):
            return WS[0:KC[c], c, W_AT[name] + a:W_AT[name] + b]

        KC = (96, 97)
        ident = K("ident")
        head6 = K("head6")[0:96]
        taken = [0]

        def area(width, parts=P):
            at = taken[0]
            taken[0] += width
            assert taken[0] <= AREA, taken[0]
            return AR[0:parts, at:at + width]

        def chunks(parts, width=P):
            return area(C * width, parts).rearrange("p (c t) -> p c t", c=C)

        loaded = {n: sem("loaded_" + n) for n in ("first", "later", "experts0")}
        vec, pool = sem("vector_chain"), sem("pool_chain")
        out_stored = [sem(f"out_stored{i}") for i in range(3)]
        xg_zeroed = sem("xg_zeroed")
        block = ctx.enter_context(nc.Block())

        XGT = [chunks(97) for _ in range(2)]
        PROB = area(2 * TILES).rearrange("p (k t) -> p k t", k=2)
        between_start = taken[0]
        XG_IN = [area(D) for _ in range(3)]
        shared = area(FK * (3 * P + D))
        HID = [shared[:, i * FF:(i + 1) * FF] for i in range(2)]
        HIDT = [shared[:, (2 + i) * FF:(3 + i) * FF].rearrange("p (k t) -> p k t", k=FFK) for i in range(2)]
        YG = [area(D) for _ in range(2)]
        g_exp, g_prob, g_eq, g_pick, g_off = [area(TILES * E0) for _ in range(5)]
        g_onehot = [area(TILES * E0) for _ in range(3)]
        g_scan = area(TILES * E0)
        g_max, g_sum = area(TILES), area(TILES)
        g_tiles, g_cum, g_base = area(E0), area(E0), area(E0)
        g_le = area(max(NT0 * E0, NT1 * E1))
        g_eid = area(max(NT0, NT1))
        SLOT = sb("slot_of", [P, 2, TILES], I32)
        EID = sb("expert_of", [P, max(NT0, NT1)], I32)
        ZERO = sb("zero", [P, D])
        xg_dram = nc.dram_tensor("tokens_by_expert", [max(NT0, NT1) * P, D], F32, kind="Internal").ap()
        yg_dram = nc.dram_tensor("results_by_expert", [max(NT0, NT1) * P, D], F32, kind="Internal").ap()
        scratch_start = taken[0]

        x_in = [shared[:, i * FK * P:(i + 1) * FK * P].rearrange("p (k t) -> p k t", k=FK) for i in range(3)]
        w_tok_sb = shared[:, 3 * FK * P:].rearrange("p (k e) -> p k e", k=FK)
        xn = [area(D) for _ in range(2)]
        stats1, stats2 = area(6), area(6)
        mv1, mv2 = [area(2) for _ in range(2)], [area(2) for _ in range(2)]
        rstd1, rstd2 = [area(1) for _ in range(2)], [area(1) for _ in range(2)]
        var_eps1, var_eps2, minus_half = area(1), area(1), area(1)
        xT = [chunks(97) for _ in range(2)]
        QKV = [area(5 * D) for _ in range(2)]
        qT = [chunks(96) for _ in range(2)]
        kblk = [area(C * 2 * (MS + 1) * HC, 96).rearrange("p (c s m h) -> p c s m h", c=C, s=2, m=MS + 1)
                for _ in range(2)]
        NV = (MS + 1) * H
        vblk = [area(2 * D, NV).rearrange("p (s e) -> p s e", s=2) for _ in range(2)]
        prod = [area(2 * D).rearrange("p (a e) -> p a e", a=2) for _ in range(2)]
        sraw = area(KEYS0 * H)
        smax = area(H)
        ssub = [area(KEYS0 * H) for _ in range(2)]
        ex = [area(KEYS0 * H) for _ in range(2)]
        rsum = area(H)
        rinv = [area(H) for _ in range(2)]
        exT = [area(P, NV) for _ in range(2)]
        own2 = area(2 * D).rearrange("p (a e) -> p a e", a=2)
        own = [area(D) for _ in range(2)]
        o1 = area(D)
        oatt = [area(D) for _ in range(2)]
        oT = [chunks(97) for _ in range(2)]
        x1T = [chunks(97) for _ in range(2)]

        ORDER_A = [("xT", 1), ("scores", 2), ("x1T", 4), ("pv", 3), ("embed", 0), ("oT", 3), ("logits", 4),
                   ("oproj", 3), ("softmax", 2), ("qkv", 1), ("exp", 2), ("xn", 0), ("heads", 1), ("expT", 2),
                   ("x1", 3), ("dots", 1)]
        NA = {s: TILES for s, _ in ORDER_A}

        def before_a(other, stage, u):
            return issued_before(ORDER_A, NA, other, stage, u)

        x_loaded = [sem(f"x_loaded{i}") for i in range(3)]
        prev_loaded = [sem(f"previous_loaded{i}") for i in range(2)]
        set_up = sem("set_up")
        (embed_done, h_embedded, ln1_var, ln1_rstd, xn_ready, xT_done, xT_ready, qk_done, v_done, qk_taken,
         v_taken, qT_done, kT_done, vrep_done, qT_ready, kblk_ready, vblk_ready, dots_ready, s_done, s_taken,
         s_ready, ex_ready, eT_done, eT_ready, own_ready, pv_done, o_ready, oT_done, oT_ready, oproj_done,
         h_attn, ln2_var, ln2_rstd, x1_ready, x1T_done, x1T_ready, lg_done, lg_taken) = sems(
            "a_", "embed_done h_embedded ln1_var ln1_rstd xn_ready xT_done xT_ready qk_done v_done qk_taken "
                  "v_taken qT_done kT_done vrep_done qT_ready kblk_ready vblk_ready dots_ready s_done s_taken "
                  "s_ready ex_ready eT_done eT_ready own_ready pv_done o_ready oT_done oT_ready oproj_done "
                  "h_attn ln2_var ln2_rstd x1_ready x1T_done x1T_ready lg_done lg_taken")

        def zero_rows(sp, first, tiles):
            sp.dma_start(xg_dram[first * P:(first + tiles) * P].rearrange("(t p) d -> p t d", p=P),
                         ZERO[:, :].unsqueeze(1).broadcast_to([P, tiles, D])).then_inc(xg_zeroed, 16)

        def a_sync(sp):
            first_rows, first_cols = R_AT["ln1_g"], W_AT["qkv1"]
            sp.dma_start(ROWS[:, 0:first_rows], rows_in[:, 0:first_rows].broadcast_to([P, first_rows]))\
                .then_inc(loaded["first"], 16)
            sp.dma_start(KON[:, :], consts_in).then_inc(loaded["first"], 16)
            sp.dma_start(WS[:, :, 0:first_cols], w_small[:, :, 0:first_cols]).then_inc(loaded["first"], 16)
            sp.dma_start(w_tok_sb, w_tok).then_inc(loaded["first"], 16)
            for stage, u in bodies(ORDER_A, NA):
                if stage == "embed" and u == TILES - 1:
                    sp.wait_ge(set_up, 2)
                    zero_rows(sp, 0, NT0)
                if stage == "embed" and u > 0:
                    wait(sp, embed_done, u - 3)
                    sp.dma_start(x_in[(u - 1) % 3], x_feat[u - 1]).then_inc(x_loaded[(u - 1) % 3], 16)
                    if u == 12:
                        sp.dma_start(ROWS[:, first_rows:], rows_in[:, first_rows:].broadcast_to([P, RCOLS - first_rows]))\
                            .then_inc(loaded["later"], 16)
                        sp.dma_start(WS[:, :, first_cols:], w_small[:, :, first_cols:]).then_inc(loaded["later"], 16)
                    if u % 2 == 0:
                        e = u // 2 - 1
                        sp.dma_start(W1[:, :, e, :], w1_0[:, :, e, :]).then_inc(loaded["experts0"], 16)
                        sp.dma_start(W2[:, e], w2_0[:, e]).then_inc(loaded["experts0"], 16)

        def a_tensor(pe):
            def embed(u):
                if u == 0:
                    return
                pe.wait_ge(x_loaded[(u - 1) % 3], 16 * ((u - 1) // 3 + 1))
                wait(pe, h_embedded, u)
                wait(pe, lg_taken, before_a("logits", "embed", u))
                for k in range(FK):
                    mm = pe.matmul(PS[:, 0, 0:D], x_in[(u - 1) % 3][:, k, :], w_tok_sb[:, k, :],
                                   start=k == 0, stop=k == FK - 1)
                mm.then_inc(embed_done, 1)

            def transposed(u, src, bank, done):
                for c in range(C):
                    mm = pe.transpose(PS[0:96, bank, c * P:(c + 1) * P], src[:, 96 * c:96 * c + 96], ident)
                mm.then_inc(done, 1)

            def projected(xt, name, a, b, bank, done):
                for c in range(C):
                    mm = pe.matmul(PS[:, bank, 0:b - a], xt[0:KC[c], c, :], w_small_at(name, c, a, b),
                                   start=c == 0, stop=c == C - 1)
                mm.then_inc(done, 1)

            def to_features(u):
                pe.wait_ge(xn_ready, u + 1)
                wait(pe, xT_ready, u)
                wait(pe, x1T_ready, before_a("x1T", "xT", u))
                transposed(u, xn[u % 2], 1, xT_done)

            def qkv(u):
                pe.wait_ge(xT_ready, u + 1)
                wait(pe, qk_taken, u)
                projected(xT[u % 2], "qkv0", 0, 2 * D, 2, qk_done)
                wait(pe, v_taken, u)
                wait(pe, h_attn, before_a("oproj", "qkv", u))
                projected(xT[u % 2], "qkv0", 2 * D, 3 * D, 3, v_done)

            def heads(u):
                pe.wait_ge(qk_taken, u + 1)
                qkv_u = QKV[u % 2]
                if u > 0:
                    wait(pe, qT_ready, u - 1)
                    wait(pe, oT_ready, before_a("oT", "heads", u))
                    transposed(u, qkv_u[:, 0:D], 4, qT_done)
                wait(pe, kblk_ready, u)
                transposed(u, qkv_u[:, D:2 * D], 5, kT_done)
                pe.wait_ge(v_taken, u + 1)
                wait(pe, vblk_ready, u)
                wait(pe, o_ready, before_a("pv", "heads", u))
                v = qkv_u[:, 2 * D:3 * D]
                if u == 0:
                    mm = pe.matmul(PS[MS * H:NV, 7, 0:D], K("first"), v, start=True, stop=True)
                else:
                    for s in range(2):
                        mm = pe.matmul(PS[0:MS * H, 7, s * D:(s + 1) * D],
                                       K("pick_v")[:, s * MS * H:(s + 1) * MS * H], v, start=True, stop=True)
                mm.then_inc(vrep_done, 1)

            def scores(u):
                if u == 0:
                    return
                pe.wait_ge(qT_ready, u)
                pe.wait_ge(kblk_ready, u + 1)
                wait(pe, s_taken, u - 1)
                wait(pe, eT_ready, before_a("expT", "scores", u) - 1)
                for s in range(2):
                    for c in range(C):
                        out_s = PS[S * s:S * s + S, 6, 0:NV].rearrange("p (m c h) -> p c m h", c=C, h=HC)[:, c]
                        mm = pe.matmul(out_s, qT[u % 2][:, c, S * s:S * s + S], kblk[u % 2][:, c, s],
                                       start=True, stop=True)
                mm.then_inc(s_done, 1)

            def exp_t(u):
                if u == 0:
                    return
                pe.wait_ge(ex_ready, u)
                wait(pe, s_taken, u)
                pe.transpose(PS[0:NV, 6, 0:P], ex[u % 2][:, 0:NV], ident).then_inc(eT_done, 1)

            def pv(u):
                if u == 0:
                    return
                pe.wait_ge(eT_ready, u)
                pe.wait_ge(vblk_ready, before_a("heads", "pv", u))
                wait(pe, o_ready, u)
                for s in range(2):
                    mm = pe.matmul(PS[S * s:S * s + S, 7, 0:D], exT[u % 2][:, S * s:S * s + S],
                                   vblk[u % 2][:, s], start=True, stop=True)
                mm.then_inc(pv_done, 1)

            def out_t(u):
                pe.wait_ge(o_ready, u + 1)
                wait(pe, oT_ready, u)
                wait(pe, qT_ready, before_a("heads", "oT", u) - 1)
                transposed(u, oatt[u % 2], 4, oT_done)

            def out_projection(u):
                pe.wait_ge(oT_ready, u + 1)
                wait(pe, h_attn, u)
                wait(pe, v_taken, before_a("qkv", "oproj", u))
                projected(oT[u % 2], "out0", 0, D, 3, oproj_done)

            def x1_t(u):
                pe.wait_ge(x1_ready, u + 1)
                wait(pe, x1T_ready, u)
                wait(pe, xT_ready, before_a("xT", "x1T", u))
                transposed(u, X1[:, tile_of(u), :], 1, x1T_done)

            def logits(u):
                pe.wait_ge(x1T_ready, u + 1)
                wait(pe, lg_taken, u)
                wait(pe, h_embedded, before_a("embed", "logits", u))
                projected(x1T[u % 2], "gate0", 0, E0, 0, lg_done)

            pe.wait_ge(loaded["first"], 16 * 4)
            pe.wait_ge(set_up, 2)
            step = {"embed": embed, "xT": to_features, "qkv": qkv, "heads": heads, "scores": scores,
                    "expT": exp_t, "pv": pv, "oT": out_t, "oproj": out_projection, "x1T": x1_t, "logits": logits}
            for stage, u in bodies(ORDER_A, NA):
                if stage in step:
                    step[stage](u)

        def a_scalar(act):
            def copy(out_ap, in_ap):
                return act.activation(out_ap, in_ap, ACT.Copy)

            for stage, u in bodies(ORDER_A, NA):
                i = u % 2
                if stage == "xT":
                    act.wait_ge(xT_done, u + 1)
                    wait(act, v_done, u - 1)
                    copy(xT[i][0:96], PS[0:96, 1, 0:C * P].rearrange("p (c t) -> p c t", c=C)).then_inc(xT_ready, 1)
                elif stage == "qkv":
                    act.wait_ge(qk_done, u + 1)
                    wait(act, vrep_done, u - 1)
                    wait(act, own_ready, u - 2)
                    if u == 12:
                        act.wait_ge(o_ready, 1)
                    copy(QKV[i][:, 0:2 * D], PS[:, 2, 0:2 * D]).then_inc(qk_taken, 1)
                    act.wait_ge(v_done, u + 1)
                    copy(QKV[i][:, 2 * D:3 * D], PS[:, 3, 0:D]).then_inc(v_taken, 1)
                elif stage == "heads" and u > 0:
                    act.wait_ge(qT_done, u)
                    wait(act, s_done, u - 2)
                    copy(qT[i], PS[0:96, 4, 0:C * P].rearrange("p (c t) -> p c t", c=C)).then_inc(qT_ready, 1)
                    act.wait_ge(qk_taken, u + 1)
                    act.wait_ge(v_taken, u + 1)
                    for a, b in ((0, 112), (112, 127)):
                        act.dma_start(QKV[i][a + 1:b + 1, 3 * D:5 * D], QKV[i][a:b, D:3 * D]).then_inc(prev_loaded[i], 16)
                elif stage == "exp" and u > 0:
                    act.wait_ge(s_ready, u)
                    wait(act, eT_done, u - 2)
                    wait(act, own_ready, u - 2)
                    act.activation(ex[i], ssub[i], ACT.Exp, scale=HEAD_SCALE).then_inc(ex_ready, 1)
                elif stage == "expT" and u > 0:
                    act.wait_ge(eT_done, u)
                    wait(act, pv_done, u - 2)
                    copy(exT[i], PS[0:NV, 6, 0:P]).then_inc(eT_ready, 1)
                elif stage == "oT":
                    act.wait_ge(oT_done, u + 1)
                    wait(act, oproj_done, u - 1)
                    copy(oT[i][0:96], PS[0:96, 4, 0:C * P].rearrange("p (c t) -> p c t", c=C)).then_inc(oT_ready, 1)
                elif stage == "x1T":
                    act.wait_ge(x1T_done, u + 1)
                    wait(act, lg_done, u - 1)
                    copy(x1T[i][0:96], PS[0:96, 1, 0:C * P].rearrange("p (c t) -> p c t", c=C)).then_inc(x1T_ready, 1)

        def layer_norm_stats(v, chain, src, stats, mv, done):
            chain.link(v.bn_stats(stats, src))
            v.bn_aggr(mv, stats).then_inc(done, 1)

        def a_vector(v, chain):
            v.memset(minus_half, -0.5).then_inc(set_up, 1)
            for i in range(2):
                v.memset(QKV[i][:, 3 * D:5 * D], 0.0)
                v.memset(xT[i][96:97], 1.0)
                v.memset(oT[i][96:97], 1.0)
                v.memset(XGT[i][96:97], 1.0)
                v.memset(x1T[i][96:97], 1.0)
            v.memset(ZERO[:, :], 0.0).then_inc(set_up, 1)
            v.wait_ge(loaded["first"], 16 * 4)
            v.wait_ge(set_up, 2)
            for stage, u in bodies(ORDER_A, NA):
                i, t = u % 2, tile_of(u)
                if stage == "embed":
                    if u == 0:
                        v.tensor_copy(HT[:, t], ROW("cls")).then_inc(h_embedded, 1)
                    else:
                        v.wait_ge(embed_done, u)
                        v.tensor_tensor(HT[:, t], PS[:, 0, 0:D], ROW("b_tok"), ALU.add).then_inc(h_embedded, 1)
                    v.wait_ge(h_embedded, u + 1)
                    layer_norm_stats(v, chain, HT[:, t], stats1, mv1[i], ln1_var)
                elif stage == "xn":
                    v.wait_ge(ln1_rstd, u + 1)
                    wait(v, xT_done, u - 1)
                    v.tensor_scalar(xn[i], HT[:, t], mv1[i][:, 0:1], rstd1[i], ALU.subtract, ALU.mult)\
                        .then_inc(xn_ready, 1)
                elif stage == "heads":
                    v.wait_ge(kT_done, u + 1)
                    wait(v, s_done, u - 2)
                    kT = PS[0:96, 5, 0:C * P].rearrange("p (c t) -> p c t", c=C)
                    mask = head6.unsqueeze(1).unsqueeze(1)
                    if u == 0:
                        for j in range(2):
                            last = v.tensor_tensor(
                                kblk[j][:, :, :, MS, :], kT[:, :, 0:1].unsqueeze(2).broadcast_to([96, C, 2, HC]),
                                mask.broadcast_to([96, C, 2, HC]), ALU.mult)
                    else:
                        for s in range(2):
                            keys = kT[:, :, S * s + STRIDE - 1:S * (s + 1):STRIDE]
                            last = v.tensor_tensor(kblk[i][:, :, s, 0:MS, :],
                                                   keys.unsqueeze(3).broadcast_to([96, C, MS, HC]),
                                                   mask.broadcast_to([96, C, MS, HC]), ALU.mult)
                    last.then_inc(kblk_ready, 1)
                    v.wait_ge(vrep_done, u + 1)
                    wait(v, pv_done, u - 2)
                    if u == 0:
                        rows = slice(MS * H, NV)
                        for j in range(2):
                            last = v.tensor_tensor(vblk[j][rows], PS[rows, 7, 0:D].unsqueeze(1).broadcast_to([H, 2, D]),
                                                   K("head_rows")[rows].unsqueeze(1).broadcast_to([H, 2, D]), ALU.mult)
                    else:
                        n = MS * H
                        last = v.tensor_tensor(vblk[i][0:n], PS[0:n, 7, 0:2 * D].rearrange("p (s e) -> p s e", s=2),
                                               K("head_rows")[0:n].unsqueeze(1).broadcast_to([n, 2, D]), ALU.mult)
                    last.then_inc(vblk_ready, 1)
                elif stage == "scores" and u > 0:
                    v.wait_ge(s_done, u)
                    v.tensor_tensor(sraw[:, 0:NV], PS[:, 6, 0:NV], K("mask0")[:, 0:NV], ALU.add).then_inc(s_taken, 1)
                elif stage == "softmax" and u > 0:
                    v.wait_ge(dots_ready, u)
                    chain.link(v.tensor_reduce(sraw[:, NV:], prod[i].rearrange("p a (h d) -> p (a h) d", d=HD),
                                               AX.X, ALU.add))
                    chain.link(v.tensor_tensor(sraw[:, NV:], sraw[:, NV:], K("mask0")[:, NV:], ALU.add))
                    v.wait_ge(s_taken, u)
                    chain.link(v.tensor_reduce(smax, sraw.rearrange("p (m h) -> p h m", h=H), AX.X, ALU.max))
                    wait(v, ex_ready, u - 2)
                    v.tensor_tensor(ssub[i].rearrange("p (m h) -> p m h", h=H),
                                    sraw.rearrange("p (m h) -> p m h", h=H),
                                    smax.unsqueeze(1).broadcast_to([P, KEYS0, H]), ALU.subtract).then_inc(s_ready, 1)
                elif stage == "expT" and u > 0:
                    v.wait_ge(ex_ready, u)
                    chain.link(v.tensor_reduce(rsum, ex[i].rearrange("p (m h) -> p h m", h=H), AX.X, ALU.add))
                    chain.link(v.reciprocal(rinv[i], rsum))
                elif stage == "pv":
                    wait(v, oT_done, u - 1)
                    if u == 0:
                        v.wait_ge(v_taken, 1)
                        v.tensor_copy(oatt[i], QKV[i][:, 2 * D:3 * D]).then_inc(o_ready, 1)
                    else:
                        v.wait_ge(pv_done, u)
                        v.wait_ge(own_ready, u)
                        chain.link(v.tensor_tensor(o1, PS[:, 7, 0:D], own[i], ALU.add))
                        v.tensor_tensor(oatt[i].rearrange("p (h d) -> p h d", h=H),
                                        o1.rearrange("p (h d) -> p h d", h=H),
                                        rinv[i].unsqueeze(2).broadcast_to([P, H, HD]), ALU.mult).then_inc(o_ready, 1)
                elif stage == "oproj":
                    v.wait_ge(oproj_done, u + 1)
                    v.tensor_tensor(HT[:, t], PS[:, 3, 0:D], HT[:, t], ALU.add).then_inc(h_attn, 1)
                    v.wait_ge(h_attn, u + 1)
                    layer_norm_stats(v, chain, HT[:, t], stats2, mv2[i], ln2_var)
                elif stage == "x1":
                    v.wait_ge(ln2_rstd, u + 1)
                    v.tensor_scalar(X1[:, t], HT[:, t], mv2[i][:, 0:1], rstd2[i], ALU.subtract, ALU.mult)\
                        .then_inc(x1_ready, 1)
                elif stage == "logits":
                    v.wait_ge(lg_done, u + 1)
                    v.tensor_copy(LG[:, t], PS[:, 0, 0:E0]).then_inc(lg_taken, 1)

        def root(g, chain, mv, var_eps, rstd, done):
            chain.link(g.tensor_scalar(var_eps, mv[:, 1:2], EPS_LN, None, ALU.add))
            g.tensor_tensor(rstd, var_eps, minus_half, ALU.pow).then_inc(done, 1)

        def a_gpsimd(g, chain):
            g.wait_ge(set_up, 1)
            for stage, u in bodies(ORDER_A, NA):
                i = u % 2
                if stage == "embed":
                    g.wait_ge(ln1_var, u + 1)
                    root(g, chain, mv1[i], var_eps1, rstd1[i], ln1_rstd)
                elif stage == "oproj":
                    g.wait_ge(ln2_var, u + 1)
                    root(g, chain, mv2[i], var_eps2, rstd2[i], ln2_rstd)
                elif stage == "dots" and u > 0:
                    g.wait_ge(qk_taken, u + 1)
                    n = (u + 1) // 2 if i else u // 2
                    g.wait_ge(prev_loaded[i], 32 * n)
                    wait(g, s_ready, u - 2)
                    keys = QKV[i][:, D:5 * D].rearrange("p (a e) -> p a e", a=2)[:, :, 0:D]
                    g.tensor_tensor(prod[i], keys, QKV[i][:, 0:D].unsqueeze(1).broadcast_to([P, 2, D]), ALU.mult)\
                        .then_inc(dots_ready, 1)
                elif stage == "expT" and u > 0:
                    g.wait_ge(ex_ready, u)
                    vals = QKV[i][:, D:5 * D].rearrange("p (a e) -> p a e", a=2)[:, :, D:2 * D]
                    w = ex[i][:, NV:].unsqueeze(2).broadcast_to([P, 2 * H, HD])
                    chain.link(g.tensor_tensor(own2.rearrange("p a (h d) -> p a h d", h=H),
                                               vals.rearrange("p a (h d) -> p a h d", h=H),
                                               w.rearrange("p (a h) d -> p a h d", a=2), ALU.mult))
                    wait(g, o_ready, u - 1)
                    g.tensor_tensor(own[i], own2[:, 0], own2[:, 1], ALU.add).then_inc(own_ready, 1)


        (r_shifted, r_exp, r_onehot, r_counted, r_slots, r_done) = sems(
            "r_", "shifted exp onehot counted slots done")

        def r_vector(v, chain, layer):
            E, top, tiles = ((E0, TOP0, NT0), (E1, TOP1, NT1))[layer]

            def grid(a):
                return a[:, 0:TILES * E].rearrange("p (t e) -> p t e", e=E)

            def per_tile(a):
                return a.unsqueeze(2).broadcast_to([P, TILES, E])

            def per_expert(a):
                return a.unsqueeze(1).broadcast_to([P, TILES, E])

            lg, ex_, pr, eq, pk, off = LG[:, :, 0:E], grid(g_exp), grid(g_prob), grid(g_eq), grid(g_pick), grid(g_off)
            hot = [grid(a) for a in g_onehot]
            v.wait_ge(lg_taken, TILES * (layer + 1))
            v.wait_ge(loaded["later"], 16 * 2)
            chain.link(v.tensor_reduce(g_max, lg, AX.X, ALU.max))
            v.tensor_tensor(ex_, lg, per_tile(g_max), ALU.subtract).then_inc(r_shifted, 1)
            v.wait_ge(r_exp, layer + 1)
            chain.link(v.tensor_reduce(g_sum, pr, AX.X, ALU.add))
            chain.link(v.reciprocal(g_sum, g_sum))
            chain.link(v.tensor_tensor(pr, pr, per_tile(g_sum), ALU.mult))
            src = pr
            for k in range(top):
                chain.link(v.tensor_reduce(PROB[:, k], src, AX.X, ALU.max))
                chain.link(v.tensor_tensor(eq, src, per_tile(PROB[:, k]), ALU.is_equal))
                chain.link(v.tensor_tensor(pk, eq, per_expert(K("prio")[:, 0:E]), ALU.mult))
                chain.link(v.tensor_reduce(g_max, pk, AX.X, ALU.max))
                chain.link(v.tensor_tensor(hot[k], pk, per_tile(g_max), ALU.is_equal))
                if k + 1 < top:
                    chain.link(v.scalar_tensor_tensor(ex_, hot[k], -2.0, pr, ALU.mult, ALU.add))
                    src = ex_
            for k in range(top):
                chain.link(v.tensor_tensor(hot[k], hot[k], per_tile(K("valid")), ALU.mult))
            if top == 2:
                v.tensor_tensor(hot[2], hot[0], hot[1], ALU.add).then_inc(r_onehot, 1)
            else:
                v.tensor_copy(hot[2], hot[0]).then_inc(r_onehot, 1)
            v.wait_ge(r_counted, layer + 1)
            rows_before = PS[:, 0, 0:TILES * E].rearrange("p (t e) -> p t e", e=E)
            counts = PS[:, 1, 0:TILES * E].rearrange("p (t e) -> p t e", e=E)
            scan = g_scan[:, 0:TILES * E].rearrange("p (e t) -> p e t", e=E)
            for e in range(E):
                last = v.tensor_tensor_scan(scan[:, e], K("ones")[:, 0:TILES], counts[:, :, e], 0.0, ALU.mult, ALU.add)
            chain.link(last)
            chain.link(v.tensor_tensor(off, rows_before, scan.rearrange("p e t -> p t e"), ALU.add))
            chain.link(v.tensor_tensor(off, off, counts, ALU.subtract))
            tl, cum, base = g_tiles[:, 0:E], g_cum[:, 0:E], g_base[:, 0:E]
            chain.link(v.tensor_scalar(tl, scan[:, :, TILES - 1], 1.0 / P, (P - 1) / P - (P - 1) / (2 * P),
                                       ALU.mult, ALU.add))
            chain.link(v.tensor_scalar(tl, tl, MAGIC, MAGIC, ALU.add, ALU.subtract))
            chain.link(v.tensor_tensor_scan(cum, K("ones")[:, 0:E], tl, 0.0, ALU.mult, ALU.add))
            chain.link(v.tensor_tensor(base, cum, tl, ALU.subtract))
            chain.link(v.scalar_tensor_tensor(off, per_expert(base), float(P), off, ALU.mult, ALU.add))
            for k in range(top):
                chain.link(v.tensor_tensor(pk, hot[k], off, ALU.mult))
                chain.link(v.tensor_reduce(g_max, pk, AX.X, ALU.add))
                last = v.tensor_copy(SLOT[:, k], g_max)
                last.then_inc(r_slots, 1)
                v.wait_ge(r_slots, (0, TOP0)[layer] + k + 1)
            le = g_le[:, 0:tiles * E].rearrange("p (t e) -> p t e", e=E)
            chain.link(v.tensor_tensor(le, cum.unsqueeze(1).broadcast_to([P, tiles, E]),
                                       K("tile_no")[:, 0:tiles].unsqueeze(2).broadcast_to([P, tiles, E]), ALU.is_le))
            chain.link(v.tensor_reduce(g_eid[:, 0:tiles], le, AX.X, ALU.add))
            v.tensor_scalar(EID[:, 0:tiles], g_eid[:, 0:tiles], float(E - 1), None, ALU.min).then_inc(r_done, 1)
            v.wait_ge(r_done, layer + 1)

        def r_scalar(act, layer):
            E = (E0, E1)[layer]
            act.wait_ge(r_shifted, layer + 1)
            act.activation(g_prob[:, 0:TILES * E], g_exp[:, 0:TILES * E], ACT.Exp).then_inc(r_exp, 1)

        def r_tensor(pe, layer, bank_free):
            E = (E0, E1)[layer]
            pe.wait_ge(loaded["later"], 16 * 2)
            pe.wait_ge(r_onehot, layer + 1)
            bank_free(pe)
            pe.matmul(PS[:, 0, 0:TILES * E], K("before"), g_onehot[2][:, 0:TILES * E], start=True, stop=True)
            pe.matmul(PS[:, 1, 0:TILES * E], K("ones"), g_onehot[2][:, 0:TILES * E], start=True, stop=True)\
                .then_inc(r_counted, 1)

        def r_gpsimd(g, layer):
            top = (TOP0, TOP1)[layer]
            g.wait_ge(xg_zeroed, 16 * (1, 1 + ZERO_PARTS)[layer])
            for k in range(top):
                g.wait_ge(r_slots, (0, TOP0)[layer] + k + 1)
                for t in range(TILES):
                    n = P if t < CLS else IMAGES
                    slots = bass.IndirectOffsetOnAxis(ap=SLOT[0:n, k, t:t + 1], axis=0)
                    g.indirect_dma_start(out=xg_dram[0:(NT0, NT1)[layer] * P], out_offset=slots, in_=X1[0:n, t],
                                         in_offset=None).then_inc(xg_written, 16)

        xg_written = sem("xg_written")
        xg_loaded = [sem(f"xg_loaded{i}") for i in range(3)]
        yg_stored = [sem(f"yg_stored{i}") for i in range(2)]
        (m_xT_done, m_xT_ready, m_h_done, m_act_ready, m_hT_done, m_hT_ready_a, m_hT_ready_v, m_y_done,
         m_y_ready) = sems("m_", "xT_done xT_ready h_done act_ready hT_done hT_ready_a hT_ready_v y_done y_ready")
        ORDER_M = [("hT", 2), ("xT", 0), ("h", 1), ("y", 2)]
        LAYER = ((E0, NT0, 0), (E1, NT1, NT0))

        def m_steps(eng, layer, order):
            _, tiles, _ = LAYER[layer]
            for k in range(UNROLL):
                for stage, lag in order:
                    if k >= lag:
                        yield stage, 0, k - lag
            with eng.Fori(1, tiles // UNROLL) as i:
                for k in range(UNROLL):
                    for stage, lag in order:
                        yield stage, i, k - lag
            for k in range(max(lag for _, lag in order)):
                for stage, lag in order:
                    if k < lag:
                        yield stage, tiles // UNROLL, k - lag

        def m_tiles(layer, i, r, ahead=0):
            return i * UNROLL + (LAYER[layer][2] + r + ahead)

        def m_slot_loads(layer, i, r, slots):
            return i * (UNROLL // slots) + (LAYER[layer][2] // slots + r // slots + 1)

        def m_sync(sp, layer):
            _, tiles, t0 = LAYER[layer]
            sp.wait_ge(xg_written, 16 * TILES * (TOP0, TOP0 + TOP1)[layer])
            for stage, i, r in m_steps(sp, layer, [("load", 0), ("store", 3)]):
                rows = bass.ds((i * UNROLL + r) * P, P)
                if stage == "load":
                    wait(sp, m_xT_done, m_tiles(layer, i, r, -2))
                    sp.dma_start(XG_IN[r % 3], xg_dram[rows]).then_inc(xg_loaded[r % 3], 16)
                else:
                    sp.wait_ge(m_y_ready, m_tiles(layer, i, r, 1))
                    sp.dma_start(yg_dram[rows], YG[r % 2]).then_inc(yg_stored[r % 2], 16)

        def m_tensor(pe, layer):
            E = LAYER[layer][0]

            def expert(i, r):
                return pe.value_load(EID[0:1, bass.ds(i * UNROLL + r, 1)], min_val=0, max_val=E - 1)

            pe.wait_ge(r_done, layer + 1)
            for stage, i, r in m_steps(pe, layer, ORDER_M):
                before, this, k2 = m_tiles(layer, i, r), m_tiles(layer, i, r, 1), r % 2
                if stage == "xT":
                    pe.wait_ge(xg_loaded[r % 3], m_slot_loads(layer, i, r, 3) * 16)
                    wait(pe, m_xT_ready, before)
                    for c in range(C):
                        mm = pe.transpose(PS[0:96, 0, c * P:(c + 1) * P], XG_IN[r % 3][:, 96 * c:96 * c + 96], ident)
                    mm.then_inc(m_xT_done, 1)
                elif stage == "h":
                    e = expert(i, r)
                    pe.wait_ge(m_xT_ready, this)
                    wait(pe, m_act_ready, before)
                    for b in range(2):
                        for c in range(C):
                            mm = pe.matmul(PS[:, 2 + b, 0:HALF], XGT[k2][0:KC[c], c],
                                           W1[0:KC[c], c, bass.ds(e, 1), b * HALF:(b + 1) * HALF]
                                           .rearrange("p a f -> p (a f)"), start=c == 0, stop=c == C - 1)
                    mm.then_inc(m_h_done, 1)
                elif stage == "hT":
                    pe.wait_ge(m_act_ready, this)
                    wait(pe, m_hT_ready_a, before)
                    wait(pe, m_hT_ready_v, before)
                    for k in range(FFK):
                        mm = pe.transpose(PS[:, 4 + k // 3, (k % 3) * P:(k % 3 + 1) * P],
                                          HID[k2][:, k * P:(k + 1) * P], ident)
                    mm.then_inc(m_hT_done, 1)
                elif stage == "y":
                    e = expert(i, r)
                    pe.wait_ge(m_hT_ready_a, this)
                    pe.wait_ge(m_hT_ready_v, this)
                    wait(pe, m_y_ready, before)
                    for k in range(FFK):
                        mm = pe.matmul(PS[:, 6, 0:D], HIDT[k2][:, k],
                                       W2[:, bass.ds(e, 1), k].rearrange("p a d -> p (a d)"),
                                       start=k == 0, stop=k == FFK - 1)
                    mm.then_inc(m_y_done, 1)

        def m_scalar(act, layer):
            func = (ACT.Gelu, ACT.Relu)[layer]
            for stage, i, r in m_steps(act, layer, ORDER_M):
                last_but_one, this, k2 = m_tiles(layer, i, r, -1), m_tiles(layer, i, r, 1), r % 2
                if stage == "xT":
                    act.wait_ge(m_xT_done, this)
                    wait(act, m_h_done, last_but_one)
                    act.activation(XGT[k2][0:96], PS[0:96, 0, 0:C * P].rearrange("p (c t) -> p c t", c=C),
                                   ACT.Copy).then_inc(m_xT_ready, 1)
                elif stage == "h":
                    act.wait_ge(m_h_done, this)
                    wait(act, m_hT_done, last_but_one)
                    act.activation(HID[k2].rearrange("p (b f) -> p b f", b=2), PS[:, 2:4, 0:HALF], func)\
                        .then_inc(m_act_ready, 1)
                elif stage == "hT":
                    act.wait_ge(m_hT_done, this)
                    wait(act, m_y_done, last_but_one)
                    act.activation(HIDT[k2][:, 0:3], PS[:, 4, 0:3 * P].rearrange("p (k t) -> p k t", k=3),
                                   ACT.Copy).then_inc(m_hT_ready_a, 1)

        def m_vector(v, layer):
            E = LAYER[layer][0]
            for stage, i, r in m_steps(v, layer, ORDER_M):
                last_but_one, this, k2 = m_tiles(layer, i, r, -1), m_tiles(layer, i, r, 1), r % 2
                if stage == "hT":
                    v.wait_ge(m_hT_done, this)
                    wait(v, m_y_done, last_but_one)
                    v.tensor_copy(HIDT[k2][:, 3:6], PS[:, 5, 0:3 * P].rearrange("p (k t) -> p k t", k=3))\
                        .then_inc(m_hT_ready_v, 1)
                elif stage == "y":
                    e = v.value_load(EID[0:1, bass.ds(i * UNROLL + r, 1)], min_val=0, max_val=E - 1)
                    v.wait_ge(m_y_done, this)
                    wait(v, yg_stored[k2], (m_slot_loads(layer, i, r, 2) - 1) * 16)
                    b2 = ROWS[:, bass.ds(e * D + R_AT[("b2_0", "b2_1")[layer]], D)]
                    v.tensor_tensor(YG[k2], PS[:, 6, 0:D], b2, ALU.add).then_inc(m_y_ready, 1)

        taken[0] = between_start
        Y = [area(D) for _ in range(3)]
        c_stats = area(6)
        c_mv = [area(2) for _ in range(2)]
        c_eps, c_minus_half, c_magic = area(1), area(1), area(1)
        c_rstd = [area(1) for _ in range(2)]
        inv_q, inv_k, inv_v, alpha, beta = [area(1) for _ in range(5)]
        c_xn = [area(D) for _ in range(2)]
        common_start = taken[0]

        def half_area(width, parts=P):
            return area((width + 1) // 2, parts).bitcast(BF16)[:, 0:width]

        def tokens(parts=97):
            return area(C * 2 * TOK, parts).rearrange("p (c t) -> p c t", c=C)

        def patches(a):
            return a[:, :, 0:P].rearrange("p c (s t) -> p c s t", s=2)

        c_xT = [tokens() for _ in range(2)]
        clsT = area(C * IMAGES, 97).rearrange("p (c b) -> p c b", c=C)
        clsOT = area(C * IMAGES, 97).rearrange("p (c b) -> p c b", c=C)
        cls_v = half_area(D, IMAGES)
        ident_h = half_area(P)
        twice = half_area(2 * P).rearrange("p (s d t) -> p s d t", s=2, d=2)
        t_qk = [area(2 * C * 2 * TOK, 96).rearrange("p (a c t) -> p a c t", a=2, c=C) for _ in range(2)]
        t_v = [area(D) for _ in range(2)]
        t_v_h = [half_area(D) for _ in range(2)]
        t_s = [area(3 * C * 2 * TOK).rearrange("p (j t) -> p j t", j=3) for _ in range(2)]
        t_sc = [area(2 * TOK, H).rearrange("p (s t) -> p s t", s=2) for _ in range(2)]
        t_o = [area(C * 2 * TOK, 96).rearrange("p (c s t) -> p c s t", c=C, s=2) for _ in range(2)]
        q_h = [half_area(C * 2 * TOK, 96).rearrange("p (c s t) -> p c s t", c=C, s=2) for _ in range(2)]
        k_h = [half_area(C * 2 * P, 96).rearrange("p (c s a t) -> p c s a t", c=C, s=2, a=2) for _ in range(2)]
        kc_h = [half_area(C * 2 * H, 96).rearrange("p (c s h) -> p c s h", c=C, s=2) for _ in range(2)]
        v_h = [half_area(2 * D).rearrange("p (s e) -> p s e", s=2) for _ in range(2)]
        c_kc = area(2 * C, 96).rearrange("p (c s) -> p c s", c=C)
        vc_h = [half_area(2 * D, H).rearrange("p (s e) -> p s e", s=2) for _ in range(2)]
        a_h = [half_area(3 * C * 2 * TOK).rearrange("p (j t) -> p j t", j=3) for _ in range(2)]
        ac_h = [half_area(2 * TOK, H).rearrange("p (s t) -> p s t", s=2) for _ in range(2)]
        c_oT = [chunks(97) for _ in range(2)]

        c_gathered = [sem(f"c_gathered{i}") for i in range(3)]
        (h_moe, q_var, q_rstd, q_xn, q_xT_done, q_xT_ready, q_cls_ready, q_qk_done, q_v_done, q_vc_done,
         q_qk_taken, q_v_taken, q_qk_clipped, q_q_ready, q_k_ready, q_kc_ready, q_v_whole, q_vrep_done,
         q_v_ready, q_vc_ready, q_s_done, q_s_taken,
         q_s_clipped, q_a_ready, q_pv_done, q_o_taken, q_o_clipped, q_oT_ready, q_oproj_done, h_quant) = sems(
            "q_", "moe var rstd xn xT_done xT_ready cls_ready qk_done v_done vc_done qk_taken v_taken "
                  "qk_clipped q_ready k_ready kc_ready v_whole vrep_done v_ready vc_ready s_done s_taken "
                  "s_clipped a_ready pv_done o_taken "
                  "o_clipped oT_ready oproj_done h_quant")
        loaded_experts1 = sem("loaded_experts1")
        ORDER_Q = [("gather", 0), ("quant", 4), ("oproj", 6), ("xT", 3), ("vrep", 4), ("pv", 5), ("moe", 2),
                   ("scores", 4), ("qkv", 3), ("norm", 2)]
        NQ = {s: TILES for s, _ in ORDER_Q}

        def before_q(other, stage, u):
            return issued_before(ORDER_Q, NQ, other, stage, u)

        def stored_total(layer):
            n = LAYER[layer][1] + LAYER[layer][2]
            return [16 * ((n + 1 - i) // 2) for i in range(2)]

        def experts_done(eng, layer):
            for i, n in enumerate(stored_total(layer)):
                eng.wait_ge(yg_stored[i], n)

        def q_sync(sp):
            experts_done(sp, 0)
            for part in range(ZERO_PARTS):
                sp.wait_ge(h_moe, part + 1)
                zero_rows(sp, part * NT1 // ZERO_PARTS, NT1 // ZERO_PARTS)
            for e in range(E1):
                sp.wait_ge(h_moe, ZERO_PARTS + 2 * e + 2)
                sp.dma_start(W1[:, :, e, :], w1_1[:, :, e, :]).then_inc(loaded_experts1, 16)
                sp.dma_start(W2[:, e], w2_1[:, e]).then_inc(loaded_experts1, 16)

        def q_tensor(pe):
            def to_features(u):
                pe.wait_ge(q_xn, u + 1)
                wait(pe, q_xT_ready, u)
                wait(pe, q_v_taken, u)
                for c in range(C):
                    mm = pe.transpose(PS[0:96, 0, c * P:(c + 1) * P], c_xn[u % 2][:, 96 * c:96 * c + 96], ident)
                mm.then_inc(q_xT_done, 1)

            def qkv(u):
                pe.wait_ge(q_xT_ready, u + 1)
                if u == 0:
                    for c in range(C):
                        mm = pe.matmul(PS[0:IMAGES, 0, C * P:C * P + D], clsT[0:KC[c], c],
                                       w_small_at("qkv1", c, 2 * D, 3 * D), start=c == 0, stop=c == C - 1)
                    mm.then_inc(q_v_done, 1)
                    return
                x = c_xT[u % 2]
                for c in range(C):
                    mm = pe.matmul(PS[:, 0, C * P:C * P + D], x[0:KC[c], c, 0:P], w_small_at("qkv1", c, 2 * D, 3 * D),
                                   start=c == 0, stop=c == C - 1)
                mm.then_inc(q_v_done, 1)
                pe.wait_ge(q_cls_ready, u)
                wait(pe, q_qk_taken, u - 1)
                wait(pe, q_vc_ready, before_q("vrep", "qkv", u) - 1)
                for a in range(2):
                    for oc in range(C):
                        for c in range(C):
                            at = a * D + 96 * oc
                            mm = pe.matmul(PS[0:96, 1 + a, oc * 2 * TOK:(oc + 1) * 2 * TOK],
                                           w_small_at("qkv1", c, at, at + 96), x[0:KC[c], c],
                                           start=c == 0, stop=c == C - 1)
                mm.then_inc(q_qk_done, 1)

            def replicate(u):
                if u == 0:
                    return
                pe.wait_ge(q_v_whole, u + 1)
                wait(pe, q_v_ready, u - 1)
                for s in range(2):
                    mm = pe.matmul(PS[:, 3, s * D:(s + 1) * D], twice[:, s].rearrange("p d t -> p (d t)"),
                                   t_v_h[u % 2], start=True, stop=True)
                mm.then_inc(q_vrep_done, 1)
                wait(pe, q_vc_ready, u - 1)
                wait(pe, q_qk_taken, before_q("qkv", "vrep", u) - 1)
                for s in range(2):
                    b = 2 * (u - 1) + s
                    mm = pe.matmul(PS[0:H, 1 + s, 4 * TOK:4 * TOK + D], ident_h[0:IMAGES, b:b + 1].broadcast_to([IMAGES, H]),
                                   cls_v, start=True, stop=True)
                mm.then_inc(q_vc_done, 1)

            def scores(u):
                if u == 0:
                    return
                q, k, kc = q_h[u % 2], k_h[u % 2], kc_h[u % 2]
                pe.wait_ge(q_q_ready, u)
                pe.wait_ge(q_k_ready, u)
                pe.wait_ge(q_kc_ready, u)
                wait(pe, q_s_taken, u - 1)
                wait(pe, h_quant, before_q("oproj", "scores", u) - 1)
                for c in range(C):
                    for s in range(2):
                        for j in range(3):
                            r, at = slice(32 * j, 32 * j + 32), (2 * c + s) * TOK
                            pe.matmul(PS[:, 4 + j, at:at + TOK], k[r, c, s].rearrange("p a t -> p (a t)"),
                                      q[r, c, s], start=True, stop=True)
                for s in range(2):
                    for c in range(C):
                        mm = pe.matmul(PS[0:H, 4, (4 + s) * TOK:(5 + s) * TOK], kc[:, c, s], q[:, c, s],
                                       start=c == 0, stop=c == C - 1)
                mm.then_inc(q_s_done, 1)

            def pv(u):
                if u == 0:
                    return
                pe.wait_ge(q_a_ready, u)
                pe.wait_ge(q_v_ready, u)
                pe.wait_ge(q_vc_ready, u)
                wait(pe, q_o_taken, u - 1)
                for s in range(2):
                    for c in range(C):
                        out_at = PS[0:96, 7, (c * 2 + s) * TOK:(c * 2 + s + 1) * TOK]
                        pe.matmul(out_at, vc_h[u % 2][:, s, 96 * c:96 * c + 96], ac_h[u % 2][:, s],
                                  start=True, stop=False, skip_group_check=True)
                        for jj in range(3):
                            cols = slice(96 * c + 32 * jj, 96 * c + 32 * jj + 32)
                            mm = pe.matmul(PS[32 * jj:32 * jj + 32, 7, (c * 2 + s) * TOK:(c * 2 + s + 1) * TOK],
                                           v_h[u % 2][:, s, cols],
                                           a_h[u % 2][:, jj, (c * 2 + s) * TOK:(c * 2 + s + 1) * TOK],
                                           start=False, stop=True, skip_group_check=True)
                mm.then_inc(q_pv_done, 1)

            def out_projection(n, u):
                pe.wait_ge(q_oT_ready, u or PAIRS)
                wait(pe, h_quant, n - 1)
                wait(pe, q_s_taken, before_q("scores", "oproj", u) - 1 if u else PAIRS)
                m = IMAGES if u == 0 else P
                for c in range(C):
                    o = clsOT[0:KC[c], c] if u == 0 else c_oT[u % 2][0:KC[c], c]
                    mm = pe.matmul(PS[0:m, 5, 4 * TOK:4 * TOK + D], o, w_small_at("out1", c, 0, D),
                                   start=c == 0, stop=c == C - 1)
                mm.then_inc(q_oproj_done, 1)

            pe.wait_ge(set_up, 3)
            for stage, u in bodies(ORDER_Q, NQ):
                if stage == "xT":
                    to_features(u)
                elif stage == "qkv":
                    qkv(u)
                elif stage == "vrep":
                    replicate(u)
                elif stage == "scores":
                    scores(u)
                elif stage == "pv":
                    pv(u)
                elif stage == "oproj" and u > 0:
                    out_projection(u, u)
            out_projection(TILES, 0)

        def q_scalar(act):
            def rounded(out_ap, in_ap, scale):
                n = in_ap.shape[0]
                return act.activation(out_ap, in_ap, ACT.Identity, bias=c_magic[0:n], scale=scale[0:n])

            act.wait_ge(set_up, 3)
            for stage, u in bodies(ORDER_Q, NQ):
                i = u % 2
                if stage == "xT":
                    act.wait_ge(q_xT_done, u + 1)
                    ps = PS[0:96, 0, 0:C * P].rearrange("p (c t) -> p c t", c=C)
                    if u == 0:
                        act.activation(clsT[0:96], ps[:, :, 0:IMAGES], ACT.Copy).then_inc(q_xT_ready, 1)
                    else:
                        wait(act, q_qk_done, u - 2)
                        act.activation(c_xT[i][0:96, :, 0:P], ps, ACT.Copy).then_inc(q_xT_ready, 1)
                elif stage == "qkv":
                    act.wait_ge(q_v_done, u + 1)
                    wait(act, q_v_whole, u - 1)
                    n = IMAGES if u == 0 else P
                    rounded(t_v[i][0:n], PS[0:n, 0, C * P:C * P + D], inv_v).then_inc(q_v_taken, 1)
                    if u > 0:
                        act.wait_ge(q_qk_done, u)
                        wait(act, q_q_ready, u - 2)
                        wait(act, q_k_ready, u - 2)
                        wait(act, q_kc_ready, u - 2)
                        for a, inv in ((0, inv_q), (1, inv_k)):
                            last = rounded(t_qk[i][:, a], PS[0:96, 1 + a, 0:C * 2 * TOK]
                                           .rearrange("p (c t) -> p c t", c=C), inv)
                        last.then_inc(q_qk_taken, 1)
                elif stage == "scores" and u > 0:
                    act.wait_ge(q_s_done, u)
                    wait(act, q_a_ready, u - 2)
                    rounded(t_s[i], PS[:, 4:7, 0:4 * TOK], alpha)
                    rounded(t_sc[i], PS[0:H, 4, 4 * TOK:6 * TOK].rearrange("p (s t) -> p s t", s=2), alpha)\
                        .then_inc(q_s_taken, 1)
                elif stage == "pv" and u > 0:
                    act.wait_ge(q_pv_done, u)
                    wait(act, q_oT_ready, u - 2)
                    rounded(t_o[i], PS[0:96, 7, 0:C * 2 * TOK].rearrange("p (c s t) -> p c s t", c=C, s=2), beta)\
                        .then_inc(q_o_taken, 1)

        def q_vector(v, chain):
            def clip(x, lo, hi):
                return v.tensor_scalar(x, x, MAGIC + lo, MAGIC + hi, ALU.max, ALU.min)

            experts_done(v, 0)
            v.memset(c_minus_half, -0.5)
            v.memset(c_magic, MAGIC)
            for i in range(2):
                v.memset(c_xT[i][96:97], 1.0)
                v.memset(c_oT[i][96:97], 1.0)
            v.memset(clsT[96:97], 1.0)
            v.memset(clsOT[96:97], 1.0)
            v.tensor_copy(ident_h, ident)
            for s in range(2):
                last = v.tensor_copy(twice[:, s], ident[:, s * S:(s + 1) * S].unsqueeze(1).broadcast_to([P, 2, S]))
            chain.link(last)
            chain.link(v.reciprocal(inv_q, ROW("s_q", 1)))
            chain.link(v.reciprocal(inv_k, ROW("s_k", 1)))
            chain.link(v.reciprocal(inv_v, ROW("s_v", 1)))
            chain.link(v.reciprocal(alpha, ROW("s_attn", 1)))
            chain.link(v.tensor_scalar(alpha, alpha, float(np.float32(HEAD_SCALE) * np.float32(1.0 / TOK)), None, ALU.mult))
            chain.link(v.tensor_tensor(alpha, alpha, ROW("s_q", 1), ALU.mult))
            chain.link(v.tensor_tensor(alpha, alpha, ROW("s_k", 1), ALU.mult))
            chain.link(v.reciprocal(beta, ROW("s_after", 1)))
            chain.link(v.tensor_tensor(beta, beta, ROW("s_attn", 1), ALU.mult))
            v.tensor_tensor(beta, beta, ROW("s_v", 1), ALU.mult).then_inc(set_up, 1)
            for stage, u in bodies(ORDER_Q, NQ):
                i, t = u % 2, tile_of(u)
                if stage == "moe":
                    v.wait_ge(c_gathered[u % 3], 16 * (u // 3 + 1))
                    n = IMAGES if u == 0 else P
                    v.scalar_tensor_tensor(HT[0:n, t], Y[u % 3][0:n], PROB[0:n, 0, t:t + 1], HT[0:n, t], ALU.mult,
                                           ALU.add)\
                        .then_inc(h_moe, 1)
                    v.wait_ge(h_moe, u + 1)
                    layer_norm_stats(v, chain, HT[:, t], c_stats, c_mv[i], q_var)
                elif stage == "norm":
                    v.wait_ge(q_rstd, u + 1)
                    wait(v, q_xT_done, u - 1)
                    v.tensor_scalar(c_xn[i], HT[:, t], c_mv[i][:, 0:1], c_rstd[i], ALU.subtract, ALU.mult)\
                        .then_inc(q_xn, 1)
                elif stage == "qkv":
                    v.wait_ge(q_v_taken, u + 1)
                    n = IMAGES if u == 0 else P
                    chain.link(clip(t_v[i][0:n], LEVEL_LO, LEVEL_HI))
                    wait(v, q_vrep_done, u - 2)
                    v.tensor_scalar(cls_v if u == 0 else t_v_h[i], t_v[i][0:n], MAGIC, None, ALU.subtract)\
                        .then_inc(q_v_whole, 1)
                elif stage == "quant" and u > 0:
                    v.wait_ge(q_qk_taken, u)
                    clip(t_qk[i], LEVEL_LO, LEVEL_HI).then_inc(q_qk_clipped, 1)
                    v.wait_ge(q_qk_clipped, u)
                    wait(v, q_s_done, u - 2)
                    k = t_qk[i][:, 1]
                    for a in range(2):
                        last = v.tensor_scalar(k_h[i][:, :, :, a], patches(k), MAGIC, K("half")[0:96, a:a + 1],
                                               ALU.subtract, ALU.mult)
                    last.then_inc(q_k_ready, 1)
                    v.tensor_scalar(q_h[i][:, :, :, 0:S], patches(t_qk[i][:, 0]), MAGIC, None, ALU.subtract)\
                        .then_inc(q_q_ready, 1)
                elif stage == "vrep" and u > 0:
                    v.wait_ge(q_vrep_done, u)
                    wait(v, q_pv_done, u - 2)
                    v.tensor_tensor(v_h[i], PS[:, 3, 0:2 * D].rearrange("p (s e) -> p s e", s=2),
                                    K("half_cols").unsqueeze(1).broadcast_to([P, 2, D]), ALU.mult)\
                        .then_inc(q_v_ready, 1)
                    v.wait_ge(q_vc_done, u)
                    v.tensor_tensor(vc_h[i], PS[0:H, 1:3, 4 * TOK:4 * TOK + D],
                                    K("head_rows")[0:H].unsqueeze(1).broadcast_to([H, 2, D]), ALU.mult)\
                        .then_inc(q_vc_ready, 1)
                elif stage == "scores" and u > 0:
                    v.wait_ge(q_s_taken, u)
                    clip(t_s[i], 0.0, LEVEL_ATTN)
                    chain.link(clip(t_sc[i], 0.0, LEVEL_ATTN))
                    wait(v, q_pv_done, u - 2)
                    v.tensor_scalar(ac_h[i], t_sc[i], MAGIC, None, ALU.subtract)
                    v.tensor_scalar(a_h[i], t_s[i], MAGIC, None, ALU.subtract).then_inc(q_a_ready, 1)
                elif stage == "pv" and u > 0:
                    v.wait_ge(q_o_taken, u)
                    clip(t_o[i], LEVEL_LO, LEVEL_HI).then_inc(q_o_clipped, 1)
                    v.wait_ge(q_o_clipped, u)
                    wait(v, q_oproj_done, u - 2)
                    v.tensor_scalar(patches(c_oT[i][0:96]), t_o[i][:, :, :, 0:S], MAGIC,
                                    ROW("s_after", 1)[0:96], ALU.subtract, ALU.mult)
                    b = 2 * (u - 1)
                    v.tensor_scalar(clsOT[0:96, :, b:b + 2], t_o[i][:, :, :, S], MAGIC, ROW("s_after", 1)[0:96],
                                    ALU.subtract, ALU.mult).then_inc(q_oT_ready, 1)
                elif stage == "oproj" and u > 0:
                    v.wait_ge(q_oproj_done, u)
                    v.tensor_tensor(HT[:, t], PS[:, 5, 4 * TOK:4 * TOK + D], HT[:, t], ALU.add).then_inc(h_quant, 1)
            v.wait_ge(q_oproj_done, TILES)
            v.tensor_tensor(HT[0:IMAGES, CLS], PS[0:IMAGES, 5, 4 * TOK:4 * TOK + D], HT[0:IMAGES, CLS], ALU.add)\
                .then_inc(h_quant, 1)

        def q_gpsimd(g, chain):
            experts_done(g, 0)
            for stage, u in bodies(ORDER_Q, NQ):
                i, t = u % 2, tile_of(u)
                if stage == "gather":
                    n = IMAGES if u == 0 else P
                    wait(g, h_moe, u - 2)
                    g.indirect_dma_start(out=Y[u % 3][0:n], out_offset=None, in_=yg_dram[0:NT0 * P],
                                         in_offset=bass.IndirectOffsetOnAxis(ap=SLOT[0:n, 0, t:t + 1], axis=0))\
                        .then_inc(c_gathered[u % 3], 16)
                elif stage == "moe":
                    g.wait_ge(set_up, 3)
                    g.wait_ge(q_var, u + 1)
                    wait(g, q_rstd, u)
                    chain.link(g.tensor_scalar(c_eps, c_mv[i][:, 1:2], EPS_LN, None, ALU.add))
                    g.tensor_tensor(c_rstd[i], c_eps, c_minus_half, ALU.pow).then_inc(q_rstd, 1)
                elif stage == "xT" and u > 0:
                    g.wait_ge(q_xT_ready, 1)
                    wait(g, q_qk_done, u - 2)
                    b = 2 * (u - 1)
                    g.tensor_copy(c_xT[i][0:96, :, P:], clsT[0:96, :, b:b + 2]).then_inc(q_cls_ready, 1)
                elif stage == "quant" and u > 0:
                    g.wait_ge(q_qk_clipped, u)
                    wait(g, q_s_done, u - 2)
                    g.tensor_scalar(q_h[i][:, :, :, S], t_qk[i][:, 0, :, P:], MAGIC, None, ALU.subtract)
                    wait(g, q_kc_ready, u - 1)
                    chain.link(g.tensor_scalar(c_kc, t_qk[i][:, 1, :, P:], MAGIC, None, ALU.subtract))
                    g.tensor_tensor(kc_h[i], c_kc.unsqueeze(3).broadcast_to([96, C, 2, H]),
                                    K("head12")[0:96].rearrange("p (c h) -> p c h", c=C).unsqueeze(2)
                                    .broadcast_to([96, C, 2, H]), ALU.mult).then_inc(q_kc_ready, 1)

        taken[0] = common_start
        G = 2 * 2 * 3
        z_xT = [chunks(97) for _ in range(2)]
        z_clsT = area(C * IMAGES, 97).rearrange("p (c b) -> p c b", c=C)
        q_clsT = area(C * IMAGES, 96).rearrange("p (c b) -> p c b", c=C)
        k_clsT = area(C * IMAGES, 96).rearrange("p (c b) -> p c b", c=C)
        z_cls_v = area(D, IMAGES)
        z_qT = [chunks(96) for _ in range(2)]
        z_kT = [chunks(96) for _ in range(2)]
        k_sum = area(C * 2, 96).rearrange("p (c s) -> p c s", c=C)
        free_w1 = W1[0:96, 0, E1:].rearrange("p e f -> p (e f)")
        kc = [free_w1[:, i * C * 2 * TOK:(i + 1) * C * 2 * TOK].rearrange("p (c s t) -> p c s t", c=C, s=2)
              for i in range(2)]
        z_kblk = [free_w1[:, i * 2 * C * 2 * TOK:(i + 1) * 2 * C * 2 * TOK]
                  .rearrange("p (c s a t) -> p c s a t", c=C, s=2, a=2) for i in range(1, 3)]
        q_cls6 = [area(C * 2 * HC, 96).rearrange("p (c s h) -> p c s h", c=C, s=2) for _ in range(2)]
        BLOCKS, BW = H // 2, 2 * HD + 2
        z_vblk = [area(2 * BLOCKS * BW).rearrange("p (s b w) -> p s b w", s=2, b=BLOCKS) for _ in range(3)]
        vb = [area(D) for _ in range(2)]
        w_s = [area(3 * 4 * TOK).rearrange("p (j g t) -> p j g t", j=3, g=4) for _ in range(2)]
        sq = area(3 * 4 * TOK).rearrange("p (j g t) -> p j g t", j=3, g=4)
        p_j = [area(6 * P).rearrange("p (g t) -> p g t", g=G) for _ in range(2)]
        p_c = [area(H) for _ in range(2)]
        pT = [area(6 * P).rearrange("p (b t) -> p b t", b=6) for _ in range(2)]
        s_max, s_sq = area(G), [area(G) for _ in range(2)]
        deviation = [area(G) for _ in range(2)]
        z_r = [area(G) for _ in range(2)]
        p_sum = area(G)
        z_rinv = area(H)
        z_own = [area(D) for _ in range(2)]
        z_o1 = area(D)
        z_o = [area(D) for _ in range(2)]
        z_oT = [chunks(97) for _ in range(2)]
        xs = [area(D) for _ in range(2)]
        x2n = [area(D) for _ in range(2)]
        x2g = area(D)
        z_x2T = [chunks(97) for _ in range(2)]
        z_stats, z_mv2 = area(6), [area(2) for _ in range(2)]
        z_eps2, z_rstd2 = area(1), [area(1) for _ in range(2)]
        sign, gamma_abs = area(1), area(1)
        z_half, z_var_scaled = area(G), area(G)
        cls_scores = area(IMAGES * H, TOK)
        pT_cls = pT[0].rearrange("p b t -> p (b t)")[:, 0:C * PAIRS * 2 * HC]\
            .rearrange("p (c t x) -> p c t x", c=C, t=PAIRS)
        cls_mine = pT[1].rearrange("p b t -> p (b t)")[0:96, 0:C * PAIRS * 2 * HC]\
            .rearrange("p (b h) -> p b h", h=HC)
        o_cls = area(C * IMAGES, 96).rearrange("p (c b) -> p c b", c=C)
        V_ALL = W2[:, E1:].rearrange("p e k d -> p (e k d)")[:, 0:PAIRS * D].rearrange("p (t d) -> p t d", t=PAIRS)

        (z_var, z_rstd, z_src, z_xT_done, z_xT_ready, z_v_done, z_k_done, z_q_done, z_v_taken, z_q_taken, z_k_taken,
         z_centred, z_masked, z_qcls_ready, z_vrep_done, z_vblk_ready, z_vb_ready, z_s_done, z_sq_ready,
         z_w_ready, z_squares, z_deviation, z_r_ready, z_zs_ready, z_ex_ready, z_pT_done, z_pT_ready_a, z_pT_ready_v,
         z_own_ready, z_pv_done, z_o_ready, z_oT_done, z_oT_ready, z_op_done, z_var2, z_rstd2_ready, z_x2n,
         z_x2_ready, z_x2T_done, z_x2T_ready) = sems(
            "z_", "var rstd src xT_done xT_ready v_done k_done q_done v_taken q_taken k_taken centred masked qcls_ready vrep_done "
                  "vblk_ready vb_ready s_done sq_ready w_ready squares deviation r_ready zs_ready ex_ready pT_done pT_ready_a "
                  "pT_ready_v own_ready pv_done o_ready oT_done oT_ready op_done var2 rstd2 x2n "
                  "x2_ready x2T_done x2T_ready")
        z_cls_scores, z_cls_p, z_cls_done, z_cls_zero = sems("z_", "cls_scores cls_p cls_done cls_zero")
        ORDER_Z = [("norm", 1), ("norm2", 6), ("square", 3), ("exp", 4), ("qkv", 2), ("oT", 5), ("stats", 0),
                   ("scored", 3), ("centre", 2), ("pT", 4), ("own", 4), ("cls", 3), ("kept", 2), ("root", 3),
                   ("vrep", 2), ("x2T", 6), ("pv", 4), ("oproj", 5), ("mask", 2), ("logits", 6), ("scale", 3),
                   ("xT", 1), ("scores", 2)]
        ALL = TILES
        PAIRS_ONLY = ("norm", "stats", "qkv", "centre", "own", "xT", "mask", "vrep", "cls")
        NZ = {s: TILES + (s not in PAIRS_ONLY) for s, _ in ORDER_Z}

        def before_z(other, stage, u):
            return issued_before(ORDER_Z, NZ, other, stage, u) - 1

        def rows_of(m):
            return IMAGES if m == ALL else P

        def tile_z(m):
            return CLS if m == ALL else m - 1

        def z_tensor(pe):
            def to_features(u):
                pe.wait_ge(z_src, u + 1)
                wait(pe, z_xT_ready, u)
                wait(pe, z_v_taken, issued_before(ORDER_Z, NZ, "qkv", "xT", u))
                wait(pe, z_oT_ready, before_z("oT", "xT", u))
                wait(pe, z_x2T_ready, before_z("x2T", "xT", u))
                for c in range(C):
                    mm = pe.transpose(PS[0:96, 0, c * P:(c + 1) * P], X1[:, tile_of(u), 96 * c:96 * c + 96], ident)
                mm.then_inc(z_xT_done, 1)

            def qkv(u):
                pe.wait_ge(z_xT_ready, u + 1)
                x, n = (z_clsT, IMAGES) if u == 0 else (z_xT[u % 2], P)
                wait(pe, z_q_taken, u)
                wait(pe, z_k_taken, u)
                wait(pe, z_vb_ready, before_z("vrep", "qkv", u))

                def features(a, done):
                    for oc in range(C):
                        for c in range(C):
                            at = a * D + 96 * oc
                            mm = pe.matmul(PS[0:96, 1, (a * C + oc) * P:(a * C + oc) * P + n],
                                           w_small_at("qkv2", c, at, at + 96), x[0:KC[c], c],
                                           start=c == 0, stop=c == C - 1)
                    mm.then_inc(done, 1)

                features(1, z_k_done)
                wait(pe, z_oT_ready, before_z("oT", "qkv", u))
                wait(pe, z_x2T_ready, before_z("x2T", "qkv", u))
                wait(pe, z_v_taken, u)
                for c in range(C):
                    mm = pe.matmul(PS[0:n, 0, C * P:C * P + D], x[0:KC[c], c], w_small_at("qkv2", c, 2 * D, 3 * D),
                                   start=c == 0, stop=c == C - 1)
                mm.then_inc(z_v_done, 1)
                pe.wait_ge(z_k_taken, u + 1)
                features(0, z_q_done)

            def replicate(u):
                pe.wait_ge(z_v_taken, u + 1)
                wait(pe, z_vblk_ready, u - 1)
                wait(pe, z_pT_ready_v, before_z("pT", "vrep", u))
                wait(pe, z_var2, before_z("oproj", "vrep", u))
                wait(pe, z_vb_ready, u - 1)
                pe.wait_ge(z_k_taken, u + 1)
                pe.wait_ge(z_q_taken, u + 1)
                tw = K("twice").rearrange("p (s m) -> p s m", s=2)
                for s in range(2):
                    pe.matmul(PS[:, 2, s * D:(s + 1) * D], tw[:, s], V_ALL[:, u - 1], start=True, stop=True)
                    b = 2 * (u - 1) + s
                    mm = pe.matmul(PS[S * s:S * s + S, 1, 0:D],
                                   ident[0:IMAGES, b:b + 1].broadcast_to([IMAGES, S]), z_cls_v, start=True, stop=True)
                mm.then_inc(z_vrep_done, 1)

            def scores(u):
                i = u % 2
                pe.wait_ge(z_q_taken, u + 1)
                pe.wait_ge(z_masked, u)
                wait(pe, z_w_ready, u - 1)
                wait(pe, z_sq_ready, u - 1)
                for c in range(C):
                    for s in range(2):
                        for j in range(3):
                            r = slice(32 * j, 32 * j + 32)
                            mm = pe.matmul(PS[S * s:S * s + S, 4 + j, c * 2 * TOK:(c + 1) * 2 * TOK],
                                      z_qT[i][r, c, S * s:S * s + S],
                                      z_kblk[i][r, c, s].rearrange("p a t -> p (a t)"), start=True, stop=True)
                mm.then_inc(z_s_done, 1)

            def class_scores(u):
                i = u % 2
                pe.wait_ge(z_q_taken, 1)
                pe.wait_ge(z_centred, u)
                pe.wait_ge(z_qcls_ready, u)
                wait(pe, lg_taken, TILES + before_z("logits", "cls", u))
                for s in range(2):
                    for c in range(C):
                        b = 2 * (u - 1) + s
                        mm = pe.matmul(PS[0:TOK, 3, b * H + c * HC:b * H + (c + 1) * HC], kc[i][:, c, s],
                                       q_cls6[i][:, c, s], start=True, stop=True)
                mm.then_inc(z_cls_done, 1)

            def p_t(u):
                pe.wait_ge(z_ex_ready, u)
                wait(pe, z_pT_ready_a, u - 1)
                wait(pe, z_o_ready, before_z("pv", "pT", u))
                wait(pe, z_pT_ready_v, u - 1)
                wait(pe, z_vblk_ready, before_z("vrep", "pT", u))
                wait(pe, z_var2, before_z("oproj", "pT", u))
                for b in range(6):
                    bank, at = (7, b * P) if b < 4 else (2, (b - 4) * P)
                    mm = pe.transpose(PS[:, bank, at:at + P],
                                      p_j[u % 2].rearrange("p g t -> p (g t)")[:, b * P:(b + 1) * P], ident)
                mm.then_inc(z_pT_done, 1)

            def pv(u):
                pe.wait_ge(z_pT_ready_a, u)
                pe.wait_ge(z_pT_ready_v, u)
                pe.wait_ge(z_vblk_ready, u)
                wait(pe, z_o_ready, u - 1)
                for s in range(2):
                    for j in range(3):
                        for c in range(C):
                            b = 3 * c + j
                            mm = pe.matmul(PS[S * s:S * s + S, 7, b * BW:(b + 1) * BW],
                                           pT[u % 2][:, 2 * j + c, S * s:S * s + S], z_vblk[u % 3][:, s, b],
                                           start=True, stop=True)
                mm.then_inc(z_pv_done, 1)

            def transposed(m, src, done):
                n = rows_of(m)
                for c in range(C):
                    mm = pe.transpose(PS[0:96, 0, c * P:c * P + n], src[0:n, 96 * c:96 * c + 96], ident[0:n, 0:n])
                mm.then_inc(done, 1)

            def out_t(m):
                pe.wait_ge(z_o_ready, m)
                wait(pe, z_oT_ready, m - 1)
                wait(pe, z_xT_ready, before_z("xT", "oT", m) + 1)
                wait(pe, z_v_taken, before_z("qkv", "oT", m) + 1)
                wait(pe, z_x2T_ready, before_z("x2T", "oT", m))
                transposed(m, z_o[m % 2], z_oT_done)

            def out_projection(m):
                pe.wait_ge(z_oT_ready, m)
                wait(pe, z_var2, m - 1)
                wait(pe, z_vblk_ready, before_z("vrep", "oproj", m))
                wait(pe, z_pT_ready_v, min(PAIRS, before_z("pT", "oproj", m)))
                n = rows_of(m)
                for c in range(C):
                    mm = pe.matmul(PS[0:n, 2, 0:D], z_oT[m % 2][0:KC[c], c, 0:n],
                                   w_small_at("out2", c, 0, D), start=c == 0, stop=c == C - 1)
                mm.then_inc(z_op_done, 1)

            def x2_t(m):
                pe.wait_ge(z_x2_ready, m)
                wait(pe, z_x2T_ready, m - 1)
                wait(pe, z_xT_ready, before_z("xT", "x2T", m) + 1)
                wait(pe, z_v_taken, before_z("qkv", "x2T", m) + 1)
                wait(pe, z_oT_ready, before_z("oT", "x2T", m))
                transposed(m, X1[:, tile_z(m)], z_x2T_done)

            def logits(m):
                n = rows_of(m)
                pe.wait_ge(z_x2T_ready, m)
                wait(pe, lg_taken, TILES + m - 1)
                if issued_before(ORDER_Z, NZ, "kept", "logits", m) > ALL:
                    pe.wait_ge(z_cls_scores, 1)
                for c in range(C):
                    mm = pe.matmul(PS[0:n, 3, IMAGES * H:IMAGES * H + E1], z_x2T[m % 2][0:KC[c], c, 0:n],
                                   w_small_at("gate2", c, 0, E1), start=c == 0, stop=c == C - 1)
                mm.then_inc(lg_done, 1)

            def own_scores():
                pe.wait_ge(z_cls_scores, 1)
                pe.wait_ge(z_w_ready, PAIRS)
                pe.wait_ge(z_sq_ready, PAIRS)
                for h in range(H):
                    c, j, a = h // HC, h % HC // 2, h % 2
                    mm = pe.transpose(PS[0:IMAGES, 4 + j, (2 * c + a) * TOK:(2 * c + a + 1) * TOK],
                                      cls_scores[:, h:IMAGES * H:H], ident[0:TOK, 0:TOK])
                mm.then_inc(z_s_done, 1)

            def own_p_t():
                pe.wait_ge(z_cls_p, 1)
                wait(pe, z_pT_ready_a, PAIRS)
                wait(pe, z_o_ready, before_z("pv", "pT", ALL))
                for g in range(G):
                    for s in range(2):
                        mm = pe.matmul(PS[S * s:S * s + S, 7, g * PAIRS:(g + 1) * PAIRS], p_j[ALL % 2][0:IMAGES, g],
                                       ident[0:IMAGES, s:IMAGES:2], start=True, stop=True)
                mm.then_inc(z_pT_done, 1)

            def own_pv():
                pe.wait_ge(z_pT_ready_a, ALL)
                pe.wait_ge(z_w_ready, ALL)
                pe.wait_ge(z_sq_ready, ALL)
                for t in range(PAIRS):
                    for c in range(C):
                        at = (c * PAIRS + t) * 2 * HC
                        mm = pe.matmul(PS[0:96, 4, at:at + 2 * HC], V_ALL[:, t, 96 * c:96 * c + 96],
                                       pT_cls[:, c, t], start=True, stop=True)
                mm.then_inc(z_pv_done, 1)

            pe.wait_ge(set_up, 4)
            pe.wait_ge(h_quant, TILES)
            step = {"xT": to_features, "qkv": qkv, "vrep": replicate, "cls": class_scores, "scores": scores, "pT": p_t,
                    "pv": pv,
                    "oT": out_t, "oproj": out_projection, "x2T": x2_t, "logits": logits}
            own_step = {"scores": own_scores, "pT": own_p_t, "pv": own_pv}
            for stage, u in bodies(ORDER_Z, NZ):
                if u == ALL and stage in own_step:
                    own_step[stage]()
                elif stage in step and (u > 0 or stage in ("xT", "qkv")):
                    step[stage](u)

        def z_scalar(act):
            def copy(out_ap, in_ap):
                return act.activation(out_ap, in_ap, ACT.Copy)

            def square(m):
                n = rows_of(m)
                act.wait_ge(z_s_done, m)
                wait(act, z_w_ready, m - 1)
                act.activation(sq[0:n].rearrange("p j g t -> p j (g t)"), PS[0:n, 4:7, 0:4 * TOK], ACT.Square)\
                    .then_inc(z_sq_ready, 1)

            def exponent(m):
                n, i = rows_of(m), m % 2
                act.wait_ge(z_zs_ready, m)
                wait(act, z_pT_done, m - 2)
                wait(act, z_own_ready, m - 2)
                wait(act, z_o_ready, m - 2)
                w = w_s[i][0:n]
                act.activation(p_j[i][0:n].rearrange("p (j g) t -> p j g t", j=3), w[:, :, :, 0:S], ACT.Exp)
                act.activation(p_c[i][0:n].rearrange("p (c j a) -> p j c a", c=C, a=2),
                               w[:, :, :, S].rearrange("p j (c a) -> p j c a", c=C), ACT.Exp).then_inc(z_ex_ready, 1)

            def o_t(m):
                act.wait_ge(z_oT_done, m)
                wait(act, z_op_done, m - 2)
                copy(z_oT[m % 2][0:96], PS[0:96, 0, 0:C * P].rearrange("p (c t) -> p c t", c=C)).then_inc(z_oT_ready, 1)

            def x2_t(m):
                n = rows_of(m)
                act.wait_ge(z_x2T_done, m)
                wait(act, lg_done, TILES + m - 2)
                copy(z_x2T[m % 2][0:96, :, 0:n], PS[0:96, 0, 0:C * P].rearrange("p (c t) -> p c t", c=C)[:, :, 0:n])\
                    .then_inc(z_x2T_ready, 1)

            act.wait_ge(set_up, 4)
            for stage, u in bodies(ORDER_Z, NZ):
                i = u % 2
                if stage == "xT":
                    act.wait_ge(z_xT_done, u + 1)
                    ps = PS[0:96, 0, 0:C * P].rearrange("p (c t) -> p c t", c=C)
                    if u == 0:
                        copy(z_clsT[0:96], ps[:, :, 0:IMAGES]).then_inc(z_xT_ready, 1)
                    else:
                        wait(act, z_q_done, u - 1)
                        copy(z_xT[i][0:96], ps).then_inc(z_xT_ready, 1)
                elif stage == "qkv":
                    n = IMAGES if u == 0 else P
                    ps = PS[0:96, 1].rearrange("p (a c t) -> p a c t", a=2, c=C)
                    act.wait_ge(z_k_done, u + 1)
                    wait(act, z_centred, u - 2)
                    copy(k_clsT if u == 0 else z_kT[i], ps[:, 1, :, 0:n]).then_inc(z_k_taken, 1)
                    act.wait_ge(z_v_done, u + 1)
                    copy(z_cls_v if u == 0 else V_ALL[:, u - 1], PS[0:n, 0, C * P:C * P + D]).then_inc(z_v_taken, 1)
                    act.wait_ge(z_q_done, u + 1)
                    wait(act, z_s_done, u - 2)
                    act.activation(q_clsT if u == 0 else z_qT[i], ps[:, 0, :, 0:n], ACT.Copy, scale=sign[0:96])\
                        .then_inc(z_q_taken, 1)
                elif stage == "vrep" and u > 0:
                    act.wait_ge(z_vrep_done, u)
                    wait(act, z_own_ready, u - 2)
                    copy(vb[i], PS[:, 1, 0:D]).then_inc(z_vb_ready, 1)
                elif stage == "square" and u > 0:
                    square(u)
                elif stage == "mask" and u > 0:
                    act.wait_ge(z_centred, u)
                    wait(act, z_s_done, u - 2)
                    for a in range(2):
                        last = act.activation(z_kblk[i][:, :, :, a], kc[i], ACT.Copy, scale=K("half")[0:96, a:a + 1])
                    last.then_inc(z_masked, 1)
                elif stage == "exp" and u > 0:
                    exponent(u)
                elif stage == "kept" and u == ALL:
                    act.wait_ge(z_cls_done, PAIRS)
                    wait(act, lg_taken, TILES + before_z("logits", "kept", ALL))
                    copy(cls_scores, PS[0:TOK, 3, 0:IMAGES * H]).then_inc(z_cls_scores, 1)
                elif stage == "pT" and u == ALL:
                    act.wait_ge(z_pT_done, ALL)
                    act.wait_ge(z_cls_zero, 1)
                    for s in range(2):
                        rows = slice(S * s, S * s + S)
                        for c in range(C):
                            last = copy(pT_cls[rows, c, :, s * HC:(s + 1) * HC].rearrange("p t (j a) -> p j a t", a=2),
                                        PS[rows, 7, 0:G * PAIRS].rearrange("p (j c a t) -> p c j a t", j=3, c=C,
                                                                           a=2)[:, c])
                    last.then_inc(z_pT_ready_a, 1)
                elif stage == "pT" and u > 0:
                    act.wait_ge(z_pT_done, u)
                    wait(act, z_pv_done, u - 2)
                    copy(pT[i][:, 0:4], PS[:, 7].rearrange("p (b t) -> p b t", b=4)).then_inc(z_pT_ready_a, 1)
                elif stage == "oT" and 0 < u < ALL:
                    o_t(u)
                elif stage == "x2T" and u > 0:
                    x2_t(u)

        def z_vector(v, chain):
            def scored(m):
                n, i = rows_of(m), m % 2
                v.wait_ge(z_sq_ready, m)
                ps = PS[0:n, 4:7, 0:4 * TOK].rearrange("p j (g t) -> p j g t", g=4)
                mx = s_max[0:n].rearrange("p (j g) -> p j g", j=3)
                chain.link(v.tensor_reduce(mx, ps, AX.X, ALU.max))
                wait(v, z_ex_ready, m - 2)
                last = [v.tensor_tensor(w_s[i][0:n, j], ps[:, j], mx[:, j].unsqueeze(2).broadcast_to([n, 4, TOK]),
                                        ALU.subtract) for j in range(3)][-1]
                last.then_inc(z_w_ready, 1)
                wait(v, z_deviation, m - 2)
                v.tensor_reduce(s_sq[i][0:n].rearrange("p (j g) -> p j g", j=3), sq[0:n], AX.X, ALU.add)\
                    .then_inc(z_squares, 1)

            def scale(m):
                n, i = rows_of(m), m % 2
                v.wait_ge(z_deviation, m)
                wait(v, z_zs_ready, m - 2)
                chain.link(v.tensor_scalar(z_r[i][0:n], deviation[i][0:n], EPS_Z, None, ALU.add))
                chain.link(v.reciprocal(z_r[i][0:n], z_r[i][0:n]))
                v.tensor_scalar(z_r[i][0:n], z_r[i][0:n], gamma_abs[0:n], None, ALU.mult).then_inc(z_r_ready, 1)

            def attended(m):
                n, i, t = rows_of(m), m % 2, tile_z(m)
                v.wait_ge(z_op_done, m)
                chain.link(v.tensor_tensor(xs[i][0:n], PS[0:n, 2, 0:D], X1[0:n, t], ALU.add))
                chain.link(v.bn_stats(z_stats[0:n], xs[i][0:n]))
                v.bn_aggr(z_mv2[i][0:n], z_stats[0:n]).then_inc(z_var2, 1)

            def normed(m):
                n, i = rows_of(m), m % 2
                v.wait_ge(z_rstd2_ready, m)
                wait(v, z_x2_ready, m - 2)
                v.tensor_scalar(x2n[i][0:n], xs[i][0:n], z_mv2[i][0:n, 0:1], z_rstd2[i][0:n], ALU.subtract, ALU.mult)\
                    .then_inc(z_x2n, 1)

            def logits(m):
                n = rows_of(m)
                v.wait_ge(lg_done, TILES + m)
                v.tensor_copy(LG[0:n, tile_z(m), 0:E1], PS[0:n, 3, IMAGES * H:IMAGES * H + E1]).then_inc(lg_taken, 1)

            def own_p():
                i, n = ALL % 2, IMAGES
                v.wait_ge(z_pv_done, PAIRS)
                v.memset(pT_cls, 0.0).then_inc(z_cls_zero, 1)
                v.wait_ge(z_ex_ready, ALL)
                by_groups = "p (c j a) -> p j c a"
                sums = p_sum[0:n].rearrange("p (j c a) -> p j c a", j=3, c=C)
                chain.link(v.tensor_reduce(p_sum[0:n], p_j[i][0:n], AX.X, ALU.add))
                chain.link(v.tensor_tensor(sums, sums, p_c[i][0:n].rearrange(by_groups, c=C, a=2), ALU.add))
                chain.link(v.reciprocal(p_sum[0:n], p_sum[0:n]))
                v.tensor_tensor(p_j[i][0:n], p_j[i][0:n], p_sum[0:n].unsqueeze(2).broadcast_to([n, G, S]), ALU.mult)\
                    .then_inc(z_cls_p, 1)
                chain.link(v.tensor_copy(z_rinv[0:n].rearrange(by_groups, c=C, a=2), sums))
                chain.link(v.tensor_tensor(p_c[i][0:n], p_c[i][0:n], z_rinv[0:n], ALU.mult))
                wait(v, z_oT_done, PAIRS - 1)
                v.tensor_tensor(z_o[i][0:n].rearrange("p (h d) -> p h d", h=H), z_cls_v.rearrange("p (h d) -> p h d", h=H),
                                p_c[i][0:n].unsqueeze(2).broadcast_to([n, H, HD]), ALU.mult).then_inc(z_o_ready, 1)

            def own_out():
                n = IMAGES
                v.wait_ge(z_pv_done, ALL)
                chain.link(v.tensor_tensor(cls_mine, PS[0:96, 4, 0:C * PAIRS * 2 * HC].rearrange("p (b h) -> p b h", h=HC),
                                           head6.unsqueeze(1).broadcast_to([96, C * IMAGES, HC]), ALU.mult))
                chain.link(v.tensor_reduce(o_cls.rearrange("p c b -> p (c b)"), cls_mine, AX.X, ALU.add))
                v.wait_ge(z_oT_done, ALL)
                v.tensor_tensor(z_oT[ALL % 2][0:96, :, 0:n],
                                PS[0:96, 0, 0:C * P].rearrange("p (c t) -> p c t", c=C)[:, :, 0:n], o_cls, ALU.add)\
                    .then_inc(z_oT_ready, 1)

            v.wait_ge(q_oproj_done, TILES)
            v.wait_ge(h_quant, TILES)
            for i in range(2):
                v.memset(z_xT[i][96:97], 1.0)
                v.memset(z_oT[i][96:97], 1.0)
                v.memset(z_x2T[i][96:97], 1.0)
            v.memset(z_clsT[96:97], 1.0)
            v.memset(z_half, 0.5)
            for i in range(3):
                for a in range(2):
                    v.memset(z_vblk[i][S * a:S * a + S, :, :, 2 * HD + 1 - a], 0.0)
                    v.memset(z_vblk[i][S * a:S * a + S, :, :, 2 * HD + a], 1.0)
            gamma = ROW("gamma", 1)
            v.tensor_scalar(gamma_abs, gamma, 0.0, None, ALU.is_lt)
            chain.link(v.tensor_scalar(sign, gamma, 0.0, None, ALU.is_gt))
            chain.link(v.tensor_tensor(sign, sign, gamma_abs, ALU.subtract))
            v.tensor_scalar(gamma_abs, gamma, sign, HEAD_SCALE, ALU.mult, ALU.mult).then_inc(set_up, 1)
            v.wait_ge(set_up, 4)
            for stage, u in bodies(ORDER_Z, NZ):
                i, t = u % 2, tile_of(u)
                if stage == "stats":
                    wait(v, z_var, u)
                    layer_norm_stats(v, chain, HT[:, t], c_stats, c_mv[i], z_var)
                elif stage == "norm":
                    v.wait_ge(z_rstd, u + 1)
                    v.tensor_scalar(X1[:, t], HT[:, t], c_mv[i][:, 0:1], c_rstd[i], ALU.subtract, ALU.mult)\
                        .then_inc(z_src, 1)
                if u == 0:
                    continue
                if u == ALL and stage in ("pT", "pv", "oT"):
                    if stage != "pv":
                        (own_p if stage == "pT" else own_out)()
                elif stage == "centre":
                    v.wait_ge(z_k_taken, u + 1)
                    kT = z_kT[i].rearrange("p c (s t) -> p c s t", s=2)
                    k_cls = k_clsT[:, :, 2 * (u - 1):2 * u]
                    chain.link(v.tensor_reduce(k_sum, kT, AX.X, ALU.add))
                    chain.link(v.tensor_tensor(k_sum, k_sum, k_cls, ALU.add))
                    chain.link(v.tensor_scalar(k_sum, k_sum, 1.0 / TOK, None, ALU.mult))
                    wait(v, z_s_done, u - 2)
                    wait(v, z_masked, u - 2)
                    v.tensor_tensor(kc[i][:, :, :, 0:S], kT, k_sum.unsqueeze(3).broadcast_to([96, C, 2, S]), ALU.subtract)
                    v.tensor_tensor(kc[i][:, :, :, S], k_cls, k_sum, ALU.subtract).then_inc(z_centred, 1)
                elif stage == "vrep":
                    v.wait_ge(z_vrep_done, u)
                    wait(v, z_pv_done, u - 3)
                    v.tensor_tensor(z_vblk[u % 3][:, :, :, 0:2 * HD],
                                    PS[:, 2, 0:2 * D].rearrange("p (s b e) -> p s b e", s=2, b=BLOCKS),
                                    K("half_cols").rearrange("p (b e) -> p b e", b=BLOCKS).unsqueeze(1)
                                    .broadcast_to([P, 2, BLOCKS, 2 * HD]), ALU.mult)\
                        .then_inc(z_vblk_ready, 1)
                elif stage == "scored":
                    scored(u)
                elif stage == "scale":
                    scale(u)
                elif stage == "pT":
                    v.wait_ge(z_pT_done, u)
                    wait(v, z_pv_done, u - 2)
                    v.tensor_copy(pT[i][:, 4:6], PS[:, 2, 0:2 * P].rearrange("p (b t) -> p b t", b=2))\
                        .then_inc(z_pT_ready_v, 1)
                elif stage == "pv":
                    v.wait_ge(z_pv_done, u)
                    v.wait_ge(z_own_ready, u)
                    ps = PS[:, 7, 0:BLOCKS * BW].rearrange("p (b w) -> p b w", b=BLOCKS)
                    chain.link(v.tensor_tensor(z_rinv.rearrange("p (b a) -> p b a", a=2), ps[:, :, 2 * HD:],
                                               p_c[i].rearrange("p (b a) -> p b a", a=2), ALU.add))
                    v.tensor_tensor(z_o1.rearrange("p (b e) -> p b e", b=BLOCKS), ps[:, :, 0:2 * HD],
                                    z_own[i].rearrange("p (b e) -> p b e", b=BLOCKS), ALU.add)
                    chain.link(v.reciprocal(z_rinv, z_rinv))
                    wait(v, z_oT_done, u - 2)
                    v.tensor_tensor(z_o[i].rearrange("p (h d) -> p h d", h=H), z_o1.rearrange("p (h d) -> p h d", h=H),
                                    z_rinv.unsqueeze(2).broadcast_to([P, H, HD]), ALU.mult).then_inc(z_o_ready, 1)
                elif stage == "oproj":
                    attended(u)
                elif stage == "norm2":
                    normed(u)
                elif stage == "logits":
                    logits(u)

        def z_gpsimd(g, chain):
            def root(m):
                n, i = rows_of(m), m % 2
                g.wait_ge(z_squares, m)
                wait(g, z_deviation, m - 1)
                chain.link(g.tensor_scalar(z_var_scaled[0:n], s_sq[i][0:n], HEAD_SCALE * HEAD_SCALE / (TOK - 1), None,
                                           ALU.mult))
                wait(g, z_r_ready, m - 2)
                g.tensor_tensor(deviation[i][0:n], z_var_scaled[0:n], z_half[0:n], ALU.pow).then_inc(z_deviation, 1)

            def z_scores(m):
                n, i = rows_of(m), m % 2
                g.wait_ge(z_w_ready, m)
                g.wait_ge(z_r_ready, m)
                w = w_s[i][0:n].rearrange("p j g t -> p (j g) t")
                g.tensor_tensor(w, w, z_r[i][0:n].unsqueeze(2).broadcast_to([n, G, TOK]), ALU.mult).then_inc(z_zs_ready, 1)

            def root2(m):
                n, i = rows_of(m), m % 2
                g.wait_ge(z_var2, m)
                wait(g, z_rstd2_ready, m - 1)
                chain.link(g.tensor_scalar(z_eps2[0:n], z_mv2[i][0:n, 1:2], EPS_LN, None, ALU.add))
                g.tensor_tensor(z_rstd2[i][0:n], z_eps2[0:n], c_minus_half[0:n], ALU.pow).then_inc(z_rstd2_ready, 1)

            def scaled(m):
                n, i = rows_of(m), m % 2
                g.wait_ge(z_x2n, m)
                wait(g, z_x2_ready, m - 1)
                chain.link(g.tensor_tensor(x2g[0:n], x2n[i][0:n], ROW("ln1_g")[0:n], ALU.mult))
                g.tensor_tensor(X1[0:n, tile_z(m)], x2g[0:n], ROW("ln1_b")[0:n], ALU.add).then_inc(z_x2_ready, 1)

            g.wait_ge(set_up, 4)
            g.wait_ge(loaded["later"], 16 * 2)
            for stage, u in bodies(ORDER_Z, NZ):
                i, t = u % 2, tile_of(u)
                if stage == "stats":
                    g.wait_ge(z_var, u + 1)
                    wait(g, z_rstd, u)
                    chain.link(g.tensor_scalar(c_eps, c_mv[i][:, 1:2], EPS_LN, None, ALU.add))
                    g.tensor_tensor(c_rstd[i], c_eps, c_minus_half, ALU.pow).then_inc(z_rstd, 1)
                if u == 0:
                    continue
                if stage == "qkv":
                    b = 2 * (u - 1)
                    wait(g, z_s_done, u - 2)
                    g.wait_ge(z_q_taken, 1)
                    g.tensor_tensor(q_cls6[i], q_clsT[:, :, b:b + 2].unsqueeze(3).broadcast_to([96, C, 2, HC]),
                                    head6.unsqueeze(1).unsqueeze(1).broadcast_to([96, C, 2, HC]), ALU.mult)\
                        .then_inc(z_qcls_ready, 1)
                elif stage == "root":
                    root(u)
                elif stage == "scale":
                    z_scores(u)
                elif stage == "own":
                    g.wait_ge(z_ex_ready, u)
                    g.wait_ge(z_vb_ready, u)
                    wait(g, z_o_ready, u - 2)
                    g.tensor_tensor(z_own[i].rearrange("p (h d) -> p h d", h=H), vb[i].rearrange("p (h d) -> p h d", h=H),
                                    p_c[i].unsqueeze(2).broadcast_to([P, H, HD]), ALU.mult).then_inc(z_own_ready, 1)
                elif stage == "oproj":
                    root2(u)
                elif stage == "norm2":
                    scaled(u)


        taken[0] = between_start
        F_SLOTS, F_KEPT = 4, 10
        F_Y = [[area(D) for _ in range(TOP1)] for _ in range(F_SLOTS)]
        f_one, f_two = area(D), [area(D) for _ in range(F_KEPT)]
        f_stats, f_g = area(6), [area(D) for _ in range(2)]
        f_mv = area(2 * TILES).rearrange("p (u s) -> p u s", u=TILES)
        f_eps, f_rs, f_half = area(TILES), area(TILES), area(TILES)
        f_out = [area(D) for _ in range(6)]
        f_gathered = c_gathered + [sem("f_gathered3")]
        f_var, f_rstd, f_added, f_ready = sems("f_", "var rstd added ready")
        ROOTS = [(0, 1), (1, 4), (4, 7), (7, 10), (10, 13), (13, 15), (15, 17)]
        ROOT_OF = [g for g, (a, b) in enumerate(ROOTS) for _ in range(a, b)]
        assert len(ROOT_OF) == TILES

        def f_bodies():
            for b in range(TILES + 2):
                if b < TILES:
                    yield "gather", b
                if b >= 2 and b - 1 == ROOTS[ROOT_OF[b - 2]][1]:
                    yield "root", ROOT_OF[b - 2]

        def rows_u(u):
            return IMAGES if u == 0 else P

        def gathered(u):
            i = u % F_SLOTS
            first_layer = (TILES + 2 - i) // 3 if i < 3 else 0
            return f_gathered[i], 16 * (first_layer + TOP1 * (u // F_SLOTS + 1))

        def f_gpsimd(g, chain):
            g.tensor_tensor(HT[:, :], HT[:, :], ROW("ln2_b").unsqueeze(1).broadcast_to([P, TILES, D]), ALU.add)\
                .then_inc(f_added, 1)
            experts_done(g, 1)
            for stage, u in f_bodies():
                if stage == "gather":
                    n, t = rows_u(u), tile_of(u)
                    wait(g, f_var, u - F_SLOTS + 1)
                    for k in range(TOP1):
                        g.indirect_dma_start(out=F_Y[u % F_SLOTS][k][0:n], out_offset=None, in_=yg_dram,
                                             in_offset=bass.IndirectOffsetOnAxis(ap=SLOT[0:n, k, t:t + 1], axis=0))\
                            .then_inc(f_gathered[u % F_SLOTS], 16)
                elif stage == "root":
                    a, b = ROOTS[u]
                    n = rows_u(a)
                    g.wait_ge(f_var, b)
                    chain.link(g.tensor_scalar(f_eps[0:n, a:b], f_mv[0:n, a:b, 1], EPS_LN, None, ALU.add))
                    g.tensor_tensor(f_rs[0:n, a:b], f_eps[0:n, a:b], f_half[0:n, a:b], ALU.pow).then_inc(f_rstd, 1)

        def f_vector(v, chain):
            experts_done(v, 1)
            chain.link(v.memset(f_half, -0.5))

            def weigh_one(u):
                n, t = rows_u(u), tile_of(u)
                v.wait_ge(*gathered(u))
                return chain.mark(v.scalar_tensor_tensor(f_one[0:n], F_Y[u % F_SLOTS][0][0:n], PROB[0:n, 0, t:t + 1],
                                                         X1[0:n, t], ALU.mult, ALU.add))

            def weigh_two(u, one_done):
                n, t = rows_u(u), tile_of(u)
                v.wait_ge(chain.sem, one_done)
                return chain.mark(v.scalar_tensor_tensor(f_two[u % F_KEPT][0:n], F_Y[u % F_SLOTS][1][0:n],
                                                         PROB[0:n, 1, t:t + 1], f_one[0:n], ALU.mult, ALU.add))

            def centre(u):
                n = rows_u(u)
                v.wait_ge(f_rstd, ROOT_OF[u] + 1)
                wait(v, f_ready, u - 1)
                return chain.mark(v.scalar_tensor_tensor(f_g[u % 2][0:n], f_two[u % F_KEPT][0:n], f_mv[0:n, u, 0:1],
                                                         ROW("ln2_g")[0:n], ALU.subtract, ALU.mult))

            def finish(u, centred):
                n, t = rows_u(u), tile_of(u)
                v.wait_ge(chain.sem, centred)
                v.wait_ge(f_added, 1)
                wait(v, out_stored[u // 2 % 3], 2 * 16 * (u // 6))
                v.scalar_tensor_tensor(f_out[u % 6][0:n], f_g[u % 2][0:n], f_rs[0:n, u:u + 1], HT[0:n, t], ALU.mult,
                                       ALU.add).then_inc(f_ready, 1)

            f = 0
            for u in range(TILES):
                assert f > u - F_KEPT
                ends = ROOTS[ROOT_OF[f]][1] <= u - 1
                one_done = weigh_one(u)
                centred = centre(f) if ends else None
                two_done = weigh_two(u, one_done)
                if ends:
                    finish(f, centred)
                    f += 1
                v.wait_ge(chain.sem, two_done)
                wait(v, f_var, u)
                layer_norm_stats(v, chain, f_two[u % F_KEPT][0:rows_u(u)], f_stats[0:rows_u(u)],
                                 f_mv[0:rows_u(u), u], f_var)
            centred = centre(f)
            for u in range(f, TILES):
                next_centred = centre(u + 1) if u + 1 < TILES else None
                finish(u, centred)
                centred = next_centred

        def f_sync(sp):
            for u in range(TILES):
                sp.wait_ge(f_ready, u + 1)
                if u == 0:
                    sp.dma_start(out[:, 0], f_out[0][0:IMAGES]).then_inc(out_stored[u // 2 % 3], 16)
                else:
                    sp.dma_start(out[2 * (u - 1):2 * u, 1:TOK], f_out[u % 6]).then_inc(out_stored[u // 2 % 3], 16)
            for i in range(3):
                sp.wait_ge(out_stored[i], 16 * sum(u // 2 % 3 == i for u in range(TILES)))
        @block.sync
        def _(sp):
            a_sync(sp)
            sp.wait_ge(loaded["experts0"], 16 * 2 * E0)
            m_sync(sp, 0)
            q_sync(sp)
            sp.wait_ge(loaded_experts1, 16 * 2 * E1)
            m_sync(sp, 1)
            f_sync(sp)

        @block.tensor
        def _(pe):
            a_tensor(pe)
            r_tensor(pe, 0, lambda pe: pe.wait_ge(lg_taken, TILES))
            pe.wait_ge(loaded["experts0"], 16 * 2 * E0)
            m_tensor(pe, 0)
            q_tensor(pe)
            z_tensor(pe)
            r_tensor(pe, 1, lambda pe: pe.wait_ge(lg_taken, 2 * TILES))
            pe.wait_ge(loaded_experts1, 16 * 2 * E1)
            m_tensor(pe, 1)

        @block.scalar
        def _(act):
            a_scalar(act)
            r_scalar(act, 0)
            m_scalar(act, 0)
            q_scalar(act)
            z_scalar(act)
            r_scalar(act, 1)
            m_scalar(act, 1)

        @block.vector
        def _(v):
            chain = Chain(v, vec)
            a_vector(v, chain)
            r_vector(v, chain, 0)
            m_vector(v, 0)
            q_vector(v, chain)
            z_vector(v, chain)
            r_vector(v, chain, 1)
            m_vector(v, 1)
            f_vector(v, chain)

        @block.gpsimd
        def _(g):
            chain = Chain(g, pool)
            a_gpsimd(g, chain)
            r_gpsimd(g, 0)
            q_gpsimd(g, chain)
            z_gpsimd(g, chain)
            r_gpsimd(g, 1)
            f_gpsimd(g, chain)




def arrays_of(i):
    a = {k: np.asarray(v) for k, v in i.items()}
    f = np.float32
    x = a["x"].reshape(PAIRS, 2, CHANNELS, GRID, PATCH, GRID, PATCH)
    x = x.transpose(0, 4, 6, 2, 1, 3, 5).reshape(PAIRS, FK, P, P).transpose(0, 2, 1, 3)

    def small(w, b):
        o = np.zeros((97, C, w.shape[1]), f)
        o[0:96, 0], o[0:96, 1] = w[0:96], w[96:D]
        if b is not None:
            o[96, 1] = b
        return o

    qkv2 = np.concatenate([a["L1_ffn_Wq"].T, a["L1_ffn_Wk"].T, a["L1_ffn_Wv"].T], 1)
    qkv2_b = np.concatenate([a["L1_ffn_bq"], a["L1_ffn_bk"], a["L1_ffn_bv"]])
    w_small = np.concatenate([
        small(a["L0_attn_qkv_w"].T, a["L0_attn_qkv_b"]), small(a["L0_attn_out_w"].T, a["L0_attn_out_b"]),
        small(a["L0_ffn_Ws"], a["L0_ffn_bs"]), small(a["L1_attn_Wqkv"].T, None),
        small(a["L1_attn_Wproj"].T, a["L1_attn_bproj"]), small(qkv2, qkv2_b),
        small(a["L1_ffn_Wo"].T, a["L1_ffn_bo"]), small(a["L1_ffn_Wg"].T, a["L1_ffn_bg"])], 2)
    rows = np.concatenate([a[n].reshape(-1) for n in (
        "L0_tok_b", "cls_tok", "L1_ffn_ln1_g", "L1_ffn_ln1_b", "L1_ffn_ln2_g", "L1_ffn_ln2_b", "L1_attn_s_q",
        "L1_attn_s_k", "L1_attn_s_v", "L1_attn_s_attn", "L1_attn_s_after", "L1_ffn_gamma", "L0_ffn_b2",
        "L1_ffn_b2")])[None]

    def first(w, b):
        o = np.zeros((97, C, w.shape[0], FF), f)
        o[0:96] = w.reshape(-1, C, 96, FF).transpose(2, 1, 0, 3)
        o[96, 1] = b
        return o

    def second(w):
        return np.ascontiguousarray(w.reshape(-1, FFK, P, D).transpose(2, 0, 1, 3))

    return {
        "x_feat": np.ascontiguousarray(x),
        "w_tok": np.ascontiguousarray(a["L0_tok_W"].T.reshape(FK, P, D).transpose(1, 0, 2)),
        "w_small": w_small, "rows": rows, "consts": shape_constants(),
        "w1_0": first(a["L0_ffn_W1"], a["L0_ffn_b1"]), "w2_0": second(a["L0_ffn_W2"]),
        "w1_1": first(a["L1_ffn_W1"], a["L1_ffn_b1"]), "w2_1": second(a["L1_ffn_W2"]),
    }


def kernel(**inputs):
    import concourse.bacc as bacc
    from concourse.bass_utils import run_bass_kernel_spmd

    nc = bacc.Bacc("TRN2", target_bir_lowering=False, num_devices=1)
    arrays, args = {}, []
    for name, a in arrays_of(inputs).items():
        arrays["in_" + name] = a
        args.append(nc.dram_tensor("in_" + name, a.shape, mybir.dt.from_np(a.dtype), kind="ExternalInput").ap())
    args.append(nc.dram_tensor("out_0", (IMAGES, TOK, D), F32, kind="ExternalOutput").ap())
    build(nc, *args)
    return run_bass_kernel_spmd(nc, [arrays], core_ids=[0]).results[0]["out_0"]
```
